# Optimizing a Trainium2 kernel written in Bass

```python
import numpy as np
import jax
import jax.numpy as jnp

def _softmax(x, axis=-1):
    return jax.nn.softmax(x, axis=axis)

def _gelu(x):
    return jax.nn.gelu(x, approximate=True)

def _silu(x):
    return jax.nn.silu(x)

def _sigmoid(x):
    return jax.nn.sigmoid(x)

def _layernorm(x, axis=-1, eps=1e-05):
    m = jnp.mean(x, axis=axis, keepdims=True)
    v = jnp.var(x, axis=axis, keepdims=True)
    return (x - m) / jnp.sqrt(v + eps)

def _scatter_add(tgt, idx, src, axis=0):
    return tgt.at[idx].add(src)

def _segment_sum(src, seg, n):
    return jax.ops.segment_sum(src, seg, n)
kernel_name = 'mk_flamingo_gated_d2_seqx_r8_eb2b2c'

def setup_inputs(seed: int=0):
    np.random.seed(seed)
    _w = jnp.asarray

    def _rec_inputs():
        import jax
        import jax.numpy as jnp
        _rk = jax.random.key(seed)
        x = 7.22e-05 + 1 * jax.random.normal(jax.random.fold_in(_rk, 1), (32, 128, 128), jnp.float32)
        _lenS = 128 - jax.random.randint(jax.random.fold_in(_rk, 7), (32,), 0, max(1, 128 // 4) + 1, jnp.int32)
        _lenS2 = 77 - jax.random.randint(jax.random.fold_in(_rk, 8), (32,), 0, max(1, 77 // 4) + 1, jnp.int32)
        _ctx_1024P = jax.random.normal(jax.random.fold_in(_rk, 11), (32, 16, 128), jnp.float32)
        _ctx_1024c = jax.random.dirichlet(jax.random.fold_in(_rk, 511), 0.3 * jnp.ones((16,), jnp.float32), (32, 77))
        _ctx_1024t = jnp.einsum('bsk,bkd->bsd', _ctx_1024c, _ctx_1024P)
        _ctx_1024t = _ctx_1024t * jax.lax.rsqrt(jnp.mean(jnp.square(_ctx_1024t)) + 1e-12) * 0.953939
        ctx_1024 = 4.13588e-05 + 0.999923 * (_ctx_1024t + 0.3 * jax.random.normal(jax.random.fold_in(_rk, 611), (32, 77, 128), jnp.float32))
        _validS = jnp.arange(128)[None, :] < _lenS[:, None]
        _validS2 = jnp.arange(77)[None, :] < _lenS2[:, None]
        _causal = jnp.tril(jnp.ones((128, 128), dtype=bool))
        mask_SxS2_bk1 = jnp.broadcast_to(_validS2[0:1, :], (128, 77))
        _g = jax.random.normal(jax.random.fold_in(_rk, 9001), (2, 2), jnp.float32)
        _g = jnp.sign(_g) * jnp.maximum(jnp.abs(_g), 1.0) + (_g == 0) * 1.0
        g_xattn = _g[0]
        g_ffn = _g[1]
        return (x, ctx_1024, mask_SxS2_bk1, g_xattn, g_ffn)
    x, ctx_1024, mask_SxS2_bk1, g_xattn, g_ffn = _rec_inputs()

    def _L0_xattn_setup():
        import jax, jax.numpy as jnp
        import numpy as np
        INPUT_DIM = 128
        OUTPUT_DIM = 128
        B, LQ, LKV = (4, 256, 256)
        SCALE = float(np.sqrt(INPUT_DIM))
        key = jax.random.key(seed)
        k1, k2, k3, k4, k5 = jax.random.split(key, 5)
        s = 1.0 / np.sqrt(INPUT_DIM)
        return {'x1': jax.random.normal(k1, (B, LQ, INPUT_DIM), dtype=jnp.float32), 'x2': jax.random.normal(k2, (B, LKV, INPUT_DIM), dtype=jnp.float32), 'w_q': jax.random.normal(k3, (OUTPUT_DIM, INPUT_DIM), dtype=jnp.float32) * s, 'w_k': jax.random.normal(k4, (OUTPUT_DIM, INPUT_DIM), dtype=jnp.float32) * s, 'w_v': jax.random.normal(k5, (OUTPUT_DIM, INPUT_DIM), dtype=jnp.float32) * s}
    _L0_xattn_all = _L0_xattn_setup()
    _L0_xattn_in = {k: v for k, v in _L0_xattn_all.items() if k in ('w_q', 'w_k', 'w_v')}
    del _L0_xattn_all

    def _L0_ffn_setup():
        import jax, jax.numpy as jnp
        import numpy as np
        E = 8
        D = 128
        H = 256
        TOP_K = 2
        key = jax.random.key(seed)
        k_x, k_g, k_w1, k_w2 = jax.random.split(key, 4)
        B, S = (4, 256)
        inp = {'input': jax.random.normal(k_x, (B, S, D), dtype=jnp.float32), 'Wg': jax.random.normal(k_g, (D, E), dtype=jnp.float32) * 0.02, 'W1': jax.random.normal(k_w1, (E, D, H), dtype=jnp.float32) * 0.02, 'b1': jnp.zeros((E, H), dtype=jnp.float32), 'W2': jax.random.normal(k_w2, (E, H, D), dtype=jnp.float32) * 0.02, 'b2': jnp.zeros((E, D), dtype=jnp.float32)}
        return inp
    _L0_ffn_all = _L0_ffn_setup()
    _L0_ffn_in = {k: v for k, v in _L0_ffn_all.items() if k in ('Wg', 'W1', 'b1', 'W2', 'b2')}
    del _L0_ffn_all

    def _L1_xattn_setup():
        import jax, jax.numpy as jnp
        import numpy as np
        import math
        D_MODEL = 128
        NUM_HEADS = 16
        D_K = D_MODEL // NUM_HEADS
        B, S = (4, 256)
        key = jax.random.key(seed)
        ks = jax.random.split(key, 12)
        q = jax.random.normal(ks[0], (B, S, D_MODEL), dtype=jnp.float32)
        k = jax.random.normal(ks[1], (B, S, D_MODEL), dtype=jnp.float32)
        v = jax.random.normal(ks[2], (B, S, D_MODEL), dtype=jnp.float32)
        mask = jnp.triu(jnp.ones((S, S), dtype=bool), k=1)
        limit = math.sqrt(6.0 / (D_MODEL + D_MODEL))

        def xavier(kk):
            return jax.random.uniform(kk, (D_MODEL, D_MODEL), jnp.float32, -limit, limit)
        blim = 1.0 / math.sqrt(D_MODEL)

        def bias(kk):
            return jax.random.uniform(kk, (D_MODEL,), jnp.float32, -blim, blim)
        return {'q': q, 'k': k, 'v': v, 'mask': mask, 'wq': xavier(ks[3]), 'bq': bias(ks[4]), 'wk': xavier(ks[5]), 'bk': bias(ks[6]), 'wv': xavier(ks[7]), 'bv': bias(ks[8]), 'wo': xavier(ks[9]), 'bo': bias(ks[10])}
    _L1_xattn_all = _L1_xattn_setup()
    _L1_xattn_in = {k: v for k, v in _L1_xattn_all.items() if k in ('wq', 'bq', 'wk', 'bk', 'wv', 'bv', 'wo', 'bo')}
    del _L1_xattn_all

    def _L1_ffn_setup():
        import jax, jax.numpy as jnp
        import numpy as np
        TOP_K = 2
        ROUTE_SCALE = 1.0
        EPS = 1e-20
        B, S, D = (2, 64, 128)
        E = 8
        F = 96
        FS = 96 * 1
        key = jax.random.key(seed)
        ks = jax.random.split(key, 9)
        s = 0.02
        return {'hidden_states': jax.random.normal(ks[0], (B, S, D), dtype=jnp.float32), 'W_gate_router': jax.random.normal(ks[1], (D, E), dtype=jnp.float32) * s, 'expert_bias': jnp.zeros((E,), dtype=jnp.float32), 'Wg': jax.random.normal(ks[2], (E, D, F), dtype=jnp.float32) * s, 'Wu': jax.random.normal(ks[3], (E, D, F), dtype=jnp.float32) * s, 'Wd': jax.random.normal(ks[4], (E, F, D), dtype=jnp.float32) * s, 'Wg_s': jax.random.normal(ks[5], (D, FS), dtype=jnp.float32) * s, 'Wu_s': jax.random.normal(ks[6], (D, FS), dtype=jnp.float32) * s, 'Wd_s': jax.random.normal(ks[7], (FS, D), dtype=jnp.float32) * s}
    _L1_ffn_all = _L1_ffn_setup()
    _L1_ffn_in = {k: v for k, v in _L1_ffn_all.items() if k in ('W_gate_router', 'expert_bias', 'Wg', 'Wu', 'Wd', 'Wg_s', 'Wu_s', 'Wd_s')}
    del _L1_ffn_all
    return {'x': x, 'ctx_1024': ctx_1024, 'mask_SxS2_bk1': mask_SxS2_bk1, 'g_xattn': g_xattn, 'g_ffn': g_ffn, 'L0_xattn_w_q': _L0_xattn_in['w_q'], 'L0_xattn_w_k': _L0_xattn_in['w_k'], 'L0_xattn_w_v': _L0_xattn_in['w_v'], 'L0_ffn_Wg': _L0_ffn_in['Wg'], 'L0_ffn_W1': _L0_ffn_in['W1'], 'L0_ffn_b1': _L0_ffn_in['b1'], 'L0_ffn_W2': _L0_ffn_in['W2'], 'L0_ffn_b2': _L0_ffn_in['b2'], 'L1_xattn_wq': _L1_xattn_in['wq'], 'L1_xattn_bq': _L1_xattn_in['bq'], 'L1_xattn_wk': _L1_xattn_in['wk'], 'L1_xattn_bk': _L1_xattn_in['bk'], 'L1_xattn_wv': _L1_xattn_in['wv'], 'L1_xattn_bv': _L1_xattn_in['bv'], 'L1_xattn_wo': _L1_xattn_in['wo'], 'L1_xattn_bo': _L1_xattn_in['bo'], 'L1_ffn_W_gate_router': _L1_ffn_in['W_gate_router'], 'L1_ffn_expert_bias': _L1_ffn_in['expert_bias'], 'L1_ffn_Wg': _L1_ffn_in['Wg'], 'L1_ffn_Wu': _L1_ffn_in['Wu'], 'L1_ffn_Wd': _L1_ffn_in['Wd'], 'L1_ffn_Wg_s': _L1_ffn_in['Wg_s'], 'L1_ffn_Wu_s': _L1_ffn_in['Wu_s'], 'L1_ffn_Wd_s': _L1_ffn_in['Wd_s']}

def reference(x, ctx_1024, mask_SxS2_bk1, g_xattn, g_ffn, L0_xattn_w_q, L0_xattn_w_k, L0_xattn_w_v, L0_ffn_Wg, L0_ffn_W1, L0_ffn_b1, L0_ffn_W2, L0_ffn_b2, L1_xattn_wq, L1_xattn_bq, L1_xattn_wk, L1_xattn_bk, L1_xattn_wv, L1_xattn_bv, L1_xattn_wo, L1_xattn_bo, L1_ffn_W_gate_router, L1_ffn_expert_bias, L1_ffn_Wg, L1_ffn_Wu, L1_ffn_Wd, L1_ffn_Wg_s, L1_ffn_Wu_s, L1_ffn_Wd_s):
    import jax
    import jax.numpy as jnp

    def _L0_xattn_ref(x1, x2, w_q, w_k, w_v):
        import jax, jax.numpy as jnp
        import numpy as np
        INPUT_DIM = 128
        OUTPUT_DIM = 128
        B, LQ, LKV = (4, 256, 256)
        SCALE = float(np.sqrt(INPUT_DIM))
        q = jnp.einsum('bsi,oi->bso', x1, w_q)
        k = jnp.einsum('bti,oi->bto', x2, w_k)
        v = jnp.einsum('bti,oi->bto', x2, w_v)
        scores = jnp.einsum('bsd,btd->bst', q, k) / SCALE
        attn = jax.nn.softmax(scores, axis=-1)
        out = jnp.einsum('bst,btd->bsd', attn, v)
        return out

    def _L0_ffn_ref(input, Wg, W1, b1, W2, b2):
        import jax, jax.numpy as jnp
        import numpy as np
        E = 8
        D = 128
        H = 256
        TOP_K = 2
        logits = jnp.einsum('bsd,de->bse', input, Wg)
        probs = jax.nn.softmax(logits, axis=-1)
        top_vals, top_idx = jax.lax.top_k(probs, TOP_K)
        top_vals = top_vals / jnp.sum(top_vals, axis=-1, keepdims=True)
        onehot = jax.nn.one_hot(top_idx, E, dtype=input.dtype)
        mask = jnp.sum(onehot, axis=2)
        scores = jnp.sum(onehot * top_vals[..., None], axis=2)
        xm = input[None] * jnp.moveaxis(mask, -1, 0)[..., None]
        h = jnp.einsum('ebsd,edh->ebsh', xm, W1) + b1[:, None, None, :]
        h = jax.nn.relu(h)
        y = jnp.einsum('ebsh,ehd->ebsd', h, W2) + b2[:, None, None, :]
        out = jnp.sum(y * jnp.moveaxis(scores, -1, 0)[..., None], axis=0)
        return out

    def _L1_xattn_ref(q, k, v, mask, wq, bq, wk, bk, wv, bv, wo, bo):
        import jax, jax.numpy as jnp
        import numpy as np
        import math
        D_MODEL = 128
        NUM_HEADS = 16
        D_K = D_MODEL // NUM_HEADS
        B, S = (4, 256)
        b = q.shape[0]

        def proj(x, w, bb):
            return (jnp.einsum('bsd,ed->bse', x, w) + bb).reshape(b, -1, NUM_HEADS, D_K).transpose(0, 2, 1, 3)
        qh = proj(q, wq, bq)
        kh = proj(k, wk, bk)
        vh = proj(v, wv, bv)
        scores = jnp.einsum('bhqd,bhkd->bhqk', qh, kh) / math.sqrt(D_K)
        scores = jnp.where(mask, jnp.float32(-1000000000.0), scores)
        probs = jax.nn.softmax(scores, axis=-1)
        out = jnp.einsum('bhqk,bhkd->bhqd', probs, vh)
        out = out.transpose(0, 2, 1, 3).reshape(b, -1, D_MODEL)
        return jnp.einsum('bsd,ed->bse', out, wo) + bo

    def _L1_ffn_ref(hidden_states, W_gate_router, expert_bias, Wg, Wu, Wd, Wg_s, Wu_s, Wd_s):
        import jax, jax.numpy as jnp
        import numpy as np
        TOP_K = 2
        ROUTE_SCALE = 1.0
        EPS = 1e-20
        B, S, D = (2, 64, 128)
        E = 8
        F = 96
        FS = 96 * 1
        b, s, d = hidden_states.shape
        x = hidden_states.reshape(-1, d)
        T = x.shape[0]
        logits = x @ W_gate_router
        scores = jax.nn.sigmoid(logits.astype(jnp.float32))
        _, sel = jax.lax.top_k(scores + expert_bias, TOP_K)
        top_scores = jnp.take_along_axis(scores, sel, axis=1)
        top_scores = top_scores / (top_scores.sum(-1, keepdims=True) + EPS)
        top_scores = top_scores * ROUTE_SCALE
        shared = jax.nn.silu(x @ Wg_s) * (x @ Wu_s) @ Wd_s
        tok = jnp.repeat(jnp.arange(T), TOP_K)
        exp = sel.reshape(-1)
        w = top_scores.reshape(-1)
        xr = x[tok]
        h = jax.nn.silu(jnp.einsum('nd,edf->enf', xr, Wg)) * jnp.einsum('nd,edf->enf', xr, Wu)
        out_all = jnp.einsum('enf,efd->end', h, Wd)
        routed = out_all[exp, jnp.arange(exp.shape[0])]
        routed = (routed.astype(jnp.float32) * w[:, None]).astype(hidden_states.dtype)
        out = shared.at[tok].add(routed)
        return out.reshape(b, s, d)
    x = x + jnp.tanh(g_xattn[0]) * _L0_xattn_ref(_layernorm(x, axis=-1), ctx_1024, L0_xattn_w_q, L0_xattn_w_k, L0_xattn_w_v)
    x = x + jnp.tanh(g_ffn[0]) * _L0_ffn_ref(_layernorm(x, axis=-1), L0_ffn_Wg, L0_ffn_W1, L0_ffn_b1, L0_ffn_W2, L0_ffn_b2)
    x = x + jnp.tanh(g_xattn[1]) * _L1_xattn_ref(_layernorm(x, axis=-1), ctx_1024, ctx_1024, mask_SxS2_bk1, L1_xattn_wq, L1_xattn_bq, L1_xattn_wk, L1_xattn_bk, L1_xattn_wv, L1_xattn_bv, L1_xattn_wo, L1_xattn_bo)
    x = x + jnp.tanh(g_ffn[1]) * _L1_ffn_ref(_layernorm(x, axis=-1), L1_ffn_W_gate_router, L1_ffn_expert_bias, L1_ffn_Wg, L1_ffn_Wu, L1_ffn_Wd, L1_ffn_Wg_s, L1_ffn_Wu_s, L1_ffn_Wd_s)
    return x

_drawn_inputs = setup_inputs


def setup_inputs(seed=0):
    import zlib

    import numpy as np

    out = dict(_drawn_inputs(seed))
    spreads = {'g_ffn': (-1.0, 0.6),
     'L0_ffn_b1': (0.0, 0.8),
     'L0_ffn_b2': (0.0, 0.1),
     'L1_ffn_expert_bias': (0.0, 0.8)}
    factors = {'L0_ffn_W1': 3.059,
     'L1_xattn_bq': 4.397,
     'L1_xattn_bk': 8.0,
     'L1_ffn_W_gate_router': 8.0,
     'L1_ffn_Wg': 8.0,
     'L1_ffn_Wu': 8.0,
     'L1_ffn_Wd': 8.0,
     'L1_ffn_Wg_s': 8.0,
     'L1_ffn_Wu_s': 8.0,
     'L1_ffn_Wd_s': 8.0}
    for name, (base, spread) in spreads.items():
        noise = np.random.default_rng([zlib.crc32(name.encode()), seed]).standard_normal(out[name].shape)
        drawn = base * np.exp(spread * noise) if base else spread * noise
        out[name] = jnp.asarray(drawn.astype(out[name].dtype))
    for name, factor in factors.items():
        out[name] = (out[name] * factor).astype(out[name].dtype)
    return out
```

```python
from contextlib import ExitStack

import concourse.bass as bass
from concourse import mybir

F32 = mybir.dt.float32
F32R = mybir.dt.float32r
BF16 = mybir.dt.bfloat16
F16 = mybir.dt.float16
U8 = mybir.dt.uint8
ALU = mybir.AluOpType
ACT = mybir.ActivationFunctionType
AX = mybir.AxisListType

P = 128
D = 128
NB = 32
TG = 4
NG = NB // TG
GT = TG * P
S2 = 77
SK = 78
GK = TG * SK
E = 8
HC = 2
F1 = 96
FC = 7
NH = 16
DH = 8
HQ = 4
NC4 = NH // HQ
LAG = 3
VW = 10
EPS = 1e-5
EPS_ROUTE = 1e-20
MASK_FILL = -998244352.0
TAKEN = -3.0e38
HALF_RANGE = 10.397207708399179


class Group:

    def __init__(self, i, c):
        self.i, self.c, self.parity = i, c, c % 2

    def at(self, n, k):
        return n * self.c + k if self.i is None else self.i * (2 * n) + (n * self.c + k)

    def pair(self, n, k):
        return n * (self.c // 2) + k if self.i is None else self.i * n + (n * (self.c // 2) + k)

    def tiles(self):
        return bass.ds(self.at(TG, 0), TG)

    def tile(self, t):
        return bass.ds(self.at(TG, t), 1)

    def cols(self, n):
        return bass.ds(self.at(n, 0), n)


def pipeline(eng, step):
    step(Group(None, 0), None, None)
    step(Group(None, 1), Group(None, 0), None)
    with eng.Fori(0, (NG - 2) // 2) as i:
        step(Group(i, 2), Group(i, 1), Group(i, 0))
        step(Group(i, 3), Group(i, 2), Group(i, 1))
    step(None, Group(None, NG - 1), Group(None, NG - 2))
    step(None, None, Group(None, NG - 1))


class Link:

    def __init__(self, eng, sem, g, n):
        self.eng, self.sem, self.g, self.n, self.k = eng, sem, g, n, 0

    def __call__(self, ins, wait=None):
        self.k += 1
        assert self.k <= self.n, "more links than n"
        ins.then_inc(self.sem, 1)
        if wait:
            wait(self.eng, self.sem, self.g.at(self.n, self.k))
        else:
            self.eng.wait_ge(self.sem, self.g.at(self.n, self.k))

    def end(self):
        assert self.k == self.n, (self.k, self.n)


WIDTH = dict(wg0=P, b2=P, sel0=E * P, w1=E * HC * P, w2=E * HC * P, wq=NC4 * P, wg1=P, sel1=FC * P,
             wgu=2 * FC * P, wd=FC * P)
WCOL, NW = {}, 0
for _name, _w in WIDTH.items():
    WCOL[_name] = (NW, NW + _w)
    NW += _w
WPIECE = NW // NG
assert WPIECE * NG == NW and WCOL["wg0"][1] <= WPIECE


def flamingo_kernel(nc, x, ctxT, mask, gates, ident_in, part_in, rank_in, weights, wq0, wk0, wv0T,
                    b1, bqs, wks, bks, wvT, bv, woT, bo, ebias, out):
    ctx = ExitStack()

    scope = [ctx]

    def sb(name, shape, dt=F32):
        return scope[0].enter_context(nc.sbuf_tensor(name, shape, dt))

    def new_scope():
        if scope[0] is not ctx:
            scope[0].close()
        scope[0] = ExitStack()

    def sem(name):
        return ctx.enter_context(nc.semaphore(name))

    with ctx:
        psum = ctx.enter_context(nc.psum_tensor("psum", [P, 8, 512], F32))
        bank = [psum[:, i, :] for i in range(8)]

        x_all = sb("x_all", [P, NB, D])
        xh = sb("xh", [P, NG, GT], F32R)
        xl = sb("xl", [P, NG, GT], F32R)
        logits = sb("logits", [P, NB, E])
        sc_h = sb("sc_h", [P, NB, E], F32R)
        sc_l = sb("sc_l", [P, NB, E], F32R)
        ident = sb("ident", [P, P])
        ident_bf = sb("ident_bf", [P, P], BF16)
        part = sb("part", [P, 2])
        bqlo = sb("bqlo", [P, NC4])
        bklo = sb("bklo", [P, NC4])
        rank = sb("rank", [P, E])
        gate_in = sb("gate_in", [P, 4])
        tg = sb("tg", [P, 4])
        bias_hr = sb("bias_hr", [P, 1])
        zero_col = sb("zero_col", [P, 1])
        half_neg = sb("half_neg", [P, TG])
        w_wq0 = sb("w_wq0", [P, P])
        w_wk0 = sb("w_wk0", [P, P])
        w_m0 = sb("w_m0", [P, P])
        w_wv0 = sb("w_wv0", [P, P])
        b1s = sb("b1s", [P, E, HC])
        w_hi, w_lo = sb("w_hi", [P, NW], F32R), sb("w_lo", [P, NW], F32R)

        def wpart(name):
            c0, c1 = WCOL[name]
            return w_hi[:, c0:c1], w_lo[:, c0:c1]

        (wg0h, wg0l), (wg1h, wg1l) = wpart("wg0"), wpart("wg1")
        (w1h, w1l), (w2h, w2l), (wqh, wql) = wpart("w1"), wpart("w2"), wpart("wq")
        (wguh, wgul), (wdh, wdl), (b2h, b2l) = wpart("wgu"), wpart("wd"), wpart("b2")
        sel0 = wpart("sel0")[0].rearrange("p (e c) -> p e c", e=E)
        sel1 = wpart("sel1")[0].rearrange("p (e c) -> p e c", e=FC)
        wk1 = sb("wk1", [P, NC4 * P])
        bq1 = sb("bq1", [P, NC4])
        bk1 = sb("bk1", [P, NC4])
        wv1 = sb("wv1", [P, P])
        bv1 = sb("bv1", [S2, P])
        wo1 = sb("wo1", [P, P])
        bo1 = sb("bo1", [1, P])
        ones_row = sb("ones_row", [1, P])
        eb1 = sb("eb1", [P, E])
        mask_u8 = sb("mask_u8", [P, S2], U8)
        mask_f = sb("mask_f", [P, SK])
        mask_bf = sb("mask_bf", [P, SK], BF16)
        some_key = sb("some_key", [P, 1])
        exp_scale = sb("exp_scale", [P, 1])

        ctxg = sb("ctxg", [P, 2, GK])
        stats = sb("stats", [P, 2, TG, 6])
        mv = sb("mv", [P, 2, TG, 2])
        vpe = sb("vpe", [P, 2, TG])
        rstd = sb("rstd", [P, 2, TG])
        xn = sb("xn", [P, 2, TG, D])
        lt_s = sb("lt_s", [P, 2, GT])
        ss = sb("ss", [P, 2, TG, P])
        st = sb("st", [P, 2, GT], F32R)
        sg_gate_h, sg_gate_l = sb("sg_gate_h", [P, 1], F32R), sb("sg_gate_l", [P, 1], F32R)
        r1 = {n: sb(f"r1_{n}", [P, NB]) for n in ("m", "m2", "c", "d", "e", "w1", "w2")}
        s_x = [sem(f"x_loaded{i}") for i in range(2)]
        s_small = sem("small_weights_loaded")
        s_dma = [sem("weights_staged0"), sem("weights_staged1")]
        s_split_hi = sem("weights_high_done")
        s_pool = sem("pool_chain")
        s_split = sem("weights_split")
        s_dvec = sem("dve_setup_chain")
        s_dve_setup = sem("dve_setup_done")
        s_tanh = sem("tanh_done")
        s_m0 = sem("m0_product")
        s_m0e = sem("m0_copied")
        s_out = [sem("out_stored0"), sem("out_stored1")]
        s_route = sem("routing_done")
        s_rchain = sem("routing_chain")
        s_re = sem("routing_exp")
        s_ract = sem("routing_act")

        small = [
            (ident[:], ident_in), (part[:], part_in), (rank[:], rank_in), (gate_in[:], gates),
            (w_wq0[:], wq0), (w_wk0[:], wk0), (w_wv0[:], wv0T), (b1s[:], b1),
            (wk1[:], wks), (bq1[:], bqs), (bk1[:], bks), (wv1[:], wvT), (bv1[:], bv), (wo1[:], woT),
            (bo1[:], bo), (eb1[:], ebias), (mask_u8[:], mask),
        ]
        block = ctx.enter_context(nc.Block())

        sp_parts, act_parts, dve_parts, pe_parts, pool_parts = [], [], [], [], []

        spare_v, spare_q = sb("spare_v", [1, 1]), sb("spare_q", [1, 1])

        def wait_apart(eng, s, value):
            eng.wait_ge(s, value)
            if isinstance(value, int):
                return
            if isinstance(eng, bass.BassVectorEngine):
                eng.memset(spare_v[:], 0.0)
            else:
                eng.tensor_tensor(spare_q[:], half_neg[0:1, 0:1], half_neg[0:1, 0:1], ALU.add)

        class LayerNorm:

            def __init__(self, name, t_bank, bufs, to_split=True, dst=None):
                self.bank, self.bufs, self.split, self.dst = t_bank, bufs, to_split, dst
                self.stats_ready = sem(f"{name}_stats_ready")
                self.rstd_ready = sem(f"{name}_rstd_ready")
                self.xn_ready = sem(f"{name}_xn_ready")
                self.t_ready = sem(f"{name}_transposed")
                self.hi_done = sem(f"{name}_high_done")
                self.lo_done = sem(f"{name}_low_done")
                self.chain = sem(f"{name}_dve_chain")
                self.pchain = sem(f"{name}_pool_chain")

            def dve_stats(self, v, g):
                st, m, _, _, _ = self.bufs
                p = g.parity
                link = Link(v, self.chain, g, 1)
                for t in range(TG):
                    ins = v.bn_stats(st[:, p, t, :], x_all[:, g.tile(t), :])
                link(ins, wait_apart)
                for t in range(TG):
                    ins = v.bn_aggr(m[:, p, t, :], st[:, p, t, :])
                ins.then_inc(self.stats_ready, 1)

            def pool_rstd(self, q, g):
                _, m, ve, rs, _ = self.bufs
                p = g.parity
                wait_apart(q, self.stats_ready, g.at(1, 1))
                link = Link(q, self.pchain, g, 1)
                link(q.tensor_scalar(ve[:, p, :], m[:, p, :, 1], EPS, None, ALU.add))
                q.tensor_tensor(rs[:, p, :], ve[:, p, :], half_neg[:], ALU.pow).then_inc(self.rstd_ready, 1)

            def dve_norm(self, v, g):
                _, m, _, rs, xo = self.bufs
                p = g.parity
                v.wait_ge(self.rstd_ready, g.at(1, 1))
                for t in range(TG):
                    ins = v.tensor_scalar(xo[:, p, t, :], x_all[:, g.tile(t), :], m[:, p, t, 0:1],
                                          rs[:, p, t:t + 1], ALU.subtract, ALU.mult)
                ins.then_inc(self.xn_ready, 1)

            def pe_transpose(self, pe, g):
                xo = self.bufs[4]
                pe.wait_ge(self.xn_ready, g.at(1, 1))
                for t in range(TG):
                    ins = pe.transpose(self.bank[:, t * P:(t + 1) * P], xo[:, g.parity, t, :], ident[:])
                ins.then_inc(self.t_ready, 1)

            def act_high(self, a, g):
                a.wait_ge(self.t_ready, g.at(1, 1))
                if self.split:
                    o = xh[:, g.cols(1), :]
                    a.activation(o, self.bank.rearrange("p (a c) -> p a c", a=1), ACT.Copy).then_inc(self.hi_done, 1)
                else:
                    a.activation(self.dst[:, g.parity, :], self.bank, ACT.Copy).then_inc(self.hi_done, 1)

            def dve_low(self, v, g):
                v.wait_ge(self.hi_done, g.at(1, 1))
                v.tensor_tensor(xl[:, g.cols(1), :], self.bank.rearrange("p (a c) -> p a c", a=1),
                                xh[:, g.cols(1), :].bitcast(F32), ALU.subtract).then_inc(self.lo_done, 1)

        class RouterLogits:

            def __init__(self, name, ln, wh, wl, lt_bank, lg_bank):
                self.ln, self.wh, self.wl, self.lt_bank, self.lg_bank = ln, wh, wl, lt_bank, lg_bank
                self.lt_ready = sem(f"{name}_logits_t")
                self.lt_copied = sem(f"{name}_logits_t_copied")
                self.lg_ready = sem(f"{name}_logits_ready")
                self.lg_copied = sem(f"{name}_logits_copied")

            def pe_product(self, pe, g):
                pe.wait_ge(self.ln.lo_done, g.at(1, 1))
                h, l = xh[:, g.cols(1), :], xl[:, g.cols(1), :]
                o = self.lt_bank.rearrange("p (a c) -> p a c", a=1)
                pe.matmul(o, self.wh, h, start=True, stop=False)
                pe.matmul(o, self.wh, l, start=False, stop=False)
                pe.matmul(o, self.wl, h, start=False, stop=True).then_inc(self.lt_ready, 1)

            def act_copy(self, a, g):
                a.wait_ge(self.lt_ready, g.at(1, 1))
                a.activation(lt_s[:, g.parity, :], self.lt_bank, ACT.Copy).then_inc(self.lt_copied, 1)

            def pe_transpose(self, pe, g):
                pe.wait_ge(self.lt_copied, g.at(1, 1))
                for t in range(TG):
                    ins = pe.transpose(self.lg_bank[:, t * P:(t + 1) * P],
                                       lt_s[:, g.parity, t * P:(t + 1) * P], ident[:])
                ins.then_inc(self.lg_ready, 1)

            def dve_copy(self, v, g):
                v.wait_ge(self.lg_ready, g.at(1, 1))
                v.tensor_copy(logits[:, g.tiles(), :],
                              self.lg_bank.rearrange("p (t e) -> p t e", t=TG)[:, :, 0:E]).then_inc(self.lg_copied, 1)

        def product3(pe, o, wh, wl, h, l, start=True, stop=True):
            pe.matmul(o, wh, h, start=start, stop=False)
            pe.matmul(o, wh, l, start=False, stop=False)
            return pe.matmul(o, wl, h, start=False, stop=stop)

        def sp_setup(sp):
            xv = x.rearrange("b p d -> p b d")
            half = NB // 2
            sp.dma_start(x_all[:, 0:half, :], xv[:, 0:half, :]).then_inc(s_x[0], 16)
            for n, (dst, src) in enumerate(small):
                sp.dma_start(dst, src).then_inc(s_small, 16)
            sp.dma_start(x_all[:, half:NB, :], xv[:, half:NB, :]).then_inc(s_x[1], 16)
        sp_parts.append(sp_setup)

        def pool_setup(q):
            q.memset(half_neg[:], -0.5).then_inc(s_pool, 1)
            q.wait_ge(s_pool, 1)
        pool_parts.append(pool_setup)

        def dve_setup(v):
            k = [0]

            def link(ins):
                k[0] += 1
                ins.then_inc(s_dvec, 1)
                v.wait_ge(s_dvec, k[0])
            v.memset(bias_hr[:], HALF_RANGE)
            v.memset(mask_f[:, S2:SK], 0.0)
            v.memset(zero_col[:], 0.0)
            link(v.memset(ones_row[:], 1.0))
            v.wait_ge(s_small, 16 * len(small))
            v.tensor_copy(ident_bf[:], ident[:])
            link(v.tensor_copy(mask_f[:, 0:S2], mask_u8[:]))
            v.tensor_scalar(mask_bf[:], mask_f[:], MASK_FILL, None, ALU.mult)
            link(v.tensor_reduce(some_key[:], mask_f[:, 0:S2], AX.X, ALU.min))
            link(v.tensor_scalar(exp_scale[:], some_key[:], -float(DH) ** -0.5, float(DH) ** -0.5, ALU.mult, ALU.add))
            v.tensor_scalar(bqlo[:], bq1[:], part[:, 0:1], None, ALU.mult)
            v.tensor_scalar(bklo[:], bk1[:], part[:, 1:2], None, ALU.mult).then_inc(s_dve_setup, 1)
        dve_parts.append(dve_setup)

        def act_setup(a):
            a.wait_ge(s_small, 16 * len(small))
            a.activation(tg[:], gate_in[:], ACT.Tanh).then_inc(s_tanh, 1)
            a.wait_ge(s_m0, 1)
            a.activation(w_m0[:], bank[0][:, 0:P], ACT.Copy).then_inc(s_m0e, 1)
        act_parts.append(act_setup)

        def pe_setup(pe):
            pe.wait_ge(s_small, 16 * len(small))
            pe.matmul(bank[0][:, 0:P], w_wk0[:], w_wq0[:], start=True, stop=True).then_inc(s_m0, 1)
            pe.wait_ge(s_dve_setup, 1)
            pe.wait_ge(s_m0e, 1)
        pe_parts.append(pe_setup)

        def pool_split(q, a):
            raw, cols = stage[:, a.parity, :], a.cols(WPIECE)
            wait_apart(q, s_dma[a.parity], a.pair(16, 16))
            q.tensor_copy(w_hi[:, cols], raw).then_inc(s_split_hi, 1)
            q.wait_ge(s_split_hi, a.at(1, 1))
            q.tensor_tensor(w_lo[:, cols], raw, w_hi[:, cols].bitcast(F32), ALU.subtract).then_inc(s_split, 1)

        new_scope()
        stage = sb("stage", [P, 2, WPIECE])
        stats0, mv0 = sb("stats0", [P, 2, TG, 6]), sb("mv0", [P, 2, TG, 2])
        vpe0, rstd0, xn0 = sb("vpe0", [P, 2, TG]), sb("rstd0", [P, 2, TG]), sb("xn0", [P, 2, TG, D])
        with_a = dict(
            xt=sb("a_xt", [P, 2, GT]), k0=sb("a_k0", [P, 2, GK]), v0=sb("a_v0", [S2, 2, GT]),
            sm=sb("a_sm", [P, 2, TG, S2]), pr=sb("a_pr", [P, 2, TG, S2]), mx=sb("a_mx", [P, 2, TG]),
            rs=sb("a_rs", [P, 2, TG]), ri=sb("a_ri", [P, 2, TG]), rg=sb("a_rg", [P, 2, TG]),
            pt=sb("a_pt", [S2, 2, GT]))
        A = with_a
        a_ctx = [sem("a_ctx_loaded0"), sem("a_ctx_loaded1")]
        a_k_ready, a_v_ready = sem("a_keys_ready"), sem("a_values_ready")
        a_k_done, a_v_done = sem("a_keys_copied"), sem("a_values_copied")
        a_s_ready, a_sub = sem("a_scores_ready"), sem("a_scores_shifted")
        a_exp = sem("a_exp_done")
        a_pt_ready, a_pt_done = sem("a_probs_transposed"), sem("a_probs_copied")
        a_o_ready, a_res = sem("a_out_ready"), sem("a_residual_done")
        a_ch1, a_ch2 = sem("a_chain_max"), sem("a_chain_sum")
        a_rg = sem("a_inverse_ready")
        ln0 = LayerNorm("a_ln0", bank[0], (stats0, mv0, vpe0, rstd0, xn0), to_split=False, dst=A["xt"])
        ln1 = LayerNorm("a_ln1", bank[6], (stats, mv, vpe, rstd, xn))
        lg0 = RouterLogits("a_router", ln1, wg0h, wg0l, bank[7], bank[6])

        def sp_a(sp):
            for g in range(NG):
                if g >= 2:
                    sp.wait_ge(a_v_ready, g - 1)
                sp.dma_start(ctxg[:, g % 2, :], ctxT[:, g * GK:(g + 1) * GK]).then_inc(a_ctx[g % 2], 16)
                if g >= 2:
                    sp.wait_ge(s_split, g - 1)
                sp.dma_start(stage[:, g % 2, :], weights[:, g * WPIECE:(g + 1) * WPIECE]).then_inc(s_dma[g % 2], 16)
        sp_parts.append(sp_a)

        def pool_a(q):
            def step(a, m, t):
                if t:
                    ln1.pool_rstd(q, t)
                if a:
                    ln0.pool_rstd(q, a)
                    pool_split(q, a)
            pipeline(q, step)
        pool_parts.append(pool_a)

        def pe_a(pe):
            def step(a, m, t):
                if m:
                    p = m.parity
                    pe.wait_ge(ln0.hi_done, m.at(1, 1))
                    pe.wait_ge(a_k_done, m.at(1, 1))
                    if not (m.i is None and m.c == 0):
                        pe.wait_ge(a_sub, m.at(1, 0))
                    for b in range(TG):
                        ins = pe.matmul(bank[3][:, b * SK:(b + 1) * SK], A["xt"][:, p, b * P:(b + 1) * P],
                                        A["k0"][:, p, b * SK:(b + 1) * SK], start=True, stop=True)
                    ins.then_inc(a_s_ready, 1)
                if a:
                    p = a.parity
                    first = a.i is None and a.c == 0
                    pe.wait_ge(a_ctx[p], a.pair(16, 16))
                    if not first:
                        pe.wait_ge(a_k_done, a.at(1, 0))
                        pe.wait_ge(a_v_done, a.at(1, 0))
                        pe.wait_ge(ln0.hi_done, a.at(1, 0))
                    pe.matmul(bank[1][:, 0:GK], w_m0[:], ctxg[:, p, :], start=True, stop=True).then_inc(a_k_ready, 1)
                    for b in range(TG):
                        ins = pe.matmul(bank[2][0:S2, b * P:(b + 1) * P], ctxg[:, p, b * SK:b * SK + S2],
                                        w_wv0[:], start=True, stop=True)
                    ins.then_inc(a_v_ready, 1)
                    ln0.pe_transpose(pe, a)
                if m:
                    p = m.parity
                    pe.wait_ge(a_exp, m.at(1, 1))
                    if not (m.i is None and m.c == 0):
                        pe.wait_ge(a_pt_done, m.at(1, 0))
                    for b in range(TG):
                        ins = pe.transpose(bank[4][0:S2, b * P:(b + 1) * P], A["pr"][:, p, b, :], ident[:])
                    ins.then_inc(a_pt_ready, 1)
                if t:
                    ln1.pe_transpose(pe, t)
                if m:
                    p = m.parity
                    pe.wait_ge(a_pt_done, m.at(1, 1))
                    pe.wait_ge(a_v_done, m.at(1, 1))
                    if not (m.i is None and m.c == 0):
                        pe.wait_ge(a_res, m.at(1, 0))
                    for b in range(TG):
                        ins = pe.matmul(bank[5][:, b * P:(b + 1) * P], A["pt"][:, p, b * P:(b + 1) * P],
                                        A["v0"][:, p, b * P:(b + 1) * P], start=True, stop=True)
                    ins.then_inc(a_o_ready, 1)
                if t:
                    pe.wait_ge(s_split, t.at(1, 1))
                    lg0.pe_product(pe, t)
                    lg0.pe_transpose(pe, t)
            pipeline(pe, step)
        pe_parts.append(pe_a)

        def act_a(a_):
            def step(a, m, t):
                if a:
                    p = a.parity
                    a_.wait_ge(a_k_ready, a.at(1, 1))
                    a_.activation(A["k0"][:, p, :], bank[1][:, 0:GK], ACT.Copy).then_inc(a_k_done, 1)
                    a_.wait_ge(a_v_ready, a.at(1, 1))
                    a_.activation(A["v0"][:, p, :], bank[2][0:S2, :], ACT.Copy).then_inc(a_v_done, 1)
                    ln0.act_high(a_, a)
                if m:
                    p = m.parity
                    a_.wait_ge(a_sub, m.at(1, 1))
                    a_.activation(A["pr"][:, p, :, :], A["sm"][:, p, :, :], ACT.Exp,
                                  bias=zero_col[:, 0:1], scale=float(D) ** -0.5).then_inc(a_exp, 1)
                    a_.wait_ge(a_pt_ready, m.at(1, 1))
                    a_.activation(A["pt"][:, p, :], bank[4][0:S2, :], ACT.Copy).then_inc(a_pt_done, 1)
                if t:
                    ln1.act_high(a_, t)
                    lg0.act_copy(a_, t)
            pipeline(a_, step)
        act_parts.append(act_a)

        def dve_a(v):
            v.wait_ge(s_x[0], 16)
            v.wait_ge(s_x[1], 16)
            v.wait_ge(s_tanh, 1)

            def step(a, m, t):
                if t:
                    p = t.parity
                    v.wait_ge(a_o_ready, t.at(1, 1))
                    for b in range(TG):
                        ins = v.scalar_tensor_tensor(
                            out=x_all[:, t.tile(b), :], in0=bank[5][:, b * P:(b + 1) * P].rearrange("p (a c) -> p a c", a=1),
                            scalar=A["rg"][:, p, b:b + 1], in1=x_all[:, t.tile(b), :], op0=ALU.mult, op1=ALU.add)
                    ins.then_inc(a_res, 1)
                    wait_apart(v, a_res, t.at(1, 1))
                    ln1.dve_stats(v, t)
                if m:
                    p = m.parity
                    v.wait_ge(a_s_ready, m.at(1, 1))
                    s = bank[3][:, 0:GK].rearrange("p (b k) -> p b k", b=TG)[:, :, 0:S2]
                    link = Link(v, a_ch1, m, 1)
                    link(v.tensor_reduce(A["mx"][:, p, :], s, AX.X, ALU.max))
                    v.tensor_tensor(A["sm"][:, p, :, :], s,
                                    A["mx"][:, p, :].unsqueeze(2).broadcast_to([P, TG, S2]), ALU.subtract).then_inc(a_sub, 1)
                if a:
                    ln0.dve_stats(v, a)
                if t:
                    ln1.dve_norm(v, t)
                if a:
                    if not (a.i is None and a.c < 2):
                        v.wait_ge(ln0.t_ready, a.at(1, -1))
                    ln0.dve_norm(v, a)
                if m:
                    p = m.parity
                    v.wait_ge(a_exp, m.at(1, 1))
                    link = Link(v, a_ch2, m, 2)
                    link(v.tensor_reduce(A["rs"][:, p, :], A["pr"][:, p, :, :], AX.X, ALU.add))
                    link(v.reciprocal(A["ri"][:, p, :], A["rs"][:, p, :]))
                    v.tensor_scalar(A["rg"][:, p, :], A["ri"][:, p, :], tg[:, 0:1], None, ALU.mult).then_inc(a_rg, 1)
                    v.wait_ge(a_rg, m.at(1, 1))
                if t:
                    ln1.dve_low(v, t)
                    lg0.dve_copy(v, t)
            pipeline(v, step)
        dve_parts.append(dve_a)

        new_scope()
        rt = {n: sb(f"r_{n}", [P, NB, E]) for n in ("val", "pick", "tmp", "first", "second", "sig", "wt")}

        def dve_route(v, layer, base, exp_base, rt, r1):
            k = [base]

            def link(ins):
                k[0] += 1
                ins.then_inc(s_rchain, 1)
                v.wait_ge(s_rchain, k[0])

            def bc(t):
                return t[:].unsqueeze(2).broadcast_to([P, NB, E])

            rankb = rank[:].unsqueeze(1).broadcast_to([P, NB, E])

            def pick(values, best, onehot):
                link(v.tensor_reduce(best[:], values, AX.X, ALU.max))
                link(v.tensor_tensor(rt["pick"][:], values, bc(best), ALU.is_ge))
                link(v.tensor_tensor(rt["tmp"][:], rt["pick"][:], rankb, ALU.mult))
                link(v.tensor_reduce(r1["c"][:], rt["tmp"][:], AX.X, ALU.max))
                link(v.tensor_tensor(onehot, rt["tmp"][:], bc(r1["c"]), ALU.is_equal))

            if layer == 0:
                values = logits[:]
            else:
                v.wait_ge(s_re, exp_base + 1)
                link(v.tensor_scalar(rt["tmp"][:], rt["wt"][:], 1.0, None, ALU.add))
                link(v.reciprocal(rt["sig"][:], rt["tmp"][:]))
                link(v.tensor_tensor(rt["val"][:], rt["sig"][:],
                                     eb1[:].unsqueeze(1).broadcast_to([P, NB, E]), ALU.add))
                values = rt["val"][:]
            pick(values, r1["m"], rt["first"][:])
            link(v.scalar_tensor_tensor(out=rt["wt"][:], in0=rt["first"][:], scalar=TAKEN, in1=values,
                                        op0=ALU.mult, op1=ALU.add))
            pick(rt["wt"][:], r1["m2"], rt["second"][:])
            if layer == 0:
                link(v.tensor_tensor(r1["d"][:], r1["m2"][:], r1["m"][:], ALU.subtract))
                v.sem_inc(s_ract, 1)
                v.wait_ge(s_re, exp_base + 1)
                link(v.tensor_scalar(r1["m"][:], r1["e"][:], 1.0, None, ALU.add))
                link(v.reciprocal(r1["w1"][:], r1["m"][:]))
                link(v.tensor_tensor(r1["w2"][:], r1["e"][:], r1["w1"][:], ALU.mult))
                link(v.tensor_tensor(rt["pick"][:], rt["first"][:], bc(r1["w1"]), ALU.mult))
                link(v.tensor_tensor(rt["tmp"][:], rt["second"][:], bc(r1["w2"]), ALU.mult))
                link(v.tensor_tensor(rt["wt"][:], rt["pick"][:], rt["tmp"][:], ALU.add))
            else:
                link(v.tensor_tensor(rt["pick"][:], rt["first"][:], rt["second"][:], ALU.add))
                link(v.tensor_tensor(rt["tmp"][:], rt["pick"][:], rt["sig"][:], ALU.mult))
                link(v.tensor_reduce(r1["d"][:], rt["tmp"][:], AX.X, ALU.add))
                link(v.tensor_scalar(r1["m"][:], r1["d"][:], EPS_ROUTE, None, ALU.add))
                link(v.reciprocal(r1["w1"][:], r1["m"][:]))
                link(v.tensor_tensor(rt["wt"][:], rt["tmp"][:], bc(r1["w1"]), ALU.mult))
            gate = tg[:, 2 + layer:3 + layer]
            link(v.tensor_scalar(rt["pick"][:], rt["wt"][:], gate, None, ALU.mult))
            link(v.tensor_copy(sc_h[:], rt["pick"][:]))
            v.tensor_tensor(sc_l[:], rt["pick"][:], sc_h[:].bitcast(F32), ALU.subtract).then_inc(s_route, 1)
            v.wait_ge(s_route, 1 + layer)
            return k[0]

        links_used, rt_b = [0], rt

        def dve_route0(v):
            v.wait_ge(lg0.lg_copied, NG)
            links_used[0] = dve_route(v, 0, 0, 0, rt_b, r1)
        dve_parts.append(dve_route0)

        def act_route0(a):
            a.wait_ge(s_ract, 1)
            a.activation(r1["e"][:], r1["d"][:], ACT.Exp, bias=zero_col[:, 0:1]).then_inc(s_re, 1)
        act_parts.append(act_route0)


        B = dict(hr=sb("b_hr", [P, 2, HC, GT]), hs=sb("b_hs", [P, 2, HC, GT]),
                 hh=sb("b_hh", [P, 2, HC, GT], F32R), hl=sb("b_hl", [P, 2, HC, GT], F32R),
                 y=sb("b_y", [P, 2, GT]))

        class ExpertPass:

            def __init__(self, name, n, y):
                self.n, self.y = n, y
                self.ss_ready = sem(f"{name}_weights_placed")
                self.ss_chain = sem(f"{name}_weights_chain")
                self.st_ready = sem(f"{name}_weights_transposed")
                self.st_done = sem(f"{name}_weights_copied")
                self.z_ready = sem(f"{name}_hidden_ready")
                self.z_read = sem(f"{name}_hidden_read")
                self.bc_ready = sem(f"{name}_spread_ready")
                self.scaled = sem(f"{name}_hidden_scaled")
                self.hi_done = sem(f"{name}_hidden_high")
                self.lo_done = sem(f"{name}_hidden_low")
                self.used = sem(f"{name}_hidden_used")
                self.y_done = sem(f"{name}_y_copied")
                self.yt_ready = sem(f"{name}_y_transposed")
                self.res = sem(f"{name}_residual_done")

            def first(self, g):
                return g.i is None and g.c == 0

            def before(self, eng, s, g, k, back):
                if g.i is None and self.n * g.c + k - back < 0:
                    return
                eng.wait_ge(s, g.at(self.n, k - back + 1))

            def prev(self, m, t, k, back=1):
                return (m, k - back) if k >= back else (t, self.n + k - back)

            def dve_place(self, v, a):
                p = a.parity
                if not (a.i is None and a.c < 2):
                    v.wait_ge(self.st_ready, a.at(1, -1))
                v.tensor_copy(ss[:, p, :, 0:E], sc_h[:, a.tiles(), :].bitcast(F32))
                v.tensor_copy(ss[:, p, :, 32:32 + E], sc_l[:, a.tiles(), :].bitcast(F32)).then_inc(self.ss_ready, 1)

            def pe_place(self, pe, a, misc):
                pe.wait_ge(self.ss_ready, a.at(1, 1))
                for b in range(TG):
                    ins = pe.transpose(misc[:, b * P:(b + 1) * P], ss[:, a.parity, b, :], ident[:])
                ins.then_inc(self.st_ready, 1)

            def act_place(self, a_, a, misc):
                a_.wait_ge(self.st_ready, a.at(1, 1))
                a_.activation(st[:, a.parity, :], misc, ACT.Copy).then_inc(self.st_done, 1)

            def act_high(self, a_, g, k):
                self.before(a_, self.scaled, g, k, 0)
                self.before(a_, self.used, g, k, 2)
                q = (self.n * g.c + k) % 2
                a_.activation(*self.high(q), ACT.Copy).then_inc(self.hi_done, 1)

            def dve_low(self, v, g, k):
                self.before(v, self.hi_done, g, k, 0)
                q = (self.n * g.c + k) % 2
                o, i0, i1 = self.low(q)
                v.tensor_tensor(o, i0, i1, ALU.subtract).then_inc(self.lo_done, 1)

            def act_y(self, a_, t, ybank):
                a_.wait_ge(self.used, t.at(self.n, self.n))
                a_.activation(self.y[:, t.parity, :], ybank, ACT.Copy).then_inc(self.y_done, 1)

            def pe_y(self, pe, t, misc):
                pe.wait_ge(self.y_done, t.at(1, 1))
                for b in range(TG):
                    ins = pe.transpose(misc[:, b * P:(b + 1) * P], self.y[:, t.parity, b * P:(b + 1) * P], ident[:])
                ins.then_inc(self.yt_ready, 1)

            def dve_residual(self, v, t, misc):
                v.wait_ge(self.yt_ready, t.at(1, 1))
                xt = x_all[:, t.tiles(), :]
                v.tensor_tensor(xt, misc.rearrange("p (b c) -> p b c", b=TG), xt, ALU.add).then_inc(self.res, 1)
                wait_apart(v, self.res, t.at(1, 1))

        Z, SBC, Y, MISC = [bank[0:2], bank[2:4]], [bank[4], bank[5]], bank[6], bank[7]
        xb = ExpertPass("b", E, B["y"])
        Bb = B
        xb.high = lambda q: (Bb["hh"][:, q, :, :], Bb["hs"][:, q, :, :])
        xb.low = lambda q: (Bb["hl"][:, q, :, :], Bb["hs"][:, q, :, :], Bb["hh"][:, q, :, :].bitcast(F32))
        ln2 = LayerNorm("b_ln", MISC, (stats, mv, vpe, rstd, xn))

        def w1s(w, e, c):
            return w[:, (e * HC + c) * P:(e * HC + c + 1) * P]

        def pe_b(pe):
            pe.wait_ge(s_split, NG)
            pe.wait_ge(ln1.lo_done, NG)

            def up(g, e):
                q = e % 2
                h, l = xh[:, g.cols(1), :], xl[:, g.cols(1), :]
                xb.before(pe, xb.z_read, g, e, 2)
                for c in range(HC):
                    o = Z[q][c].rearrange("p (a c) -> p a c", a=1)
                    ins = product3(pe, o, w1s(w1h, e, c), w1s(w1l, e, c), h, l)
                ins.then_inc(xb.z_ready, 1)
                if e == 0:
                    pe.wait_ge(xb.st_done, g.at(1, 1))
                xb.before(pe, xb.scaled, g, e, 2)
                pe.matmul(SBC[q], sel0[:, e, :], st[:, g.parity, :], start=True, stop=True).then_inc(xb.bc_ready, 1)

            def down(g, e):
                q = e % 2
                if e == 0:
                    if not xb.first(g):
                        pe.wait_ge(xb.y_done, g.at(1, 0))
                    pe.matmul(Y, b2h, st[:, g.parity, :], start=True, stop=False)
                    pe.matmul(Y, b2l, st[:, g.parity, :], start=False, stop=False)
                xb.before(pe, xb.lo_done, g, e, 0)
                for c in range(HC):
                    ins = product3(pe, Y, w1s(w2h, e, c), w1s(w2l, e, c), Bb["hh"][:, q, c, :], Bb["hl"][:, q, c, :],
                                   start=False, stop=(e == E - 1 and c == HC - 1))
                ins.then_inc(xb.used, 1)

            def place(a):
                xb.pe_place(pe, a, MISC)

            def y_back(a, t):
                if a:
                    pe.wait_ge(xb.st_done, a.at(1, 1))
                elif not xb.first(t):
                    pe.wait_ge(ln2.lo_done, t.at(1, 0))
                xb.pe_y(pe, t, MISC)

            def step(a, m, t):
                for e in range(E if m else LAG):
                    if m:
                        up(m, e)
                    g, k = xb.prev(m, t, e, LAG)
                    if g:
                        down(g, k)
                    if m and e == 1 and a:
                        place(a)
                    if m and e == 4 and t:
                        y_back(a, t)
                    if m and e == 7 and t:
                        ln2.pe_transpose(pe, t)
                if not m:
                    if a:
                        place(a)
                    if t:
                        y_back(a, t)
                        ln2.pe_transpose(pe, t)
            pipeline(pe, step)
        pe_parts.append(pe_b)

        def act_b(a_):
            def relu(g, e):
                q = e % 2
                xb.before(a_, xb.z_ready, g, e, 0)
                xb.before(a_, xb.scaled, g, e, 2)
                for c in range(HC):
                    ins = a_.activation(Bb["hr"][:, q, c, :], Z[q][c], ACT.Relu, bias=b1s[:, e, c:c + 1])
                ins.then_inc(xb.z_read, 1)

            def step(a, m, t):
                if m:
                    for e in range(E):
                        if e == LAG and t:
                            xb.act_y(a_, t, Y)
                        relu(m, e)
                        g, k = xb.prev(m, t, e)
                        if g:
                            xb.act_high(a_, g, k)
                        if e == 2 and a:
                            xb.act_place(a_, a, MISC)
                        if e == 7 and t:
                            ln2.act_high(a_, t)
                else:
                    if t:
                        xb.act_high(a_, t, E - 1)
                        xb.act_y(a_, t, Y)
                    if a:
                        xb.act_place(a_, a, MISC)
                    if t:
                        ln2.act_high(a_, t)
            pipeline(a_, step)
        act_parts.append(act_b)

        def dve_b(v):
            v.memset(ss[:], 0.0).then_inc(xb.ss_chain, 1)
            v.wait_ge(xb.ss_chain, 1)

            def scale(g, e):
                q = e % 2
                xb.before(v, xb.z_read, g, e, 0)
                xb.before(v, xb.bc_ready, g, e, 0)
                xb.before(v, xb.lo_done, g, e, 2)
                v.tensor_tensor(Bb["hs"][:, q, :, :], Bb["hr"][:, q, :, :],
                                SBC[q].unsqueeze(1).broadcast_to([P, HC, GT]), ALU.mult).then_inc(xb.scaled, 1)

            def low(g, k):
                xb.before(v, xb.used, g, k, 2)
                xb.dve_low(v, g, k)

            def step(a, m, t):
                if m:
                    for e in range(E):
                        scale(m, e)
                        g, k = xb.prev(m, t, e)
                        if g:
                            low(g, k)
                        if e == 0 and a:
                            xb.dve_place(v, a)
                        if e == 5 and t:
                            xb.dve_residual(v, t, MISC)
                            ln2.dve_stats(v, t)
                        if e == 6 and t:
                            ln2.dve_norm(v, t)
                        if e == 7 and t:
                            ln2.dve_low(v, t)
                else:
                    if a:
                        xb.dve_place(v, a)
                    if t:
                        low(t, E - 1)
                        xb.dve_residual(v, t, MISC)
                        ln2.dve_stats(v, t)
                        ln2.dve_norm(v, t)
                        ln2.dve_low(v, t)
            pipeline(v, step)
        dve_parts.append(dve_b)

        def pool_b(q):
            def step(a, m, t):
                if t:
                    ln2.pool_rstd(q, t)
            pipeline(q, step)
        pool_parts.append(pool_b)

        new_scope()
        NU = 9
        NQ = TG * NC4
        NHALF = NQ // 2
        w1_0, w1_1 = WCOL["w1"][0], WCOL["w2"][1]
        qs = w_hi[:, w1_0:w1_1].rearrange("p (a c t) -> p a c t", a=2, c=NC4)
        ks = w_lo[:, w1_0:w1_0 + 2 * NC4 * GK].rearrange("p (a c b k) -> p a c b k", a=2, c=NC4, b=TG)
        kb = sb("c_kb", [P, 2, NC4, HQ, SK], F32R)
        lowpart = sb("c_lowpart", [P, 2, GT], F32R)
        v3 = sb("c_v3", [S2, 2, TG, NH, 3, VW], BF16)
        vf = sb("c_vf", [S2, TG * D])
        vr = sb("c_vr", [S2, TG * D])
        vr2 = sb("c_vr2", [S2, TG * D])
        mx1 = sb("c_mx", [P, 2, 2 * HQ])
        sm1 = sb("c_sm", [P, 2, 2 * HQ, S2])
        pf1 = sb("c_pf", [P, 2, 2 * HQ, S2])
        ph = sb("c_ph", [S2, 2, HQ * P], F16)
        pl_ = sb("c_pl", [S2, 2, HQ * P], F16)
        o10 = sb("c_o10", [P, NH, VW])
        oi = sb("c_oi", [P, NH])
        on = sb("c_on", [P, 2, TG, D])
        ot = sb("c_ot", [P, 2, GT])
        c_ctx = [sem("c_ctx_loaded0"), sem("c_ctx_loaded1")]
        u_ready, u_act, u_read = sem("c_prep_ready"), sem("c_prep_low"), sem("c_prep_read")
        v_ready, v_split, v_chain = sem("c_values_ready"), sem("c_values_split"), sem("c_values_chain")
        kb_zero, kb_ready = sem("c_keys_cleared"), sem("c_keys_placed")
        s1_ready, s1_max, s1_sub, s1_exp = sem("c_scores"), sem("c_max"), sem("c_shifted"), sem("c_exp")
        t1_ready, hi_done, lo_done, pv_used = sem("c_probs_t"), sem("c_probs_high"), sem("c_probs_low"), sem("c_pv")
        o_read, o_inv, o_done = sem("c_out_summed"), sem("c_out_inverse"), sem("c_out_normed")
        ot_ready, ot_done = sem("c_out_transposed"), sem("c_out_t_copied")
        wo_ready, c_res = sem("c_projected"), sem("c_residual_done")
        M1 = bank[6]
        MU = [bank[5], bank[7]]
        ln3 = LayerNorm("c_ln", M1, (stats, mv, vpe, rstd, xn))
        lg1 = RouterLogits("c_router", ln3, wg1h, wg1l, M1, M1)

        def before(eng, s, n, g, k, back=0, wait=None):
            if g.i is None and n * g.c + k - back < 0:
                return
            if wait:
                wait(eng, s, g.at(n, k - back + 1))
            else:
                eng.wait_ge(s, g.at(n, k - back + 1))

        def lagged(m, t, k):
            return (m, k) if k >= 0 else (t, NQ + k)

        def sp_c(sp):
            for g in range(NG):
                if g < 2:
                    sp.wait_ge(a_v_ready, NG)
                else:
                    sp.wait_ge(u_ready, NU * (g - 1))
                sp.dma_start(ctxg[:, g % 2, :], ctxT[:, g * GK:(g + 1) * GK]).then_inc(c_ctx[g % 2], 16)
        sp_parts.append(sp_c)

        def pe_c(pe):
            def prepare(a, u):
                p = a.parity
                o = MU[(NU * a.c + u) % 2]
                before(pe, u_read, NU, a, u, 2)
                if u < NC4:
                    w = slice(u * P, (u + 1) * P)
                    ins = product3(pe, o.rearrange("p (a c) -> p a c", a=1), wqh[:, w], wql[:, w],
                                   xh[:, a.cols(1), :], xl[:, a.cols(1), :])
                elif u < 2 * NC4:
                    if u == NC4:
                        pe.wait_ge(c_ctx[p], a.pair(16, 16))
                    c = u - NC4
                    ins = pe.matmul(o[:, 0:GK], wk1[:, c * P:(c + 1) * P], ctxg[:, p, :], start=True, stop=True)
                else:
                    for b in range(TG):
                        ins = pe.matmul(o[0:S2, b * D:(b + 1) * D], ctxg[:, p, b * SK:b * SK + S2], wv1[:],
                                        start=True, stop=True)
                ins.then_inc(u_ready, 1)

            def scores(m, h):
                b = h // 2
                before(pe, s1_sub, NHALF, m, h, 1)
                if h == 0:
                    pe.wait_ge(u_read, m.at(NU, NU))
                if h % 2 == 0:
                    pe.wait_ge(kb_ready, m.at(TG, b + 1))
                for k in range(2):
                    c = (h % 2) * 2 + k
                    o = bank[k][:, 0:GK]
                    pe.matmul(o, ident_bf[:], mask_bf[:].unsqueeze(1).broadcast_to([P, HQ, SK]), start=True, stop=False)
                    ins = pe.matmul(o, qs[:, m.parity, c, b * P:(b + 1) * P],
                                    kb[:, b % 2, c, :, :].rearrange("p j k -> p (j k)"), start=False, stop=True)
                ins.then_inc(s1_ready, 1)

            def transpose(g, q):
                h = q // 2
                before(pe, s1_exp, NHALF, g, h)
                before(pe, lo_done, NQ, g, q, 2)
                for j in range(HQ):
                    ins = pe.transpose(bank[2 + q % 2][0:S2, j * P:(j + 1) * P],
                                       pf1[:, h % 2, (q % 2) * HQ + j, :], ident[:])
                ins.then_inc(t1_ready, 1)

            def values(g, q):
                b, c = q // NC4, q % NC4
                before(pe, lo_done, NQ, g, q)
                if c == 0:
                    before(pe, o_read, TG, g, b, 1)
                    if b == 0:
                        pe.wait_ge(v_split, g.at(1, 1))
                for j in range(HQ):
                    h = c * HQ + j
                    o = bank[4][:, h * 3 * VW:(h + 1) * 3 * VW]
                    vv = v3[:, g.parity, b, h, :, :].rearrange("p s d -> p (s d)")
                    pe.matmul(o, ph[:, q % 2, j * P:(j + 1) * P], vv, start=True, stop=False)
                    ins = pe.matmul(o, pl_[:, q % 2, j * P:(j + 1) * P], vv, start=False, stop=True)
                ins.then_inc(pv_used, 1)

            def turn_out(t):
                pe.wait_ge(o_done, t.at(TG, TG))
                for b in range(TG):
                    ins = pe.transpose(M1[:, b * P:(b + 1) * P], on[:, t.parity, b, :], ident[:])
                ins.then_inc(ot_ready, 1)

            def project(t):
                pe.wait_ge(ot_done, t.at(1, 1))
                for b in range(TG):
                    o = M1[:, b * P:(b + 1) * P]
                    pe.matmul(o, ones_row[:], bo1[:], start=True, stop=False)
                    ins = pe.matmul(o, ot[:, t.parity, b * P:(b + 1) * P], wo1[:], start=False, stop=True)
                ins.then_inc(wo_ready, 1)

            def step(a, m, t):
                for i in range(NQ):
                    if m and i % 2 == 0:
                        scores(m, i // 2)
                    g, q = lagged(m, t, i - 3)
                    if g:
                        transpose(g, q)
                    g, q = lagged(m, t, i - 5)
                    if g:
                        values(g, q)
                    if a and 0 <= i - 5 < NU:
                        prepare(a, i - 5)
                    if t and i == 7:
                        turn_out(t)
                    if t and i == 9:
                        project(t)
                    if t and i == 12:
                        ln3.pe_transpose(pe, t)
                    if t and i == 13:
                        lg1.pe_product(pe, t)
                    if t and i == 15:
                        lg1.pe_transpose(pe, t)
            pe.wait_ge(ln2.lo_done, NG)
            pipeline(pe, step)
        pe_parts.append(pe_c)

        def act_c(a_):
            def prepare(a, u):
                o = MU[(NU * a.c + u) % 2]
                k, c, w = (0, u, GT) if u < NC4 else (1, u - NC4, GK)
                before(a_, u_ready, NU, a, u)
                blo = (bqlo, bklo)[k]
                a_.activation(lowpart[:, (NU * a.c + u) % 2, 0:w], o[:, 0:w], ACT.Identity, bias=blo[:, c:c + 1],
                              scale=part[:, k:k + 1]).then_inc(u_act, 1)

            def high(g, q):
                before(a_, t1_ready, NQ, g, q)
                before(a_, pv_used, NQ, g, q, 2)
                a_.activation(ph[:, q % 2, :], bank[2 + q % 2][0:S2, :], ACT.Copy).then_inc(hi_done, 1)

            def exp(m, h):
                before(a_, s1_sub, NHALF, m, h)
                before(a_, t1_ready, NQ, m, 2 * h + 1, 4)
                a_.activation(pf1[:, h % 2, :, :], sm1[:, h % 2, :, :], ACT.Exp, bias=bias_hr[:, 0:1],
                              scale=exp_scale[:, 0:1]).then_inc(s1_exp, 1)

            def step(a, m, t):
                for i in range(NQ):
                    g, q = lagged(m, t, i - 3)
                    if g:
                        high(g, q)
                    if m and i % 2 == 1:
                        exp(m, i // 2)
                    if a and 0 <= i - 5 < NU - 1:
                        prepare(a, i - 5)
                    if t and i == 8:
                        a_.wait_ge(ot_ready, t.at(1, 1))
                        a_.activation(ot[:, t.parity, :], M1, ACT.Copy).then_inc(ot_done, 1)
                    if t and i == 12:
                        ln3.act_high(a_, t)
                    if t and i == 14:
                        lg1.act_copy(a_, t)
            pipeline(a_, step)
        act_parts.append(act_c)

        def dve_c(v):
            def prepare(a, u):
                p = a.parity
                o = MU[(NU * a.c + u) % 2]
                lp = lowpart[:, (NU * a.c + u) % 2, :].bitcast(F32)
                if u < NC4:
                    before(v, u_act, NU - 1, a, u)
                    v.scalar_tensor_tensor(out=qs[:, p, u, :], in0=o, scalar=bq1[:, u:u + 1], in1=lp,
                                           op0=ALU.add, op1=ALU.subtract).then_inc(u_read, 1)
                elif u < 2 * NC4:
                    c = u - NC4
                    before(v, u_act, NU - 1, a, u)
                    v.scalar_tensor_tensor(out=ks[:, p, c, :, :].rearrange("p b k -> p (b k)"), in0=o[:, 0:GK],
                                           scalar=bk1[:, c:c + 1], in1=lp[:, 0:GK],
                                           op0=ALU.add, op1=ALU.subtract).then_inc(u_read, 1)
                else:
                    before(v, u_ready, NU, a, u)
                    before(v, v_split, 1, a, 0, 1)
                    v.tensor_tensor(vf[:].rearrange("p (b d) -> p b d", b=TG), o[0:S2, :].rearrange("p (b d) -> p b d", b=TG),
                                    bv1[:].unsqueeze(1).broadcast_to([S2, TG, D]), ALU.add).then_inc(u_read, 1)

            def shift(m, h):
                before(v, s1_ready, NHALF, m, h)
                before(v, s1_exp, NHALF, m, h, 2)
                s = psum[:, 0:2, 0:GK].rearrange("p k (j s) -> p k j s", j=HQ)[:, :, :, 0:S2]
                mm = mx1[:, h % 2, :].rearrange("p (k j) -> p k j", k=2)
                v.tensor_reduce(mm, s, AX.X, ALU.max).then_inc(s1_max, 1)
                before(v, s1_max, NHALF, m, h)
                v.tensor_tensor(sm1[:, h % 2, :, :].rearrange("p (k j) s -> p k j s", k=2), s,
                                mm.unsqueeze(3).broadcast_to([P, 2, HQ, S2]), ALU.subtract).then_inc(s1_sub, 1)

            def low(g, q):
                before(v, hi_done, NQ, g, q)
                before(v, pv_used, NQ, g, q, 2)
                v.tensor_tensor(pl_[:, q % 2, :], bank[2 + q % 2][0:S2, :], ph[:, q % 2, :], ALU.subtract).then_inc(lo_done, 1)

            def combine(g, b):
                before(v, pv_used, NQ, g, NC4 * b + NC4 - 1)
                v.tensor_reduce(o10[:], bank[4][:, 0:NH * 3 * VW].rearrange("p (h s d) -> p h d s", h=NH, s=3),
                                AX.X, ALU.add).then_inc(o_read, 1)
                before(v, o_read, TG, g, b)
                v.reciprocal(oi[:], o10[:, :, DH]).then_inc(o_inv, 1)
                before(v, o_inv, TG, g, b)
                v.tensor_tensor(on[:, g.parity, b, :].rearrange("p (h d) -> p h d", h=NH), o10[:, :, 0:DH],
                                oi[:].unsqueeze(2).broadcast_to([P, NH, DH]), ALU.mult).then_inc(o_done, 1)

            def residual(t):
                v.wait_ge(wo_ready, t.at(1, 1))
                xt = x_all[:, t.tiles(), :].rearrange("p b d -> p (b d)")
                v.scalar_tensor_tensor(out=xt, in0=M1, scalar=tg[:, 1:2], in1=xt,
                                       op0=ALU.mult, op1=ALU.add).then_inc(c_res, 1)
                wait_apart(v, c_res, t.at(1, 1))

            def step(a, m, t):
                for i in range(NQ):
                    if m and i % 2 == 0:
                        shift(m, i // 2)
                    g, q = lagged(m, t, i - 3)
                    if g:
                        low(g, q)
                    if i % NC4 == 0:
                        g, q = lagged(m, t, i - 8)
                        if g:
                            combine(g, q // NC4)
                    if a and 0 <= i - 6 < NU:
                        prepare(a, i - 6)
                    if t and i == 10:
                        residual(t)
                        ln3.dve_stats(v, t)
                    if t and i == 11:
                        ln3.dve_norm(v, t)
                    if t and i == 13:
                        ln3.dve_low(v, t)
                    if t and i == 15:
                        lg1.dve_copy(v, t)
            pipeline(v, step)
        dve_parts.append(dve_c)

        def pool_c(q_):
            q_.wait_ge(ln2.lo_done, NG)
            q_.memset(kb[:].bitcast(F32), 0.0).then_inc(kb_zero, 1)
            q_.memset(v3[:], 0.0).then_inc(kb_zero, 1)
            q_.wait_ge(kb_zero, 2)
            q_.memset(v3[:, :, :, :, 0, DH:DH + 1], 1.0).then_inc(kb_zero, 1)
            q_.wait_ge(kb_zero, 3)

            def split_values(a):
                before(q_, u_read, NU, a, NU - 1)
                p = a.parity
                link = Link(q_, v_chain, a, 4)

                def heads(t):
                    return t[:].rearrange("p (b h d) -> p b h d", b=TG, h=NH)

                def split(s):
                    return v3[:, p, :, :, s, 0:DH]
                before(q_, pv_used, NQ, a, NQ - 1, 2 * NQ, wait_apart)
                link(q_.tensor_copy(split(0), heads(vf)))
                link(q_.tensor_tensor(heads(vr), heads(vf), split(0), ALU.subtract), wait_apart)
                link(q_.tensor_copy(split(1), heads(vr)))
                link(q_.tensor_tensor(heads(vr2), heads(vr), split(1), ALU.subtract), wait_apart)
                q_.tensor_copy(split(2), heads(vr2)).then_inc(v_split, 1)
                q_.wait_ge(v_split, a.at(1, 1))

            def place_keys(m, b):
                before(q_, u_read, NU, m, 2 * NC4 - 1)
                before(q_, s1_ready, NHALF, m, 2 * b + 1, 4, wait_apart)
                for j in range(HQ):
                    r = slice(4 * DH * j, 4 * DH * (j + 1))
                    ins = q_.tensor_copy(kb[r, b % 2, :, j, :], ks[r, m.parity, :, b, :])
                ins.then_inc(kb_ready, 1)
                q_.wait_ge(kb_ready, m.at(TG, b + 1))

            def step(a, m, t):
                if m:
                    place_keys(m, 0)
                    place_keys(m, 1)
                    place_keys(m, 2)
                    place_keys(m, 3)
                if t:
                    ln3.pool_rstd(q_, t)
                if a:
                    split_values(a)
            pipeline(q_, step)
        pool_parts.append(pool_c)


        new_scope()
        rt = {n: sb(f"r1_{n}_all", [P, NB, E]) for n in ("val", "pick", "tmp", "first", "second", "sig", "wt")}
        B = dict(hr=sb("d_hr", [P, 2, HC, GT]), hs=sb("d_hs", [P, 2, 1, GT]),
                 hh=sb("d_hh", [P, 2, 1, GT], F32R), hl=sb("d_hl", [P, 2, 1, GT], F32R),
                 y=sb("d_y", [P, 2, GT]))
        xd = ExpertPass("d", FC, B["y"])
        sg = B["hr"]
        d_silu, d_mul = sem("d_silu_done"), sem("d_product_done")
        xd.high = lambda q: (B["hh"][:, q, 0, :], B["hs"][:, q, 0, :])
        xd.low = lambda q: (B["hl"][:, q, 0, :], B["hs"][:, q, 0, :], B["hh"][:, q, 0, :].bitcast(F32))

        def act_route1(a):
            a.wait_ge(lg1.lg_copied, NG)
            a.activation(rt["wt"][:], logits[:], ACT.Exp, bias=zero_col[:, 0:1], scale=-1.0).then_inc(s_re, 1)
        act_parts.append(act_route1)

        def dve_route1(v):
            dve_route(v, 1, links_used[0], 1, rt, r1)
        dve_parts.append(dve_route1)

        def gus(w, k, c):
            return w[:, (k * FC + c) * P:(k * FC + c + 1) * P]

        def pe_d(pe):
            pe.wait_ge(ln3.lo_done, NG)

            def up(g, e):
                q = (FC * g.c + e) % 2
                h, l = xh[:, g.cols(1), :], xl[:, g.cols(1), :]
                xd.before(pe, d_mul, g, e, 2)
                for k in range(2):
                    o = Z[q][k].rearrange("p (a c) -> p a c", a=1)
                    ins = product3(pe, o, gus(wguh, k, e), gus(wgul, k, e), h, l)
                ins.then_inc(xd.z_ready, 1)
                if e == 0:
                    pe.wait_ge(xd.st_done, g.at(1, 1))
                xd.before(pe, xd.scaled, g, e, 2)
                pe.matmul(SBC[q], sel1[:, e, :], st[:, g.parity, :], start=True, stop=True).then_inc(xd.bc_ready, 1)

            def down(g, e):
                q = (FC * g.c + e) % 2
                if e == 0 and not xd.first(g):
                    pe.wait_ge(xd.y_done, g.at(1, 0))
                xd.before(pe, xd.lo_done, g, e, 0)
                product3(pe, Y, wdh[:, e * P:(e + 1) * P], wdl[:, e * P:(e + 1) * P], B["hh"][:, q, 0, :],
                         B["hl"][:, q, 0, :], start=(e == 0), stop=(e == FC - 1)).then_inc(xd.used, 1)

            def place(a):
                xd.pe_place(pe, a, MISC)

            def y_back(a, t):
                if a:
                    pe.wait_ge(xd.st_done, a.at(1, 1))
                elif not xd.first(t):
                    pe.wait_ge(xd.res, t.at(1, 0))
                xd.pe_y(pe, t, MISC)

            def step(a, m, t):
                for e in range(FC if m else LAG):
                    if m:
                        up(m, e)
                    g, k = xd.prev(m, t, e, LAG)
                    if g:
                        down(g, k)
                    if m and e == 1 and a:
                        place(a)
                    if m and e == 5 and t:
                        y_back(a, t)
                if not m:
                    if a:
                        place(a)
                    if t:
                        y_back(a, t)
            pipeline(pe, step)
        pe_parts.append(pe_d)

        def act_d(a_):
            def silu(g, e):
                q = (FC * g.c + e) % 2
                xd.before(a_, xd.z_ready, g, e, 0)
                xd.before(a_, d_mul, g, e, 2)
                a_.activation(sg[:, q, 0, :], Z[q][0], ACT.Silu).then_inc(d_silu, 1)

            def step(a, m, t):
                if m:
                    for e in range(FC):
                        if e == LAG and t:
                            xd.act_y(a_, t, Y)
                        silu(m, e)
                        g, k = xd.prev(m, t, e)
                        if g:
                            xd.act_high(a_, g, k)
                        if e == 2 and a:
                            xd.act_place(a_, a, MISC)
                else:
                    if t:
                        xd.act_high(a_, t, FC - 1)
                        xd.act_y(a_, t, Y)
                    if a:
                        xd.act_place(a_, a, MISC)
            pipeline(a_, step)
        act_parts.append(act_d)

        def dve_d(v):
            v.tensor_copy(sg_gate_h[:], tg[:, 3:4]).then_inc(xd.ss_chain, 1)
            v.wait_ge(xd.ss_chain, 1)
            v.tensor_tensor(sg_gate_l[:], tg[:, 3:4], sg_gate_h[:].bitcast(F32), ALU.subtract).then_inc(xd.ss_chain, 1)
            v.wait_ge(xd.ss_chain, 2)
            v.tensor_copy(ss[:, :, :, E:E + 1].rearrange("p a b c -> p (a b) c"),
                          sg_gate_h[:].bitcast(F32).unsqueeze(1).broadcast_to([P, 2 * TG, 1]))
            v.tensor_copy(ss[:, :, :, 32 + E:33 + E].rearrange("p a b c -> p (a b) c"),
                          sg_gate_l[:].bitcast(F32).unsqueeze(1).broadcast_to([P, 2 * TG, 1]))

            def mul(g, e):
                q = (FC * g.c + e) % 2
                xd.before(v, d_silu, g, e, 0)
                v.tensor_tensor(sg[:, q, 1, :], sg[:, q, 0, :], Z[q][1], ALU.mult).then_inc(d_mul, 1)

            def scale(g, e):
                q = (FC * g.c + e) % 2
                xd.before(v, d_mul, g, e, 0)
                xd.before(v, xd.bc_ready, g, e, 0)
                xd.before(v, xd.lo_done, g, e, 2)
                v.tensor_tensor(B["hs"][:, q, 0, :], sg[:, q, 1, :], SBC[q], ALU.mult).then_inc(xd.scaled, 1)

            def low(g, k):
                xd.before(v, xd.used, g, k, 2)
                xd.dve_low(v, g, k)

            def step(a, m, t):
                if m:
                    for e in range(FC):
                        mul(m, e)
                        g, k = xd.prev(m, t, e)
                        if g:
                            low(g, k)
                        scale(m, e)
                        if e == 0 and a:
                            xd.dve_place(v, a)
                        if e == 6 and t:
                            xd.dve_residual(v, t, MISC)
                else:
                    if a:
                        xd.dve_place(v, a)
                    if t:
                        low(t, FC - 1)
                        xd.dve_residual(v, t, MISC)
            pipeline(v, step)
        dve_parts.append(dve_d)

        def sp_d(sp):
            ov = out.rearrange("b p d -> p b d")
            with sp.Fori(0, NG // 2) as i:
                for c in range(2):
                    g = Group(i, c)
                    sp.wait_ge(xd.res, g.at(1, 1))
                    sp.dma_start(ov[:, g.tiles(), :], x_all[:, g.tiles(), :]).then_inc(s_out[c], 16)
            for c in range(2):
                sp.wait_ge(s_out[c], 16 * (NG // 2))
        sp_parts.append(sp_d)

        scope[0].close()

        @block.sync
        def _(sp):
            for f in sp_parts:
                f(sp)

        @block.gpsimd
        def _(q):
            for f in pool_parts:
                f(q)

        @block.scalar
        def _(a):
            for f in act_parts:
                f(a)

        @block.vector
        def _(v):
            for f in dve_parts:
                f(v)

        @block.tensor
        def _(pe):
            for f in pe_parts:
                f(pe)


_OUT_SHAPE = (NB, P, D)


def kernel(**inputs):
    import numpy as np
    import concourse.bacc as bacc
    from concourse.bass_utils import run_bass_kernel_spmd

    a = {k: np.asarray(v) for k, v in inputs.items()}
    z = lambda *shape: np.zeros(shape, np.float32)

    ctxT = z(D, NB, SK)
    ctxT[:, :, :S2] = a["ctx_1024"].transpose(2, 0, 1)
    gates = np.broadcast_to(np.concatenate([a["g_xattn"], a["g_ffn"]])[None, :], (P, 4))

    def stack(w):
        o = np.zeros(w.shape[:-1] + (NC4, HQ, 4, DH), np.float32)
        o[..., 0:3, :] = w.reshape(w.shape[:-1] + (NC4, HQ, 1, DH))
        return o.reshape(w.shape[:-1] + (NC4 * P,))

    def columns(v):
        return stack(v).reshape(NC4, P).T

    def side_by_side(w):
        n = -(-w.shape[0] // P)
        o = z(n * P, w.shape[1])
        o[:w.shape[0]] = w
        return o.reshape(n, P, w.shape[1]).transpose(1, 0, 2).reshape(P, -1)

    def router(w):
        o = z(D, P)
        o[:, :E] = w
        return o

    def hidden(experts, shared):
        o = z(D, FC * P)
        o[:, :E * F1] = experts.transpose(1, 0, 2).reshape(D, E * F1)
        o[:, E * F1:(E + 1) * F1] = shared
        return o

    b2 = z(P, D)
    b2[0:E] = a["L0_ffn_b2"]
    b2[32:32 + E] = a["L0_ffn_b2"]
    part = {
        "wg0": router(a["L0_ffn_Wg"]), "b2": b2,
        "w1": a["L0_ffn_W1"].transpose(1, 0, 2).reshape(D, -1),
        "w2": side_by_side(a["L0_ffn_W2"].reshape(-1, D)),
        "wq": stack(a["L1_xattn_wq"].T), "wg1": router(a["L1_ffn_W_gate_router"]),
        "wgu": np.concatenate([hidden(a["L1_ffn_Wg"], a["L1_ffn_Wg_s"]),
                               hidden(a["L1_ffn_Wu"], a["L1_ffn_Wu_s"])], 1),
        "wd": side_by_side(np.concatenate([a["L1_ffn_Wd"].reshape(-1, D), a["L1_ffn_Wd_s"]])),
    }
    sel0, sel1 = z(P, E, P), z(P, FC, P)
    for e in range(E):
        sel0[[e, 32 + e], e, :] = 1.0
    for r in range(FC * P):
        e = r // F1
        if e <= E:
            sel1[[e, 32 + e], r // P, r % P] = 1.0
    part["sel0"], part["sel1"] = sel0.reshape(P, -1), sel1.reshape(P, -1)
    lows = z(P, 2)
    rows = np.arange(P) % (4 * DH) // DH
    lows[rows == 2, 0] = 1.0
    lows[rows == 1, 1] = 1.0
    rank = np.broadcast_to(np.arange(E, 0, -1).astype(np.float32)[None, :], (P, E))

    arrays = dict(
        x=a["x"], ctxT=ctxT.reshape(D, -1), mask=a["mask_SxS2_bk1"], gates=gates, ident_in=np.eye(P, dtype=np.float32),
        part_in=lows, rank_in=rank, weights=np.concatenate([part[n] for n in WIDTH], 1),
        wq0=a["L0_xattn_w_q"], wk0=a["L0_xattn_w_k"], wv0T=a["L0_xattn_w_v"].T,
        b1=a["L0_ffn_b1"].reshape(E, HC, P).transpose(2, 0, 1),
        bqs=columns(a["L1_xattn_bq"]), wks=stack(a["L1_xattn_wk"].T), bks=columns(a["L1_xattn_bk"]),
        wvT=a["L1_xattn_wv"].T, bv=np.broadcast_to(a["L1_xattn_bv"][None, :], (S2, D)),
        woT=a["L1_xattn_wo"].T, bo=a["L1_xattn_bo"][None, :],
        ebias=np.broadcast_to(a["L1_ffn_expert_bias"][None, :], (P, E)))

    nc = bacc.Bacc("TRN2", target_bir_lowering=False, num_devices=1)
    maps, args = {}, {}
    for name, v in arrays.items():
        v = np.ascontiguousarray(v)
        maps[f"in_{name}"] = v
        args[name] = nc.dram_tensor(f"in_{name}", v.shape, mybir.dt.from_np(v.dtype), kind="ExternalInput").ap()
    args["out"] = nc.dram_tensor("out_dram", _OUT_SHAPE, F32, kind="ExternalOutput").ap()
    flamingo_kernel(nc, **args)
    r = run_bass_kernel_spmd(nc, [maps], core_ids=[0])
    return r.results[0]["out_dram"]
```

```python
from contextlib import ExitStack

import concourse.bass as bass
from concourse import mybir

F32 = mybir.dt.float32
F32R = mybir.dt.float32r
BF16 = mybir.dt.bfloat16
F16 = mybir.dt.float16
U8 = mybir.dt.uint8
ALU = mybir.AluOpType
ACT = mybir.ActivationFunctionType
AX = mybir.AxisListType

P = 128
D = 128
NB = 32
TG = 4
NG = NB // TG
GT = TG * P
S2 = 77
SK = 78
GK = TG * SK
E = 8
HC = 2
F1 = 96
FC = 7
NH = 16
DH = 8
HQ = 4
NC4 = NH // HQ
LAG = 3
VW = 10
EPS = 1e-5
EPS_ROUTE = 1e-20
MASK_FILL = -998244352.0
TAKEN = -3.0e38
HALF_RANGE = 10.397207708399179


class Group:

    def __init__(self, i, c):
        self.i, self.c, self.parity = i, c, c % 2

    def at(self, n, k):
        return n * self.c + k if self.i is None else self.i * (2 * n) + (n * self.c + k)

    def pair(self, n, k):
        return n * (self.c // 2) + k if self.i is None else self.i * n + (n * (self.c // 2) + k)

    def tiles(self):
        return bass.ds(self.at(TG, 0), TG)

    def tile(self, t):
        return bass.ds(self.at(TG, t), 1)

    def cols(self, n):
        return bass.ds(self.at(n, 0), n)


def pipeline(eng, step):
    step(Group(None, 0), None, None)
    step(Group(None, 1), Group(None, 0), None)
    with eng.Fori(0, (NG - 2) // 2) as i:
        step(Group(i, 2), Group(i, 1), Group(i, 0))
        step(Group(i, 3), Group(i, 2), Group(i, 1))
    step(None, Group(None, NG - 1), Group(None, NG - 2))
    step(None, None, Group(None, NG - 1))


class Link:

    def __init__(self, eng, sem, g, n):
        self.eng, self.sem, self.g, self.n, self.k = eng, sem, g, n, 0

    def __call__(self, ins, wait=None):
        self.k += 1
        assert self.k <= self.n, "more links than n"
        ins.then_inc(self.sem, 1)
        if wait:
            wait(self.eng, self.sem, self.g.at(self.n, self.k))
        else:
            self.eng.wait_ge(self.sem, self.g.at(self.n, self.k))

    def end(self):
        assert self.k == self.n, (self.k, self.n)


WIDTH = dict(wg0=P, b2=P, sel0=E * P, w1=E * HC * P, w2=E * HC * P, wq=NC4 * P, wg1=P, sel1=FC * P,
             wgu=2 * FC * P, wd=FC * P)
WCOL, NW = {}, 0
for _name, _w in WIDTH.items():
    WCOL[_name] = (NW, NW + _w)
    NW += _w
WPIECE = NW // NG
assert WPIECE * NG == NW and WCOL["wg0"][1] <= WPIECE


def flamingo_kernel(nc, x, ctxT, mask, gates, ident_in, part_in, rank_in, weights, wq0, wk0, wv0T,
                    b1, bqs, wks, bks, wvT, bv, woT, bo, ebias, out):
    ctx = ExitStack()

    scope = [ctx]

    def sb(name, shape, dt=F32):
        return scope[0].enter_context(nc.sbuf_tensor(name, shape, dt))

    def new_scope():
        if scope[0] is not ctx:
            scope[0].close()
        scope[0] = ExitStack()

    def sem(name):
        return ctx.enter_context(nc.semaphore(name))

    with ctx:
        psum = ctx.enter_context(nc.psum_tensor("psum", [P, 8, 512], F32))
        bank = [psum[:, i, :] for i in range(8)]

        x_all = sb("x_all", [P, NB, D])
        xh = sb("xh", [P, NG, GT], F32R)
        xl = sb("xl", [P, NG, GT], F32R)
        logits = sb("logits", [P, NB, E])
        sc_h = sb("sc_h", [P, NB, E], F32R)
        sc_l = sb("sc_l", [P, NB, E], F32R)
        ident = sb("ident", [P, P])
        ident_bf = sb("ident_bf", [P, P], BF16)
        part = sb("part", [P, 2])
        bqlo = sb("bqlo", [P, NC4])
        bklo = sb("bklo", [P, NC4])
        rank = sb("rank", [P, E])
        gate_in = sb("gate_in", [P, 4])
        tg = sb("tg", [P, 4])
        bias_hr = sb("bias_hr", [P, 1])
        zero_col = sb("zero_col", [P, 1])
        half_neg = sb("half_neg", [P, TG])
        w_wq0 = sb("w_wq0", [P, P])
        w_wk0 = sb("w_wk0", [P, P])
        w_m0 = sb("w_m0", [P, P])
        w_wv0 = sb("w_wv0", [P, P])
        b1s = sb("b1s", [P, E, HC])
        w_hi, w_lo = sb("w_hi", [P, NW], F32R), sb("w_lo", [P, NW], F32R)

        def wpart(name):
            c0, c1 = WCOL[name]
            return w_hi[:, c0:c1], w_lo[:, c0:c1]

        (wg0h, wg0l), (wg1h, wg1l) = wpart("wg0"), wpart("wg1")
        (w1h, w1l), (w2h, w2l), (wqh, wql) = wpart("w1"), wpart("w2"), wpart("wq")
        (wguh, wgul), (wdh, wdl), (b2h, b2l) = wpart("wgu"), wpart("wd"), wpart("b2")
        sel0 = wpart("sel0")[0].rearrange("p (e c) -> p e c", e=E)
        sel1 = wpart("sel1")[0].rearrange("p (e c) -> p e c", e=FC)
        wk1 = sb("wk1", [P, NC4 * P])
        bq1 = sb("bq1", [P, NC4])
        bk1 = sb("bk1", [P, NC4])
        wv1 = sb("wv1", [P, P])
        bv1 = sb("bv1", [P, 1])
        wo1 = sb("wo1", [P, P])
        bo1 = sb("bo1", [1, P])
        bo_all = sb("bo_all", [1, P])
        ones_row = sb("ones_row", [1, P])
        eb1 = sb("eb1", [P, E])
        mask_u8 = sb("mask_u8", [P, S2], U8)
        mask_f = sb("mask_f", [P, SK])
        mask_bf = sb("mask_bf", [P, SK], BF16)
        some_key = sb("some_key", [P, 1])
        exp_scale = sb("exp_scale", [P, 1])

        ctxg = sb("ctxg", [P, 2, GK])
        stats = sb("stats", [P, 2, TG, 6])
        mv = sb("mv", [P, 2, TG, 2])
        vpe = sb("vpe", [P, 2, TG])
        rstd = sb("rstd", [P, 2, TG])
        xn = sb("xn", [P, 2, TG, D])
        lt_s = sb("lt_s", [P, 2, GT])
        ss = sb("ss", [P, 2, TG, P])
        st = sb("st", [P, 2, GT], F32R)
        sg_gate_h, sg_gate_l = sb("sg_gate_h", [P, 1], F32R), sb("sg_gate_l", [P, 1], F32R)
        r1 = {n: sb(f"r1_{n}", [P, NB]) for n in ("m", "m2", "c", "d", "e", "w1", "w2")}
        s_x = [sem(f"x_loaded{i}") for i in range(2)]
        s_first = sem("first_weights_loaded")
        s_small = sem("small_weights_loaded")
        s_dma = [sem("weights_staged0"), sem("weights_staged1")]
        s_split_hi = sem("weights_high_done")
        s_pool = sem("pool_chain")
        s_split = sem("weights_split")
        s_dvec = sem("dve_setup_chain")
        s_dve_setup = sem("dve_setup_done")
        s_tanh = sem("tanh_done")
        s_m0 = sem("m0_product")
        s_m0e = sem("m0_copied")
        s_out = [sem("out_stored0"), sem("out_stored1")]
        s_route = sem("routing_done")
        s_rchain = sem("routing_chain")
        s_re = sem("routing_exp")
        s_ract = sem("routing_act")

        first = [
            (w_wq0[:], wq0), (w_wk0[:], wk0), (w_wv0[:], wv0T), (gate_in[:], gates), (ident[:], ident_in),
        ]
        small = [
            (part[:], part_in), (rank[:], rank_in), (b1s[:], b1),
            (wk1[:], wks), (bq1[:], bqs), (bk1[:], bks), (wv1[:], wvT), (bv1[:], bv), (wo1[:], woT),
            (bo1[:], bo), (eb1[:], ebias), (mask_u8[:], mask),
        ]
        block = ctx.enter_context(nc.Block())

        sp_parts, act_parts, dve_parts, pe_parts, pool_parts = [], [], [], [], []

        spare_v, spare_q = sb("spare_v", [1, 1]), sb("spare_q", [1, 1])

        def wait_apart(eng, s, value):
            eng.wait_ge(s, value)
            if isinstance(value, int):
                return
            if isinstance(eng, bass.BassVectorEngine):
                eng.memset(spare_v[:], 0.0)
            else:
                eng.tensor_tensor(spare_q[:], half_neg[0:1, 0:1], half_neg[0:1, 0:1], ALU.add)

        class LayerNorm:

            def __init__(self, name, t_bank, bufs, to_split=True, dst=None):
                self.bank, self.bufs, self.split, self.dst = t_bank, bufs, to_split, dst
                self.stats_ready = sem(f"{name}_stats_ready")
                self.rstd_ready = sem(f"{name}_rstd_ready")
                self.xn_ready = sem(f"{name}_xn_ready")
                self.t_ready = sem(f"{name}_transposed")
                self.hi_done = sem(f"{name}_high_done")
                self.lo_done = sem(f"{name}_low_done")
                self.chain = sem(f"{name}_dve_chain")
                self.pchain = sem(f"{name}_pool_chain")
                self.centred = sem(f"{name}_centred")

            def dve_stats(self, v, g):
                st, m, _, _, _ = self.bufs
                p = g.parity
                link = Link(v, self.chain, g, 1)
                for t in range(TG):
                    ins = v.bn_stats(st[:, p, t, :], x_all[:, g.tile(t), :])
                link(ins, wait_apart)
                for t in range(TG):
                    ins = v.bn_aggr(m[:, p, t, :], st[:, p, t, :])
                ins.then_inc(self.stats_ready, 1)

            def pool_rstd(self, q, g):
                _, m, ve, rs, _ = self.bufs
                p = g.parity
                wait_apart(q, self.stats_ready, g.at(1, 1))
                link = Link(q, self.pchain, g, 1)
                link(q.tensor_scalar(ve[:, p, :], m[:, p, :, 1], EPS, None, ALU.add))
                q.tensor_tensor(rs[:, p, :], ve[:, p, :], half_neg[:], ALU.pow).then_inc(self.rstd_ready, 1)

            def dve_norm(self, v, g):
                _, m, _, rs, xo = self.bufs
                p = g.parity
                v.wait_ge(self.rstd_ready, g.at(1, 1))
                for t in range(TG):
                    ins = v.tensor_scalar(xo[:, p, t, :], x_all[:, g.tile(t), :], m[:, p, t, 0:1],
                                          rs[:, p, t:t + 1], ALU.subtract, ALU.mult)
                ins.then_inc(self.xn_ready, 1)

            def pool_norm(self, q, g):
                _, m, _, rs, xo = self.bufs
                p = g.parity
                q.tensor_tensor(xo[:, p], x_all[:, g.tiles(), :],
                                m[:, p, :, 0:1].broadcast_to([P, TG, D]), ALU.subtract).then_inc(self.centred, 1)
                q.wait_ge(self.rstd_ready, g.at(1, 1))
                q.wait_ge(self.centred, g.at(1, 1))
                q.tensor_tensor(xo[:, p], xo[:, p], rs[:, p, :].unsqueeze(2).broadcast_to([P, TG, D]),
                                ALU.mult).then_inc(self.xn_ready, 1)

            def pe_transpose(self, pe, g):
                xo = self.bufs[4]
                pe.wait_ge(self.xn_ready, g.at(1, 1))
                for t in range(TG):
                    ins = pe.transpose(self.bank[:, t * P:(t + 1) * P], xo[:, g.parity, t, :], ident[:])
                ins.then_inc(self.t_ready, 1)

            def act_high(self, a, g):
                a.wait_ge(self.t_ready, g.at(1, 1))
                if self.split:
                    o = xh[:, g.cols(1), :]
                    a.activation(o, self.bank.rearrange("p (a c) -> p a c", a=1), ACT.Copy).then_inc(self.hi_done, 1)
                else:
                    a.activation(self.dst[:, g.parity, :], self.bank, ACT.Copy).then_inc(self.hi_done, 1)

            def dve_low(self, v, g):
                v.wait_ge(self.hi_done, g.at(1, 1))
                v.tensor_tensor(xl[:, g.cols(1), :], self.bank.rearrange("p (a c) -> p a c", a=1),
                                xh[:, g.cols(1), :].bitcast(F32), ALU.subtract).then_inc(self.lo_done, 1)

        class RouterLogits:

            def __init__(self, name, ln, wh, wl, lt_bank, lg_bank):
                self.ln, self.wh, self.wl, self.lt_bank, self.lg_bank = ln, wh, wl, lt_bank, lg_bank
                self.lt_ready = sem(f"{name}_logits_t")
                self.lt_copied = sem(f"{name}_logits_t_copied")
                self.lg_ready = sem(f"{name}_logits_ready")
                self.lg_copied = sem(f"{name}_logits_copied")

            def pe_product(self, pe, g):
                pe.wait_ge(self.ln.lo_done, g.at(1, 1))
                h, l = xh[:, g.cols(1), :], xl[:, g.cols(1), :]
                o = self.lt_bank.rearrange("p (a c) -> p a c", a=1)
                pe.matmul(o, self.wh, h, start=True, stop=False)
                pe.matmul(o, self.wh, l, start=False, stop=False)
                pe.matmul(o, self.wl, h, start=False, stop=True).then_inc(self.lt_ready, 1)

            def act_copy(self, a, g):
                a.wait_ge(self.lt_ready, g.at(1, 1))
                a.activation(lt_s[:, g.parity, :], self.lt_bank, ACT.Copy).then_inc(self.lt_copied, 1)

            def pe_transpose(self, pe, g):
                pe.wait_ge(self.lt_copied, g.at(1, 1))
                for t in range(TG):
                    ins = pe.transpose(self.lg_bank[:, t * P:(t + 1) * P],
                                       lt_s[:, g.parity, t * P:(t + 1) * P], ident[:])
                ins.then_inc(self.lg_ready, 1)

            def dve_copy(self, v, g):
                v.wait_ge(self.lg_ready, g.at(1, 1))
                v.tensor_copy(logits[:, g.tiles(), :],
                              self.lg_bank.rearrange("p (t e) -> p t e", t=TG)[:, :, 0:E]).then_inc(self.lg_copied, 1)

        def product3(pe, o, wh, wl, h, l, start=True, stop=True):
            pe.matmul(o, wh, h, start=start, stop=False)
            pe.matmul(o, wh, l, start=False, stop=False)
            return pe.matmul(o, wl, h, start=False, stop=stop)

        def sp_x(sp, g):
            xv = x.rearrange("b p d -> p b d")
            sp.dma_start(x_all[:, g * TG:(g + 1) * TG, :], xv[:, g * TG:(g + 1) * TG, :]).then_inc(s_x[g % 2], 16)

        def sp_setup(sp):
            for dst, src in first:
                sp.dma_start(dst, src).then_inc(s_first, 16)
            sp_x(sp, 0)
        sp_parts.append(sp_setup)

        def pool_setup(q):
            q.memset(half_neg[:], -0.5).then_inc(s_pool, 1)
            q.wait_ge(s_pool, 1)
        pool_parts.append(pool_setup)

        def dve_setup(v):
            v.memset(zero_col[:], 0.0).then_inc(s_dvec, 1)
        dve_parts.append(dve_setup)

        def act_setup(a):
            a.wait_ge(s_first, 16 * len(first))
            a.activation(tg[:], gate_in[:], ACT.Tanh).then_inc(s_tanh, 1)
            a.wait_ge(s_m0, 1)
            a.activation(w_m0[:], bank[0][:, 0:P], ACT.Copy).then_inc(s_m0e, 1)
            a.wait_ge(s_dvec, 1)
        act_parts.append(act_setup)

        def pe_setup(pe):
            pe.wait_ge(s_first, 16 * len(first))
            pe.matmul(bank[0][:, 0:P], w_wk0[:], w_wq0[:], start=True, stop=True).then_inc(s_m0, 1)
            pe.wait_ge(s_m0e, 1)
        pe_parts.append(pe_setup)

        def dve_setup_late(v):
            k = [1]

            def link(ins):
                k[0] += 1
                ins.then_inc(s_dvec, 1)
                v.wait_ge(s_dvec, k[0])
            v.memset(bias_hr[:], HALF_RANGE)
            v.memset(mask_f[:, S2:SK], 0.0)
            link(v.memset(ones_row[:], 1.0))
            v.wait_ge(s_small, 16 * len(small))
            v.tensor_copy(ident_bf[:], ident[:])
            link(v.tensor_copy(mask_f[:, 0:S2], mask_u8[:]))
            v.tensor_scalar(mask_bf[:], mask_f[:], MASK_FILL, None, ALU.mult)
            link(v.tensor_reduce(some_key[:], mask_f[:, 0:S2], AX.X, ALU.min))
            link(v.tensor_scalar(exp_scale[:], some_key[:], -float(DH) ** -0.5, float(DH) ** -0.5, ALU.mult, ALU.add))
            v.tensor_scalar(bqlo[:], bq1[:], part[:, 0:1], None, ALU.mult)
            v.tensor_scalar(bklo[:], bk1[:], part[:, 1:2], None, ALU.mult).then_inc(s_dve_setup, 1)

        def act_setup_late(a):
            a.wait_ge(s_m0, 2)
            a.activation(bo_all[:], bank[1][0:1, 0:P], ACT.Copy).then_inc(s_m0e, 1)

        def pe_setup_late(pe):
            pe.wait_ge(s_dve_setup, 1)
            pe.wait_ge(a_k_done, NG)
            pe.matmul(bank[1][0:1, 0:P], bv1[:], wo1[:], start=True, stop=False)
            pe.matmul(bank[1][0:1, 0:P], ones_row[:, 0:1], bo1[:], start=False, stop=True).then_inc(s_m0, 1)
            pe.wait_ge(s_m0e, 2)

        def act_split(a_, a):
            a_.wait_ge(s_dma[a.parity], a.pair(16, 16))
            a_.activation(w_hi[:, a.cols(WPIECE)], stage[:, a.parity, :], ACT.Copy).then_inc(s_split_hi, 1)

        def pool_split(q, a):
            q.wait_ge(s_split_hi, a.at(1, 1))
            cols = a.cols(WPIECE)
            q.tensor_tensor(w_lo[:, cols], stage[:, a.parity, :], w_hi[:, cols].bitcast(F32),
                            ALU.subtract).then_inc(s_split, 1)

        new_scope()
        stage = sb("stage", [P, 2, WPIECE])
        stats0, mv0 = sb("stats0", [P, 2, TG, 6]), sb("mv0", [P, 2, TG, 2])
        vpe0, rstd0, xn0 = sb("vpe0", [P, 2, TG]), sb("rstd0", [P, 2, TG]), sb("xn0", [P, 2, TG, D])
        with_a = dict(
            xt=sb("a_xt", [P, 2, GT]), k0=sb("a_k0", [P, 2, GK]), v0=sb("a_v0", [S2, 2, GT]),
            sm=sb("a_sm", [P, 2, TG, S2]), pr=sb("a_pr", [P, 2, TG, S2]), mx=sb("a_mx", [P, 2, TG]),
            rs=sb("a_rs", [P, 2, TG]), ri=sb("a_ri", [P, 2, TG]), rg=sb("a_rg", [P, 2, TG]),
            pt=sb("a_pt", [S2, 2, GT]))
        A = with_a
        a_ctx = [sem("a_ctx_loaded0"), sem("a_ctx_loaded1")]
        a_k_ready, a_v_ready = sem("a_keys_ready"), sem("a_values_ready")
        a_k_done, a_v_done = sem("a_keys_copied"), sem("a_values_copied")
        a_s_ready, a_sub = sem("a_scores_ready"), sem("a_scores_shifted")
        a_exp = sem("a_exp_done")
        a_pt_ready, a_pt_done = sem("a_probs_transposed"), sem("a_probs_copied")
        a_o_ready, a_res = sem("a_out_ready"), sem("a_residual_done")
        a_ch1, a_ch2 = sem("a_chain_max"), sem("a_chain_sum")
        a_rg = sem("a_inverse_ready")
        ln0 = LayerNorm("a_ln0", bank[0], (stats0, mv0, vpe0, rstd0, xn0), to_split=False, dst=A["xt"])
        ln1 = LayerNorm("a_ln1", bank[6], (stats, mv, vpe, rstd, xn))
        lg0 = RouterLogits("a_router", ln1, wg0h, wg0l, bank[7], bank[6])

        def sp_a(sp):
            for g in range(NG):
                if g >= 2:
                    sp.wait_ge(a_v_ready, g - 1)
                sp.dma_start(ctxg[:, g % 2, :], ctxT[:, g * GK:(g + 1) * GK]).then_inc(a_ctx[g % 2], 16)
                if g + 1 < NG:
                    if g >= 1:
                        sp.wait_ge(ln0.stats_ready, g)
                    sp_x(sp, g + 1)
                if g == 2:
                    for dst, src in small:
                        sp.dma_start(dst, src).then_inc(s_small, 16)
                if g >= 2:
                    sp.wait_ge(s_split, g - 1)
                sp.dma_start(stage[:, g % 2, :], weights[:, g * WPIECE:(g + 1) * WPIECE]).then_inc(s_dma[g % 2], 16)
        sp_parts.append(sp_a)

        def pool_a(q):
            def step(a, m, t):
                if t:
                    ln1.pool_rstd(q, t)
                if a:
                    ln0.pool_rstd(q, a)
                    pool_split(q, a)
            pipeline(q, step)
        pool_parts.append(pool_a)

        def pe_a(pe):
            def step(a, m, t):
                if m:
                    p = m.parity
                    pe.wait_ge(ln0.hi_done, m.at(1, 1))
                    pe.wait_ge(a_k_done, m.at(1, 1))
                    if not (m.i is None and m.c == 0):
                        pe.wait_ge(a_sub, m.at(1, 0))
                    for b in range(TG):
                        ins = pe.matmul(bank[3][:, b * SK:(b + 1) * SK], A["xt"][:, p, b * P:(b + 1) * P],
                                        A["k0"][:, p, b * SK:(b + 1) * SK], start=True, stop=True)
                    ins.then_inc(a_s_ready, 1)
                if a:
                    p = a.parity
                    first = a.i is None and a.c == 0
                    pe.wait_ge(a_ctx[p], a.pair(16, 16))
                    if not first:
                        pe.wait_ge(a_k_done, a.at(1, 0))
                        pe.wait_ge(a_v_done, a.at(1, 0))
                        pe.wait_ge(ln0.hi_done, a.at(1, 0))
                    pe.matmul(bank[1][:, 0:GK], w_m0[:], ctxg[:, p, :], start=True, stop=True).then_inc(a_k_ready, 1)
                    for b in range(TG):
                        ins = pe.matmul(bank[2][0:S2, b * P:(b + 1) * P], ctxg[:, p, b * SK:b * SK + S2],
                                        w_wv0[:], start=True, stop=True)
                    ins.then_inc(a_v_ready, 1)
                if m:
                    p = m.parity
                    pe.wait_ge(a_exp, m.at(1, 1))
                    if not (m.i is None and m.c == 0):
                        pe.wait_ge(a_pt_done, m.at(1, 0))
                    for b in range(TG):
                        ins = pe.transpose(bank[4][0:S2, b * P:(b + 1) * P], A["pr"][:, p, b, :], ident[:])
                    ins.then_inc(a_pt_ready, 1)
                if t:
                    ln1.pe_transpose(pe, t)
                if m:
                    p = m.parity
                    pe.wait_ge(a_pt_done, m.at(1, 1))
                    pe.wait_ge(a_v_done, m.at(1, 1))
                    if not (m.i is None and m.c == 0):
                        pe.wait_ge(a_res, m.at(1, 0))
                    for b in range(TG):
                        ins = pe.matmul(bank[5][:, b * P:(b + 1) * P], A["pt"][:, p, b * P:(b + 1) * P],
                                        A["v0"][:, p, b * P:(b + 1) * P], start=True, stop=True)
                    ins.then_inc(a_o_ready, 1)
                if a:
                    ln0.pe_transpose(pe, a)
                if t:
                    if t.i is None and t.c == 0:
                        pe.wait_ge(s_split, 1)
                    lg0.pe_product(pe, t)
                    lg0.pe_transpose(pe, t)
            pipeline(pe, step)
        pe_parts.append(pe_a)

        def act_a(a_):
            def step(a, m, t):
                if a:
                    p = a.parity
                    a_.wait_ge(a_k_ready, a.at(1, 1))
                    a_.activation(A["k0"][:, p, :], bank[1][:, 0:GK], ACT.Copy).then_inc(a_k_done, 1)
                    a_.wait_ge(a_v_ready, a.at(1, 1))
                    a_.activation(A["v0"][:, p, :], bank[2][0:S2, :], ACT.Copy).then_inc(a_v_done, 1)
                if m:
                    p = m.parity
                    a_.wait_ge(a_sub, m.at(1, 1))
                    a_.activation(A["pr"][:, p, :, :], A["sm"][:, p, :, :], ACT.Exp,
                                  bias=zero_col[:, 0:1], scale=float(D) ** -0.5).then_inc(a_exp, 1)
                    a_.wait_ge(a_pt_ready, m.at(1, 1))
                    a_.activation(A["pt"][:, p, :], bank[4][0:S2, :], ACT.Copy).then_inc(a_pt_done, 1)
                if a:
                    act_split(a_, a)
                if t:
                    ln1.act_high(a_, t)
                if a:
                    ln0.act_high(a_, a)
                if t:
                    lg0.act_copy(a_, t)
            pipeline(a_, step)
        act_parts.append(act_a)

        def dve_a(v):

            def step(a, m, t):
                if t:
                    p = t.parity
                    v.wait_ge(a_o_ready, t.at(1, 1))
                    for b in range(TG):
                        ins = v.scalar_tensor_tensor(
                            out=x_all[:, t.tile(b), :], in0=bank[5][:, b * P:(b + 1) * P].rearrange("p (a c) -> p a c", a=1),
                            scalar=A["rg"][:, p, b:b + 1], in1=x_all[:, t.tile(b), :], op0=ALU.mult, op1=ALU.add)
                    ins.then_inc(a_res, 1)
                    wait_apart(v, a_res, t.at(1, 1))
                    ln1.dve_stats(v, t)
                if m:
                    p = m.parity
                    v.wait_ge(a_s_ready, m.at(1, 1))
                    s = bank[3][:, 0:GK].rearrange("p (b k) -> p b k", b=TG)[:, :, 0:S2]
                    link = Link(v, a_ch1, m, 1)
                    link(v.tensor_reduce(A["mx"][:, p, :], s, AX.X, ALU.max))
                    v.tensor_tensor(A["sm"][:, p, :, :], s,
                                    A["mx"][:, p, :].unsqueeze(2).broadcast_to([P, TG, S2]), ALU.subtract).then_inc(a_sub, 1)
                if a:
                    wait_apart(v, s_x[a.parity], a.pair(16, 16))
                    ln0.dve_stats(v, a)
                if t:
                    ln1.dve_norm(v, t)
                if a:
                    if not (a.i is None and a.c < 2):
                        v.wait_ge(ln0.t_ready, a.at(1, -1))
                    ln0.dve_norm(v, a)
                if m:
                    p = m.parity
                    v.wait_ge(a_exp, m.at(1, 1))
                    link = Link(v, a_ch2, m, 2)
                    link(v.tensor_reduce(A["rs"][:, p, :], A["pr"][:, p, :, :], AX.X, ALU.add))
                    link(v.reciprocal(A["ri"][:, p, :], A["rs"][:, p, :]))
                    if m.i is None and m.c == 0:
                        v.wait_ge(s_tanh, 1)
                    v.tensor_scalar(A["rg"][:, p, :], A["ri"][:, p, :], tg[:, 0:1], None, ALU.mult).then_inc(a_rg, 1)
                    v.wait_ge(a_rg, m.at(1, 1))
                if t:
                    ln1.dve_low(v, t)
                    lg0.dve_copy(v, t)
            pipeline(v, step)
        dve_parts.append(dve_a)

        new_scope()
        rt = {n: sb(f"r_{n}", [P, NB, E]) for n in ("val", "pick", "tmp", "first", "second", "sig", "wt")}

        def dve_route(v, layer, base, exp_base, rt, r1):
            k = [base]

            def link(ins):
                k[0] += 1
                ins.then_inc(s_rchain, 1)
                v.wait_ge(s_rchain, k[0])

            def bc(t):
                return t[:].unsqueeze(2).broadcast_to([P, NB, E])

            rankb = rank[:].unsqueeze(1).broadcast_to([P, NB, E])

            def pick(values, best, onehot):
                link(v.tensor_reduce(best[:], values, AX.X, ALU.max))
                link(v.tensor_tensor(rt["pick"][:], values, bc(best), ALU.is_ge))
                link(v.tensor_tensor(rt["tmp"][:], rt["pick"][:], rankb, ALU.mult))
                link(v.tensor_reduce(r1["c"][:], rt["tmp"][:], AX.X, ALU.max))
                link(v.tensor_tensor(onehot, rt["tmp"][:], bc(r1["c"]), ALU.is_equal))

            if layer == 0:
                values = logits[:]
            else:
                v.wait_ge(s_re, exp_base + 1)
                link(v.tensor_scalar(rt["tmp"][:], rt["wt"][:], 1.0, None, ALU.add))
                link(v.reciprocal(rt["sig"][:], rt["tmp"][:]))
                link(v.tensor_tensor(rt["val"][:], rt["sig"][:],
                                     eb1[:].unsqueeze(1).broadcast_to([P, NB, E]), ALU.add))
                values = rt["val"][:]
            pick(values, r1["m"], rt["first"][:])
            link(v.scalar_tensor_tensor(out=rt["wt"][:], in0=rt["first"][:], scalar=TAKEN, in1=values,
                                        op0=ALU.mult, op1=ALU.add))
            pick(rt["wt"][:], r1["m2"], rt["second"][:])
            if layer == 0:
                link(v.tensor_tensor(r1["d"][:], r1["m2"][:], r1["m"][:], ALU.subtract))
                v.sem_inc(s_ract, 1)
                v.wait_ge(s_re, exp_base + 1)
                link(v.tensor_scalar(r1["m"][:], r1["e"][:], 1.0, None, ALU.add))
                link(v.reciprocal(r1["w1"][:], r1["m"][:]))
                link(v.tensor_tensor(r1["w2"][:], r1["e"][:], r1["w1"][:], ALU.mult))
                link(v.tensor_tensor(rt["pick"][:], rt["first"][:], bc(r1["w1"]), ALU.mult))
                link(v.tensor_tensor(rt["tmp"][:], rt["second"][:], bc(r1["w2"]), ALU.mult))
                link(v.tensor_tensor(rt["wt"][:], rt["pick"][:], rt["tmp"][:], ALU.add))
            else:
                link(v.tensor_tensor(rt["pick"][:], rt["first"][:], rt["second"][:], ALU.add))
                link(v.tensor_tensor(rt["tmp"][:], rt["pick"][:], rt["sig"][:], ALU.mult))
                link(v.tensor_reduce(r1["d"][:], rt["tmp"][:], AX.X, ALU.add))
                link(v.tensor_scalar(r1["m"][:], r1["d"][:], EPS_ROUTE, None, ALU.add))
                link(v.reciprocal(r1["w1"][:], r1["m"][:]))
                link(v.tensor_tensor(rt["wt"][:], rt["tmp"][:], bc(r1["w1"]), ALU.mult))
            gate = tg[:, 2 + layer:3 + layer]
            link(v.tensor_scalar(rt["pick"][:], rt["wt"][:], gate, None, ALU.mult))
            link(v.tensor_copy(sc_h[:], rt["pick"][:]))
            v.tensor_tensor(sc_l[:], rt["pick"][:], sc_h[:].bitcast(F32), ALU.subtract).then_inc(s_route, 1)
            v.wait_ge(s_route, 1 + layer)
            return k[0]

        links_used, rt_b = [0], rt

        def dve_route0(v):
            v.wait_ge(s_small, 16 * len(small))
            v.wait_ge(lg0.lg_copied, NG)
            links_used[0] = dve_route(v, 0, 0, 0, rt_b, r1)
        dve_parts.append(dve_route0)

        def act_route0(a):
            a.wait_ge(s_ract, 1)
            a.activation(r1["e"][:], r1["d"][:], ACT.Exp, bias=zero_col[:, 0:1]).then_inc(s_re, 1)
        act_parts.append(act_route0)


        B = dict(hr=sb("b_hr", [P, 2, HC, GT]), hs=sb("b_hs", [P, 2, HC, GT]),
                 hh=sb("b_hh", [P, 2, HC, GT], F32R), hl=sb("b_hl", [P, 2, HC, GT], F32R),
                 y=sb("b_y", [P, 2, GT]))

        class ExpertPass:

            def __init__(self, name, n, y):
                self.n, self.y = n, y
                self.ss_ready = sem(f"{name}_weights_placed")
                self.ss_chain = sem(f"{name}_weights_chain")
                self.st_ready = sem(f"{name}_weights_transposed")
                self.st_done = sem(f"{name}_weights_copied")
                self.z_ready = sem(f"{name}_hidden_ready")
                self.z_read = sem(f"{name}_hidden_read")
                self.bc_ready = sem(f"{name}_spread_ready")
                self.scaled = sem(f"{name}_hidden_scaled")
                self.hi_done = sem(f"{name}_hidden_high")
                self.lo_done = sem(f"{name}_hidden_low")
                self.used = sem(f"{name}_hidden_used")
                self.y_done = sem(f"{name}_y_copied")
                self.yt_ready = sem(f"{name}_y_transposed")
                self.res = sem(f"{name}_residual_done")

            def first(self, g):
                return g.i is None and g.c == 0

            def before(self, eng, s, g, k, back):
                if g.i is None and self.n * g.c + k - back < 0:
                    return
                eng.wait_ge(s, g.at(self.n, k - back + 1))

            def prev(self, m, t, k, back=1):
                return (m, k - back) if k >= back else (t, self.n + k - back)

            def dve_place(self, v, a):
                p = a.parity
                if not (a.i is None and a.c < 2):
                    v.wait_ge(self.st_ready, a.at(1, -1))
                v.tensor_copy(ss[:, p, :, 0:E], sc_h[:, a.tiles(), :].bitcast(F32))
                v.tensor_copy(ss[:, p, :, 32:32 + E], sc_l[:, a.tiles(), :].bitcast(F32)).then_inc(self.ss_ready, 1)

            def pe_place(self, pe, a, misc):
                pe.wait_ge(self.ss_ready, a.at(1, 1))
                for b in range(TG):
                    ins = pe.transpose(misc[:, b * P:(b + 1) * P], ss[:, a.parity, b, :], ident[:])
                ins.then_inc(self.st_ready, 1)

            def act_place(self, a_, a, misc):
                a_.wait_ge(self.st_ready, a.at(1, 1))
                a_.activation(st[:, a.parity, :], misc, ACT.Copy).then_inc(self.st_done, 1)

            def act_high(self, a_, g, k):
                self.before(a_, self.scaled, g, k, 0)
                self.before(a_, self.used, g, k, 2)
                q = (self.n * g.c + k) % 2
                a_.activation(*self.high(q), ACT.Copy).then_inc(self.hi_done, 1)

            def dve_low(self, v, g, k):
                self.before(v, self.hi_done, g, k, 0)
                q = (self.n * g.c + k) % 2
                o, i0, i1 = self.low(q)
                v.tensor_tensor(o, i0, i1, ALU.subtract).then_inc(self.lo_done, 1)

            def act_y(self, a_, t, ybank):
                a_.wait_ge(self.used, t.at(self.n, self.n))
                a_.activation(self.y[:, t.parity, :], ybank, ACT.Copy).then_inc(self.y_done, 1)

            def pe_y(self, pe, t, misc):
                pe.wait_ge(self.y_done, t.at(1, 1))
                for b in range(TG):
                    ins = pe.transpose(misc[:, b * P:(b + 1) * P], self.y[:, t.parity, b * P:(b + 1) * P], ident[:])
                ins.then_inc(self.yt_ready, 1)

            def dve_residual(self, v, t, misc):
                v.wait_ge(self.yt_ready, t.at(1, 1))
                xt = x_all[:, t.tiles(), :]
                v.tensor_tensor(xt, misc.rearrange("p (b c) -> p b c", b=TG), xt, ALU.add).then_inc(self.res, 1)
                wait_apart(v, self.res, t.at(1, 1))

        Z, SBC, Y, MISC = [bank[0:2], bank[2:4]], [bank[4], bank[5]], bank[6], bank[7]
        xb = ExpertPass("b", E, B["y"])
        Bb = B
        xb.high = lambda q: (Bb["hh"][:, q, :, :], Bb["hs"][:, q, :, :])
        xb.low = lambda q: (Bb["hl"][:, q, :, :], Bb["hs"][:, q, :, :], Bb["hh"][:, q, :, :].bitcast(F32))
        ln2 = LayerNorm("b_ln", MISC, (stats, mv, vpe, rstd, xn))

        def w1s(w, e, c):
            return w[:, (e * HC + c) * P:(e * HC + c + 1) * P]

        def pe_b(pe):
            pe_setup_late(pe)
            pe.wait_ge(s_split, NG)
            pe.wait_ge(ln1.lo_done, NG)

            def up(g, e):
                q = e % 2
                h, l = xh[:, g.cols(1), :], xl[:, g.cols(1), :]
                xb.before(pe, xb.z_read, g, e, 2)
                for c in range(HC):
                    o = Z[q][c].rearrange("p (a c) -> p a c", a=1)
                    ins = product3(pe, o, w1s(w1h, e, c), w1s(w1l, e, c), h, l)
                ins.then_inc(xb.z_ready, 1)
                if e == 0:
                    pe.wait_ge(xb.st_done, g.at(1, 1))
                xb.before(pe, xb.scaled, g, e, 2)
                pe.matmul(SBC[q], sel0[:, e, :], st[:, g.parity, :], start=True, stop=True).then_inc(xb.bc_ready, 1)

            def down(g, e):
                q = e % 2
                if e == 0:
                    if not xb.first(g):
                        pe.wait_ge(xb.y_done, g.at(1, 0))
                    pe.matmul(Y, b2h, st[:, g.parity, :], start=True, stop=False)
                    pe.matmul(Y, b2l, st[:, g.parity, :], start=False, stop=False)
                xb.before(pe, xb.lo_done, g, e, 0)
                for c in range(HC):
                    ins = product3(pe, Y, w1s(w2h, e, c), w1s(w2l, e, c), Bb["hh"][:, q, c, :], Bb["hl"][:, q, c, :],
                                   start=False, stop=(e == E - 1 and c == HC - 1))
                ins.then_inc(xb.used, 1)

            def place(a):
                xb.pe_place(pe, a, MISC)

            def y_back(a, t):
                if a:
                    pe.wait_ge(xb.st_done, a.at(1, 1))
                elif not xb.first(t):
                    pe.wait_ge(ln2.lo_done, t.at(1, 0))
                xb.pe_y(pe, t, MISC)

            def step(a, m, t):
                for e in range(E if m else LAG):
                    if m:
                        up(m, e)
                    g, k = xb.prev(m, t, e, LAG)
                    if g:
                        down(g, k)
                    if m and e == 1 and a:
                        place(a)
                    if m and e == 4 and t:
                        y_back(a, t)
                    if m and e == 7 and t:
                        ln2.pe_transpose(pe, t)
                if not m:
                    if a:
                        place(a)
                    if t:
                        y_back(a, t)
                        ln2.pe_transpose(pe, t)
            pipeline(pe, step)
        pe_parts.append(pe_b)

        def act_b(a_):
            act_setup_late(a_)
            def relu(g, e):
                q = e % 2
                xb.before(a_, xb.z_ready, g, e, 0)
                xb.before(a_, xb.scaled, g, e, 2)
                for c in range(HC):
                    ins = a_.activation(Bb["hr"][:, q, c, :], Z[q][c], ACT.Relu, bias=b1s[:, e, c:c + 1])
                ins.then_inc(xb.z_read, 1)

            def step(a, m, t):
                if m:
                    for e in range(E):
                        if e == LAG and t:
                            xb.act_y(a_, t, Y)
                        relu(m, e)
                        g, k = xb.prev(m, t, e)
                        if g:
                            xb.act_high(a_, g, k)
                        if e == 2 and a:
                            xb.act_place(a_, a, MISC)
                        if e == 7 and t:
                            ln2.act_high(a_, t)
                else:
                    if t:
                        xb.act_high(a_, t, E - 1)
                        xb.act_y(a_, t, Y)
                    if a:
                        xb.act_place(a_, a, MISC)
                    if t:
                        ln2.act_high(a_, t)
            pipeline(a_, step)
        act_parts.append(act_b)

        def dve_b(v):
            dve_setup_late(v)
            v.memset(ss[:], 0.0).then_inc(xb.ss_chain, 1)
            v.wait_ge(xb.ss_chain, 1)

            def scale(g, e):
                q = e % 2
                xb.before(v, xb.z_read, g, e, 0)
                xb.before(v, xb.bc_ready, g, e, 0)
                xb.before(v, xb.lo_done, g, e, 2)
                v.tensor_tensor(Bb["hs"][:, q, :, :], Bb["hr"][:, q, :, :],
                                SBC[q].unsqueeze(1).broadcast_to([P, HC, GT]), ALU.mult).then_inc(xb.scaled, 1)

            def low(g, k):
                xb.before(v, xb.used, g, k, 2)
                xb.dve_low(v, g, k)

            def step(a, m, t):
                if m:
                    for e in range(E):
                        scale(m, e)
                        g, k = xb.prev(m, t, e)
                        if g:
                            low(g, k)
                        if e == 0 and a:
                            xb.dve_place(v, a)
                        if e == 5 and t:
                            xb.dve_residual(v, t, MISC)
                            ln2.dve_stats(v, t)
                        if e == 6 and t:
                            ln2.dve_norm(v, t)
                        if e == 7 and t:
                            ln2.dve_low(v, t)
                else:
                    if a:
                        xb.dve_place(v, a)
                    if t:
                        low(t, E - 1)
                        xb.dve_residual(v, t, MISC)
                        ln2.dve_stats(v, t)
                        ln2.dve_norm(v, t)
                        ln2.dve_low(v, t)
            pipeline(v, step)
        dve_parts.append(dve_b)

        def pool_b(q):
            def step(a, m, t):
                if t:
                    ln2.pool_rstd(q, t)
            pipeline(q, step)
        pool_parts.append(pool_b)

        new_scope()
        NU = 2 * NC4
        NQ = TG * NC4
        NHALF = NQ // 2
        w1_0, w1_1 = WCOL["w1"][0], WCOL["w2"][1]
        qs = w_hi[:, w1_0:w1_1].rearrange("p (a c t) -> p a c t", a=2, c=NC4)
        ks = w_lo[:, w1_0:w1_0 + 2 * NC4 * GK].rearrange("p (a c b k) -> p a c b k", a=2, c=NC4, b=TG)
        kb = sb("c_kb", [P, 2, NC4, HQ, SK], F32R)
        lowpart = sb("c_lowpart", [P, 2, GT], F32R)
        v3 = sb("c_v3", [S2, 2, TG, NH, 3, VW], BF16)
        vf = sb("c_vf", [S2, TG * D])
        vr = sb("c_vr", [S2, TG * D])
        mx1 = sb("c_mx", [P, 2, 2 * HQ])
        sm1 = sb("c_sm", [P, 2, 2 * HQ, S2])
        pf1 = sb("c_pf", [P, 2, 2 * HQ, S2])
        ph = sb("c_ph", [S2, NC4, HQ * P], F16)
        pl_ = sb("c_pl", [S2, NC4, HQ * P], F16)
        pt32 = sb("c_pt32", [S2, 2, HQ * P])
        o10 = sb("c_o10", [P, NH, VW])
        oi = sb("c_oi", [P, NH])
        on = sb("c_on", [P, TG, D])
        ot = sb("c_ot", [P, GT])
        c_ctx = [sem("c_ctx_loaded0"), sem("c_ctx_loaded1")]
        u_ready, u_act, u_read = sem("c_prep_ready"), sem("c_prep_low"), sem("c_prep_read")
        v_ready, v_copied = sem("c_values_ready"), sem("c_values_copied")
        v_split, v_chain = sem("c_values_split"), sem("c_values_chain")
        kb_zero, kb_placed = sem("c_keys_cleared"), [sem("c_keys_placed0"), sem("c_keys_placed1")]
        s1_ready, s1_max, s1_sub, s1_exp = sem("c_scores"), sem("c_max"), sem("c_shifted"), sem("c_exp")
        t1_ready, hi_done, pv_used = sem("c_probs_t"), sem("c_probs_high"), sem("c_pv")
        lo_done = [sem("c_probs_low_even"), sem("c_probs_low_odd")]
        o_read, o_inv, o_done = sem("c_out_summed"), sem("c_out_inverse"), sem("c_out_normed")
        ot_ready, ot_done = sem("c_out_transposed"), sem("c_out_t_copied")
        wo_ready, c_res = sem("c_projected"), sem("c_residual_done")
        M1 = bank[6]
        MU = [bank[5], bank[7]]
        ln3 = LayerNorm("c_ln", M1, (stats, mv, vpe, rstd, xn))
        lg1 = RouterLogits("c_router", ln3, wg1h, wg1l, M1, M1)

        def before(eng, s, n, g, k, back=0, wait=None):
            if g.i is None and n * g.c + k - back < 0:
                return
            if wait:
                wait(eng, s, g.at(n, k - back + 1))
            else:
                eng.wait_ge(s, g.at(n, k - back + 1))

        def lagged(m, t, k):
            return (m, k) if k >= 0 else (t, NQ + k)

        def sp_c(sp):
            def place_keys(g, b):
                for j in range(HQ):
                    r = slice(4 * DH * j, 4 * DH * (j + 1))
                    sp.dma_start(kb[r, b % 2, :, j, :].bitcast(F32),
                                 ks[r, g.parity, :, b, :].bitcast(F32)).then_inc(kb_placed[b % 2], 16)

            def step(a, m, t):
                if m:
                    for b in range(1, TG):
                        before(sp, s1_ready, NHALF, m, 2 * b + 1, 4)
                        place_keys(m, b)
                if a:
                    if m:
                        before(sp, s1_sub, NHALF, m, 5)
                    else:
                        before(sp, u_read, NU, a, NU - 1)
                    place_keys(a, 0)
            sp.wait_ge(kb_zero, 2)
            pipeline(sp, step)
        sp_parts.append(sp_c)

        def pe_c(pe):
            def prepare(a, u):
                p = a.parity
                o = MU[u % 2]
                if u == 0:
                    before(pe, v_copied, 1, a, 0, 1)
                before(pe, u_read, NU, a, u, 2)
                if u < NC4:
                    w = slice(u * P, (u + 1) * P)
                    ins = product3(pe, o.rearrange("p (a c) -> p a c", a=1), wqh[:, w], wql[:, w],
                                   xh[:, a.cols(1), :], xl[:, a.cols(1), :])
                else:
                    if u == NC4:
                        pe.wait_ge(c_ctx[p], a.pair(16, 16))
                    c = u - NC4
                    ins = pe.matmul(o[:, 0:GK], wk1[:, c * P:(c + 1) * P], ctxg[:, p, :], start=True, stop=True)
                ins.then_inc(u_ready, 1)

            def prepare_values(a):
                before(pe, u_read, NU, a, NU - 2)
                for b in range(TG):
                    ins = pe.matmul(MU[0][0:S2, b * D:(b + 1) * D], ctxg[:, a.parity, b * SK:b * SK + S2], wv1[:],
                                    start=True, stop=True)
                ins.then_inc(v_ready, 1)

            def scores(m, h):
                b = h // 2
                before(pe, s1_sub, NHALF, m, h, 1)
                if h == 0:
                    pe.wait_ge(u_read, m.at(NU, NU))
                if h % 2 == 0:
                    pe.wait_ge(kb_placed[b % 2], m.at(16 * HQ * TG // 2, 16 * HQ * (b // 2 + 1)))
                for k in range(2):
                    c = (h % 2) * 2 + k
                    o = bank[k][:, 0:GK]
                    pe.matmul(o, ident_bf[:], mask_bf[:].unsqueeze(1).broadcast_to([P, HQ, SK]), start=True, stop=False)
                    ins = pe.matmul(o, qs[:, m.parity, c, b * P:(b + 1) * P],
                                    kb[:, b % 2, c, :, :].rearrange("p j k -> p (j k)"), start=False, stop=True)
                ins.then_inc(s1_ready, 1)

            def transpose(g, q):
                h = q // 2
                before(pe, s1_exp, NHALF, g, h)
                if q % 2 == 0:
                    before(pe, hi_done, NQ, g, q, 2)
                else:
                    before(pe, lo_done[1], NHALF, g, q // 2, 1)
                for j in range(HQ):
                    ins = pe.transpose(bank[2 + q % 2][0:S2, j * P:(j + 1) * P],
                                       pf1[:, h % 2, (q % 2) * HQ + j, :], ident[:])
                ins.then_inc(t1_ready, 1)

            def values(g, q):
                b, c = q // NC4, q % NC4
                before(pe, lo_done[q % 2], NHALF, g, q // 2)
                if c == 0:
                    before(pe, o_read, TG, g, b, 1)
                    if b == 0:
                        pe.wait_ge(v_split, g.at(1, 1))
                for j in range(HQ):
                    h = c * HQ + j
                    o = bank[4][:, h * 3 * VW:(h + 1) * 3 * VW]
                    vv = v3[:, g.parity, b, h, :, :].rearrange("p s d -> p (s d)")
                    pe.matmul(o, ph[:, q % NC4, j * P:(j + 1) * P], vv, start=True, stop=False)
                    ins = pe.matmul(o, pl_[:, q % NC4, j * P:(j + 1) * P], vv, start=False, stop=True)
                ins.then_inc(pv_used, 1)

            def turn_out(t):
                pe.wait_ge(o_done, t.at(TG, TG))
                for b in range(TG):
                    ins = pe.transpose(M1[:, b * P:(b + 1) * P], on[:, b, :], ident[:])
                ins.then_inc(ot_ready, 1)

            def project(t):
                pe.wait_ge(ot_done, t.at(1, 1))
                for b in range(TG):
                    o = M1[:, b * P:(b + 1) * P]
                    pe.matmul(o, ones_row[:], bo_all[:], start=True, stop=False)
                    ins = pe.matmul(o, ot[:, b * P:(b + 1) * P], wo1[:], start=False, stop=True)
                ins.then_inc(wo_ready, 1)

            def step(a, m, t):
                for i in range(NQ):
                    g, q = lagged(m, t, i - 6)
                    if g:
                        values(g, q)
                    if t and i == 6:
                        turn_out(t)
                    if m and i % 2 == 1 and i < NQ - 1:
                        scores(m, (i + 1) // 2)
                    if a and i == NQ - 1:
                        scores(a, 0)
                    g, q = lagged(m, t, i - 3)
                    if g:
                        transpose(g, q)
                    if t and i == 6:
                        project(t)
                    if a and i < NU:
                        prepare(a, i)
                    if a and i == NU:
                        prepare_values(a)
                    if t and i == 11:
                        ln3.pe_transpose(pe, t)
                    if t and i == 13:
                        lg1.pe_product(pe, t)
                    if t and i == 14:
                        lg1.pe_transpose(pe, t)
            pe.wait_ge(ln2.lo_done, NG)
            pipeline(pe, step)
        pe_parts.append(pe_c)

        def act_c(a_):
            def load_context(a):
                if a.i is None and a.c < 2:
                    a_.wait_ge(a_v_ready, NG)
                before(a_, v_ready, 1, a, 0, 2)
                a_.dma_start(ctxg[:, a.parity, :], ctxT[:, a.cols(GK)]).then_inc(c_ctx[a.parity], 16)

            def prepare(a, u):
                k, c, w = (0, u, GT) if u < NC4 else (1, u - NC4, GK)
                before(a_, u_ready, NU, a, u)
                blo = (bqlo, bklo)[k]
                a_.activation(lowpart[:, u % 2, 0:w], MU[u % 2][:, 0:w], ACT.Identity, bias=blo[:, c:c + 1],
                              scale=part[:, k:k + 1]).then_inc(u_act, 1)

            def prepare_values(a):
                before(a_, v_ready, 1, a, 0)
                before(a_, v_split, 1, a, 0, 1)
                a_.activation(vf[:], MU[0][0:S2, :], ACT.Copy).then_inc(v_copied, 1)

            def high(g, q):
                before(a_, t1_ready, NQ, g, q)
                before(a_, pv_used, NQ, g, q, NC4)
                if q % 2 == 0:
                    before(a_, lo_done[0], NHALF, g, q // 2, 2)
                    a_.activation(pt32[:, q // 2 % 2, :], bank[2][0:S2, :], ACT.Copy)
                a_.activation(ph[:, q % NC4, :], bank[2 + q % 2][0:S2, :], ACT.Copy).then_inc(hi_done, 1)

            def exp(m, h):
                before(a_, s1_sub, NHALF, m, h)
                before(a_, t1_ready, NQ, m, 2 * h + 1, 4)
                a_.activation(pf1[:, h % 2, :, :], sm1[:, h % 2, :, :], ACT.Exp, bias=bias_hr[:, 0:1],
                              scale=exp_scale[:, 0:1]).then_inc(s1_exp, 1)

            def step(a, m, t):
                if a:
                    load_context(a)
                for i in range(NQ):
                    if m and i % 2 == 1:
                        exp(m, i // 2)
                    if t and i == 6:
                        a_.wait_ge(ot_ready, t.at(1, 1))
                        a_.activation(ot[:], M1, ACT.Copy).then_inc(ot_done, 1)
                    g, q = lagged(m, t, i - 3)
                    if g:
                        high(g, q)
                    if a and i < NU:
                        prepare(a, i)
                    if a and i == NU:
                        prepare_values(a)
                    if t and i == 11:
                        ln3.act_high(a_, t)
                    if t and i == 13:
                        lg1.act_copy(a_, t)
            pipeline(a_, step)
        act_parts.append(act_c)

        def dve_c(v):
            def prepare(a, u):
                p, o = a.parity, MU[u % 2]
                lp = lowpart[:, u % 2, :].bitcast(F32)
                before(v, u_act, NU, a, u)
                if u < NC4:
                    v.scalar_tensor_tensor(out=qs[:, p, u, :], in0=o, scalar=bq1[:, u:u + 1], in1=lp,
                                           op0=ALU.add, op1=ALU.subtract).then_inc(u_read, 1)
                else:
                    c = u - NC4
                    v.scalar_tensor_tensor(out=ks[:, p, c, :, :].rearrange("p b k -> p (b k)"), in0=o[:, 0:GK],
                                           scalar=bk1[:, c:c + 1], in1=lp[:, 0:GK],
                                           op0=ALU.add, op1=ALU.subtract).then_inc(u_read, 1)

            def shift(m, h):
                before(v, s1_ready, NHALF, m, h)
                before(v, s1_exp, NHALF, m, h, 2)
                s = psum[:, 0:2, 0:GK].rearrange("p k (j s) -> p k j s", j=HQ)[:, :, :, 0:S2]
                mm = mx1[:, h % 2, :].rearrange("p (k j) -> p k j", k=2)
                v.tensor_reduce(mm, s, AX.X, ALU.max).then_inc(s1_max, 1)
                before(v, s1_max, NHALF, m, h)
                v.tensor_tensor(sm1[:, h % 2, :, :].rearrange("p (k j) s -> p k j s", k=2), s,
                                mm.unsqueeze(3).broadcast_to([P, 2, HQ, S2]), ALU.subtract).then_inc(s1_sub, 1)

            def low(g, q):
                before(v, hi_done, NQ, g, q)
                before(v, pv_used, NQ, g, q, NC4)
                v.tensor_tensor(pl_[:, q % NC4, :], bank[2 + q % 2][0:S2, :], ph[:, q % NC4, :],
                                ALU.subtract).then_inc(lo_done[1], 1)

            def combine(g, b):
                before(v, pv_used, NQ, g, NC4 * b + NC4 - 1)
                v.tensor_reduce(o10[:], bank[4][:, 0:NH * 3 * VW].rearrange("p (h s d) -> p h d s", h=NH, s=3),
                                AX.X, ALU.add).then_inc(o_read, 1)
                before(v, o_read, TG, g, b)
                v.reciprocal(oi[:], o10[:, :, DH]).then_inc(o_inv, 1)
                before(v, o_inv, TG, g, b)
                v.tensor_tensor(on[:, b, :].rearrange("p (h d) -> p h d", h=NH), o10[:, :, 0:DH],
                                oi[:].unsqueeze(2).broadcast_to([P, NH, DH]), ALU.mult).then_inc(o_done, 1)

            def residual(t):
                v.wait_ge(wo_ready, t.at(1, 1))
                xt = x_all[:, t.tiles(), :].rearrange("p b d -> p (b d)")
                v.scalar_tensor_tensor(out=xt, in0=M1, scalar=tg[:, 1:2], in1=xt,
                                       op0=ALU.mult, op1=ALU.add).then_inc(c_res, 1)
                wait_apart(v, c_res, t.at(1, 1))

            def step(a, m, t):
                for i in range(NQ):
                    g, q = lagged(m, t, i - 4)
                    if g and q % 2 == 1:
                        low(g, q)
                    g, q = lagged(m, t, i - 9)
                    if g and q % NC4 == 0:
                        combine(g, q // NC4)
                    if m and i % 2 == 0:
                        shift(m, i // 2)
                    if a and 0 <= i - 1 < NU:
                        prepare(a, i - 1)
                    if t and i == 7:
                        residual(t)
                        ln3.dve_stats(v, t)
                    if t and i == 12:
                        ln3.dve_low(v, t)
                    if t and i == 15:
                        lg1.dve_copy(v, t)
            pipeline(v, step)
        dve_parts.append(dve_c)

        def pool_c(q_):
            q_.wait_ge(ln2.lo_done, NG)
            q_.memset(kb[:].bitcast(F32), 0.0).then_inc(kb_zero, 1)
            q_.memset(v3[:], 0.0).then_inc(kb_zero, 1)
            q_.wait_ge(kb_zero, 2)
            q_.memset(v3[:, :, :, :, 0, DH:DH + 1], 1.0).then_inc(kb_zero, 1)
            q_.wait_ge(kb_zero, 3)

            def heads(t):
                return t[:].rearrange("p (b h d) -> p b h d", b=TG, h=NH)

            def split_values(a, part):
                def to(s):
                    return v3[:, a.parity, :, :, s, 0:DH]
                if part == 0:
                    before(q_, v_copied, 1, a, 0)
                    before(q_, pv_used, NQ, a, NQ - 1, 2 * NQ, wait_apart)
                else:
                    wait_apart(q_, v_chain, a.at(4, part))
                ins = (lambda: q_.tensor_copy(to(0), heads(vf)),
                       lambda: q_.tensor_tensor(heads(vr), heads(vf), to(0), ALU.subtract),
                       lambda: q_.tensor_copy(to(1), heads(vr)),
                       lambda: q_.tensor_tensor(heads(vf), heads(vr), to(1), ALU.subtract),
                       lambda: q_.tensor_copy(to(2), heads(vf)))[part]()
                ins.then_inc(v_chain if part < 4 else v_split, 1)

            def low(g, q):
                before(q_, pv_used, NQ, g, q, NC4)
                before(q_, hi_done, NQ, g, q)
                q_.tensor_tensor(pl_[:, q % NC4, :], pt32[:, q // 2 % 2, :], ph[:, q % NC4, :],
                                 ALU.subtract).then_inc(lo_done[0], 1)

            def step(a, m, t):
                for i in range(NQ):
                    g, q = lagged(m, t, i - 4)
                    if g and q % 2 == 0:
                        low(g, q)
                    if t and i == 7:
                        ln3.pool_rstd(q_, t)
                    if t and i == 8:
                        ln3.pool_norm(q_, t)
                    if a and i in (9, 11, 13, 15):
                        split_values(a, (i - 9) // 2)
                    if m and i == 1:
                        split_values(m, 4)
            pipeline(q_, step)
        pool_parts.append(pool_c)


        new_scope()
        rt = {n: sb(f"r1_{n}_all", [P, NB, E]) for n in ("val", "pick", "tmp", "first", "second", "sig", "wt")}
        B = dict(hr=sb("d_hr", [P, 2, HC, GT]), hs=sb("d_hs", [P, 2, 1, GT]),
                 hh=sb("d_hh", [P, 2, 1, GT], F32R), hl=sb("d_hl", [P, 2, 1, GT], F32R),
                 y=sb("d_y", [P, 2, GT]))
        xd = ExpertPass("d", FC, B["y"])
        sg = B["hr"]
        d_silu, d_mul = sem("d_silu_done"), sem("d_product_done")
        xd.high = lambda q: (B["hh"][:, q, 0, :], B["hs"][:, q, 0, :])
        xd.low = lambda q: (B["hl"][:, q, 0, :], B["hs"][:, q, 0, :], B["hh"][:, q, 0, :].bitcast(F32))

        def act_route1(a):
            a.wait_ge(lg1.lg_copied, NG)
            a.activation(rt["wt"][:], logits[:], ACT.Exp, bias=zero_col[:, 0:1], scale=-1.0).then_inc(s_re, 1)
        act_parts.append(act_route1)

        def dve_route1(v):
            dve_route(v, 1, links_used[0], 1, rt, r1)
        dve_parts.append(dve_route1)

        def gus(w, k, c):
            return w[:, (k * FC + c) * P:(k * FC + c + 1) * P]

        def pe_d(pe):
            pe.wait_ge(ln3.lo_done, NG)

            def up(g, e):
                q = (FC * g.c + e) % 2
                h, l = xh[:, g.cols(1), :], xl[:, g.cols(1), :]
                xd.before(pe, d_mul, g, e, 2)
                for k in range(2):
                    o = Z[q][k].rearrange("p (a c) -> p a c", a=1)
                    ins = product3(pe, o, gus(wguh, k, e), gus(wgul, k, e), h, l)
                ins.then_inc(xd.z_ready, 1)
                if e == 0:
                    pe.wait_ge(xd.st_done, g.at(1, 1))
                xd.before(pe, xd.scaled, g, e, 2)
                pe.matmul(SBC[q], sel1[:, e, :], st[:, g.parity, :], start=True, stop=True).then_inc(xd.bc_ready, 1)

            def down(g, e):
                q = (FC * g.c + e) % 2
                if e == 0 and not xd.first(g):
                    pe.wait_ge(xd.y_done, g.at(1, 0))
                xd.before(pe, xd.lo_done, g, e, 0)
                product3(pe, Y, wdh[:, e * P:(e + 1) * P], wdl[:, e * P:(e + 1) * P], B["hh"][:, q, 0, :],
                         B["hl"][:, q, 0, :], start=(e == 0), stop=(e == FC - 1)).then_inc(xd.used, 1)

            def place(a):
                xd.pe_place(pe, a, MISC)

            def y_back(a, t):
                if a:
                    pe.wait_ge(xd.st_done, a.at(1, 1))
                elif not xd.first(t):
                    pe.wait_ge(xd.res, t.at(1, 0))
                xd.pe_y(pe, t, MISC)

            def step(a, m, t):
                for e in range(FC if m else LAG):
                    if m:
                        up(m, e)
                    g, k = xd.prev(m, t, e, LAG)
                    if g:
                        down(g, k)
                    if m and e == 1 and a:
                        place(a)
                    if m and e == 5 and t:
                        y_back(a, t)
                if not m:
                    if a:
                        place(a)
                    if t:
                        y_back(a, t)
            pipeline(pe, step)
        pe_parts.append(pe_d)

        def act_d(a_):
            def silu(g, e):
                q = (FC * g.c + e) % 2
                xd.before(a_, xd.z_ready, g, e, 0)
                xd.before(a_, d_mul, g, e, 2)
                a_.activation(sg[:, q, 0, :], Z[q][0], ACT.Silu).then_inc(d_silu, 1)

            def step(a, m, t):
                if m:
                    for e in range(FC):
                        if e == LAG and t:
                            xd.act_y(a_, t, Y)
                        silu(m, e)
                        g, k = xd.prev(m, t, e)
                        if g:
                            xd.act_high(a_, g, k)
                        if e == 2 and a:
                            xd.act_place(a_, a, MISC)
                else:
                    if t:
                        xd.act_high(a_, t, FC - 1)
                        xd.act_y(a_, t, Y)
                    if a:
                        xd.act_place(a_, a, MISC)
            pipeline(a_, step)
        act_parts.append(act_d)

        def dve_d(v):
            v.tensor_copy(sg_gate_h[:], tg[:, 3:4]).then_inc(xd.ss_chain, 1)
            v.wait_ge(xd.ss_chain, 1)
            v.tensor_tensor(sg_gate_l[:], tg[:, 3:4], sg_gate_h[:].bitcast(F32), ALU.subtract).then_inc(xd.ss_chain, 1)
            v.wait_ge(xd.ss_chain, 2)
            v.tensor_copy(ss[:, :, :, E:E + 1].rearrange("p a b c -> p (a b) c"),
                          sg_gate_h[:].bitcast(F32).unsqueeze(1).broadcast_to([P, 2 * TG, 1]))
            v.tensor_copy(ss[:, :, :, 32 + E:33 + E].rearrange("p a b c -> p (a b) c"),
                          sg_gate_l[:].bitcast(F32).unsqueeze(1).broadcast_to([P, 2 * TG, 1]))

            def mul(g, e):
                q = (FC * g.c + e) % 2
                xd.before(v, d_silu, g, e, 0)
                v.tensor_tensor(sg[:, q, 1, :], sg[:, q, 0, :], Z[q][1], ALU.mult).then_inc(d_mul, 1)

            def scale(g, e):
                q = (FC * g.c + e) % 2
                xd.before(v, d_mul, g, e, 0)
                xd.before(v, xd.bc_ready, g, e, 0)
                xd.before(v, xd.lo_done, g, e, 2)
                v.tensor_tensor(B["hs"][:, q, 0, :], sg[:, q, 1, :], SBC[q], ALU.mult).then_inc(xd.scaled, 1)

            def low(g, k):
                xd.before(v, xd.used, g, k, 2)
                xd.dve_low(v, g, k)

            def step(a, m, t):
                if m:
                    for e in range(FC):
                        mul(m, e)
                        g, k = xd.prev(m, t, e)
                        if g:
                            low(g, k)
                        scale(m, e)
                        if e == 0 and a:
                            xd.dve_place(v, a)
                        if e == 6 and t:
                            xd.dve_residual(v, t, MISC)
                else:
                    if a:
                        xd.dve_place(v, a)
                    if t:
                        low(t, FC - 1)
                        xd.dve_residual(v, t, MISC)
            pipeline(v, step)
        dve_parts.append(dve_d)

        def sp_d(sp):
            ov = out.rearrange("b p d -> p b d")
            with sp.Fori(0, NG // 2) as i:
                for c in range(2):
                    g = Group(i, c)
                    sp.wait_ge(xd.res, g.at(1, 1))
                    sp.dma_start(ov[:, g.tiles(), :], x_all[:, g.tiles(), :]).then_inc(s_out[c], 16)
            for c in range(2):
                sp.wait_ge(s_out[c], 16 * (NG // 2))
        sp_parts.append(sp_d)

        scope[0].close()

        @block.sync
        def _(sp):
            for f in sp_parts:
                f(sp)

        @block.gpsimd
        def _(q):
            for f in pool_parts:
                f(q)

        @block.scalar
        def _(a):
            for f in act_parts:
                f(a)

        @block.vector
        def _(v):
            for f in dve_parts:
                f(v)

        @block.tensor
        def _(pe):
            for f in pe_parts:
                f(pe)


_OUT_SHAPE = (NB, P, D)


def kernel(**inputs):
    import numpy as np
    import concourse.bacc as bacc
    from concourse.bass_utils import run_bass_kernel_spmd

    a = {k: np.asarray(v) for k, v in inputs.items()}
    z = lambda *shape: np.zeros(shape, np.float32)

    ctxT = z(D, NB, SK)
    ctxT[:, :, :S2] = a["ctx_1024"].transpose(2, 0, 1)
    gates = np.broadcast_to(np.concatenate([a["g_xattn"], a["g_ffn"]])[None, :], (P, 4))

    def stack(w):
        o = np.zeros(w.shape[:-1] + (NC4, HQ, 4, DH), np.float32)
        o[..., 0:3, :] = w.reshape(w.shape[:-1] + (NC4, HQ, 1, DH))
        return o.reshape(w.shape[:-1] + (NC4 * P,))

    def columns(v):
        return stack(v).reshape(NC4, P).T

    def side_by_side(w):
        n = -(-w.shape[0] // P)
        o = z(n * P, w.shape[1])
        o[:w.shape[0]] = w
        return o.reshape(n, P, w.shape[1]).transpose(1, 0, 2).reshape(P, -1)

    def router(w):
        o = z(D, P)
        o[:, :E] = w
        return o

    def hidden(experts, shared):
        o = z(D, FC * P)
        o[:, :E * F1] = experts.transpose(1, 0, 2).reshape(D, E * F1)
        o[:, E * F1:(E + 1) * F1] = shared
        return o

    b2 = z(P, D)
    b2[0:E] = a["L0_ffn_b2"]
    b2[32:32 + E] = a["L0_ffn_b2"]
    part = {
        "wg0": router(a["L0_ffn_Wg"]), "b2": b2,
        "w1": a["L0_ffn_W1"].transpose(1, 0, 2).reshape(D, -1),
        "w2": side_by_side(a["L0_ffn_W2"].reshape(-1, D)),
        "wq": stack(a["L1_xattn_wq"].T), "wg1": router(a["L1_ffn_W_gate_router"]),
        "wgu": np.concatenate([hidden(a["L1_ffn_Wg"], a["L1_ffn_Wg_s"]),
                               hidden(a["L1_ffn_Wu"], a["L1_ffn_Wu_s"])], 1),
        "wd": side_by_side(np.concatenate([a["L1_ffn_Wd"].reshape(-1, D), a["L1_ffn_Wd_s"]])),
    }
    sel0, sel1 = z(P, E, P), z(P, FC, P)
    for e in range(E):
        sel0[[e, 32 + e], e, :] = 1.0
    for r in range(FC * P):
        e = r // F1
        if e <= E:
            sel1[[e, 32 + e], r // P, r % P] = 1.0
    part["sel0"], part["sel1"] = sel0.reshape(P, -1), sel1.reshape(P, -1)
    lows = z(P, 2)
    rows = np.arange(P) % (4 * DH) // DH
    lows[rows == 2, 0] = 1.0
    lows[rows == 1, 1] = 1.0
    rank = np.broadcast_to(np.arange(E, 0, -1).astype(np.float32)[None, :], (P, E))

    arrays = dict(
        x=a["x"], ctxT=ctxT.reshape(D, -1), mask=a["mask_SxS2_bk1"], gates=gates, ident_in=np.eye(P, dtype=np.float32),
        part_in=lows, rank_in=rank, weights=np.concatenate([part[n] for n in WIDTH], 1),
        wq0=a["L0_xattn_w_q"], wk0=a["L0_xattn_w_k"], wv0T=a["L0_xattn_w_v"].T,
        b1=a["L0_ffn_b1"].reshape(E, HC, P).transpose(2, 0, 1),
        bqs=columns(a["L1_xattn_bq"]), wks=stack(a["L1_xattn_wk"].T), bks=columns(a["L1_xattn_bk"]),
        wvT=a["L1_xattn_wv"].T, bv=a["L1_xattn_bv"][:, None],
        woT=a["L1_xattn_wo"].T, bo=a["L1_xattn_bo"][None, :],
        ebias=np.broadcast_to(a["L1_ffn_expert_bias"][None, :], (P, E)))

    nc = bacc.Bacc("TRN2", target_bir_lowering=False, num_devices=1)
    maps, args = {}, {}
    for name, v in arrays.items():
        v = np.ascontiguousarray(v)
        maps[f"in_{name}"] = v
        args[name] = nc.dram_tensor(f"in_{name}", v.shape, mybir.dt.from_np(v.dtype), kind="ExternalInput").ap()
    args["out"] = nc.dram_tensor("out_dram", _OUT_SHAPE, F32, kind="ExternalOutput").ap()
    flamingo_kernel(nc, **args)
    r = run_bass_kernel_spmd(nc, [maps], core_ids=[0])
    return r.results[0]["out_dram"]
```

```python
from contextlib import ExitStack

import concourse.bass as bass
from concourse import mybir

F32 = mybir.dt.float32
F32R = mybir.dt.float32r
BF16 = mybir.dt.bfloat16
F16 = mybir.dt.float16
U8 = mybir.dt.uint8
ALU = mybir.AluOpType
ACT = mybir.ActivationFunctionType
AX = mybir.AxisListType

P = 128
D = 128
NB = 32
TG = 4
NG = NB // TG
GT = TG * P
S2 = 77
SK = 78
GK = TG * SK
E = 8
HC = 2
F1 = 96
FC = 7
NH = 16
DH = 8
HQ = 4
NC4 = NH // HQ
LAG = 3
VW = 10
EPS = 1e-5
EPS_ROUTE = 1e-20
MASK_FILL = -998244352.0
TAKEN = -3.0e38
HALF_RANGE = 10.397207708399179


class Group:

    def __init__(self, i, c):
        self.i, self.c, self.parity = i, c, c % 2

    def at(self, n, k):
        return n * self.c + k if self.i is None else self.i * (2 * n) + (n * self.c + k)

    def pair(self, n, k):
        return n * (self.c // 2) + k if self.i is None else self.i * n + (n * (self.c // 2) + k)

    def tiles(self):
        return bass.ds(self.at(TG, 0), TG)

    def tile(self, t):
        return bass.ds(self.at(TG, t), 1)

    def cols(self, n):
        return bass.ds(self.at(n, 0), n)


def pipeline(eng, step, after_first=None):
    step(Group(None, 0), None, None)
    if after_first:
        after_first()
    step(Group(None, 1), Group(None, 0), None)
    with eng.Fori(0, (NG - 2) // 2) as i:
        step(Group(i, 2), Group(i, 1), Group(i, 0))
        step(Group(i, 3), Group(i, 2), Group(i, 1))
    step(None, Group(None, NG - 1), Group(None, NG - 2))
    step(None, None, Group(None, NG - 1))


class Link:

    def __init__(self, eng, sem, g, n):
        self.eng, self.sem, self.g, self.n, self.k = eng, sem, g, n, 0

    def __call__(self, ins, wait=None):
        self.k += 1
        assert self.k <= self.n, "more links than n"
        ins.then_inc(self.sem, 1)
        if wait:
            wait(self.eng, self.sem, self.g.at(self.n, self.k))
        else:
            self.eng.wait_ge(self.sem, self.g.at(self.n, self.k))

    def end(self):
        assert self.k == self.n, (self.k, self.n)


WIDTH = dict(wg0=P, b2=P, sel0=E * P, w1=E * HC * P, w2=E * HC * P, wq=NC4 * P, wg1=P, sel1=FC * P,
             wgu=2 * FC * P, wd=FC * P)
WCOL, NW = {}, 0
for _name, _w in WIDTH.items():
    WCOL[_name] = (NW, NW + _w)
    NW += _w
WPIECE = NW // NG
assert WPIECE * NG == NW and WCOL["wg0"][1] <= WPIECE


def flamingo_kernel(nc, x, ctxT, mask, gates, ident_in, part_in, rank_in, weights, wq0, wk0, wv0T,
                    b1, bqs, wks, bks, wvT, bv, woT, bo, ebias, out):
    ctx = ExitStack()

    scope = [ctx]

    def sb(name, shape, dt=F32):
        return scope[0].enter_context(nc.sbuf_tensor(name, shape, dt))

    def new_scope():
        if scope[0] is not ctx:
            scope[0].close()
        scope[0] = ExitStack()

    def sem(name):
        return ctx.enter_context(nc.semaphore(name))

    with ctx:
        psum = ctx.enter_context(nc.psum_tensor("psum", [P, 8, 512], F32))
        bank = [psum[:, i, :] for i in range(8)]

        x_all = sb("x_all", [P, NB, D])
        xh = sb("xh", [P, NG, GT], F32R)
        xl = sb("xl", [P, NG, GT], F32R)
        logits = sb("logits", [P, NB, E])
        sc_h = sb("sc_h", [P, NB, E], F32R)
        sc_l = sb("sc_l", [P, NB, E], F32R)
        ident = sb("ident", [P, P])
        ident_bf = sb("ident_bf", [P, P], BF16)
        part = sb("part", [P, 2])
        bqlo = sb("bqlo", [P, NC4])
        bklo = sb("bklo", [P, NC4])
        rank = sb("rank", [P, E])
        gate_in = sb("gate_in", [P, 4])
        tg = sb("tg", [P, 4])
        bias_hr = sb("bias_hr", [P, 1])
        zero_col = sb("zero_col", [P, 1])
        half_neg = sb("half_neg", [P, TG])
        w_wq0 = sb("w_wq0", [P, P])
        w_wk0 = sb("w_wk0", [P, P])
        w_m0 = sb("w_m0", [P, P])
        w_wv0 = sb("w_wv0", [P, P])
        b1s = sb("b1s", [P, E, HC])
        w_hi, w_lo = sb("w_hi", [P, NW], F32R), sb("w_lo", [P, NW], F32R)

        def wpart(name):
            c0, c1 = WCOL[name]
            return w_hi[:, c0:c1], w_lo[:, c0:c1]

        (wg0h, wg0l), (wg1h, wg1l) = wpart("wg0"), wpart("wg1")
        (w1h, w1l), (w2h, w2l), (wqh, wql) = wpart("w1"), wpart("w2"), wpart("wq")
        (wguh, wgul), (wdh, wdl), (b2h, b2l) = wpart("wgu"), wpart("wd"), wpart("b2")
        sel0 = wpart("sel0")[0].rearrange("p (e c) -> p e c", e=E)
        sel1 = wpart("sel1")[0].rearrange("p (e c) -> p e c", e=FC)
        wk1 = sb("wk1", [P, NC4 * P])
        bq1 = sb("bq1", [P, NC4])
        bk1 = sb("bk1", [P, NC4])
        wv1 = sb("wv1", [P, P])
        bv1 = sb("bv1", [P, 1])
        wo1 = sb("wo1", [P, P])
        bo1 = sb("bo1", [1, P])
        bo_all = sb("bo_all", [1, P])
        ones_row = sb("ones_row", [1, P])
        eb1 = sb("eb1", [P, E])
        mask_u8 = sb("mask_u8", [P, S2], U8)
        mask_f = sb("mask_f", [P, SK])
        mask_bf = sb("mask_bf", [P, SK], BF16)
        some_key = sb("some_key", [P, 1])
        exp_scale = sb("exp_scale", [P, 1])

        ctxg = sb("ctxg", [P, 2, GK])
        stats = sb("stats", [P, 2, TG, 6])
        mv = sb("mv", [P, 2, TG, 2])
        vpe = sb("vpe", [P, 2, TG])
        rstd = sb("rstd", [P, 2, TG])
        xn = sb("xn", [P, 2, TG, D])
        lt_s = sb("lt_s", [P, 2, GT])
        ss = sb("ss", [P, 2, TG, P])
        st = sb("st", [P, 2, GT], F32R)
        sg_gate_h, sg_gate_l = sb("sg_gate_h", [P, 1], F32R), sb("sg_gate_l", [P, 1], F32R)
        ROUTE_BUFS = ("val", "pick", "tmp", "first", "second", "sig", "wt")
        rt_tail = {n: sb(f"route_{n}", [P, TG, E]) for n in ROUTE_BUFS}
        r1 = {n: sb(f"r1_{n}", [P, NB]) for n in ("m", "m2", "c", "d", "e", "w1", "w2")}
        s_x = [sem(f"x_loaded{i}") for i in range(2)]
        s_first = sem("first_weights_loaded")
        s_small = sem("small_weights_loaded")
        s_dma = [sem("weights_staged0"), sem("weights_staged1")]
        s_split_hi = sem("weights_high_done")
        s_pool = sem("pool_chain")
        s_split = sem("weights_split")
        s_dvec = sem("dve_setup_chain")
        s_dve_setup = sem("dve_setup_done")
        s_biases = sem("low_biases_done")
        s_tanh = sem("tanh_done")
        s_m0 = sem("m0_product")
        s_m0e = sem("m0_copied")
        s_out = [sem("out_stored0"), sem("out_stored1")]
        s_route = sem("routing_done")
        s_rchain = sem("routing_chain")
        s_re = sem("routing_exp")
        s_ract = sem("routing_act")

        first = [
            (w_wq0[:], wq0), (w_wk0[:], wk0), (w_wv0[:], wv0T), (gate_in[:], gates), (ident[:], ident_in),
        ]
        small = [
            (part[:], part_in), (rank[:], rank_in), (b1s[:], b1),
            (wk1[:], wks), (bq1[:], bqs), (bk1[:], bks), (wv1[:], wvT), (bv1[:], bv), (wo1[:], woT),
            (bo1[:], bo), (eb1[:], ebias), (mask_u8[:], mask),
        ]
        block = ctx.enter_context(nc.Block())

        sp_parts, act_parts, dve_parts, pe_parts, pool_parts = [], [], [], [], []

        spare_v, spare_q = sb("spare_v", [1, 1]), sb("spare_q", [1, 1])

        def wait_apart(eng, s, value):
            eng.wait_ge(s, value)
            if isinstance(value, int):
                return
            if isinstance(eng, bass.BassVectorEngine):
                eng.memset(spare_v[:], 0.0)
            else:
                eng.tensor_tensor(spare_q[:], half_neg[0:1, 0:1], half_neg[0:1, 0:1], ALU.add)

        class LayerNorm:

            def __init__(self, name, t_bank, bufs, to_split=True, dst=None):
                self.bank, self.bufs, self.split, self.dst = t_bank, bufs, to_split, dst
                self.stats_ready = sem(f"{name}_stats_ready")
                self.rstd_ready = sem(f"{name}_rstd_ready")
                self.xn_ready = sem(f"{name}_xn_ready")
                self.t_ready = sem(f"{name}_transposed")
                self.hi_done = sem(f"{name}_high_done")
                self.lo_done = sem(f"{name}_low_done")
                self.chain = sem(f"{name}_dve_chain")
                self.pchain = sem(f"{name}_pool_chain")
                self.centred = sem(f"{name}_centred")

            def dve_stats(self, v, g):
                st, m, _, _, _ = self.bufs
                p = g.parity
                link = Link(v, self.chain, g, 1)
                for t in range(TG):
                    ins = v.bn_stats(st[:, p, t, :], x_all[:, g.tile(t), :])
                link(ins, wait_apart)
                for t in range(TG):
                    ins = v.bn_aggr(m[:, p, t, :], st[:, p, t, :])
                ins.then_inc(self.stats_ready, 1)

            def pool_rstd(self, q, g):
                _, m, ve, rs, _ = self.bufs
                p = g.parity
                wait_apart(q, self.stats_ready, g.at(1, 1))
                link = Link(q, self.pchain, g, 1)
                link(q.tensor_scalar(ve[:, p, :], m[:, p, :, 1], EPS, None, ALU.add))
                q.tensor_tensor(rs[:, p, :], ve[:, p, :], half_neg[:], ALU.pow).then_inc(self.rstd_ready, 1)

            def dve_norm(self, v, g):
                _, m, _, rs, xo = self.bufs
                p = g.parity
                v.wait_ge(self.rstd_ready, g.at(1, 1))
                for t in range(TG):
                    ins = v.tensor_scalar(xo[:, p, t, :], x_all[:, g.tile(t), :], m[:, p, t, 0:1],
                                          rs[:, p, t:t + 1], ALU.subtract, ALU.mult)
                ins.then_inc(self.xn_ready, 1)

            def pool_norm(self, q, g):
                _, m, _, rs, xo = self.bufs
                p = g.parity
                q.tensor_tensor(xo[:, p], x_all[:, g.tiles(), :],
                                m[:, p, :, 0:1].broadcast_to([P, TG, D]), ALU.subtract).then_inc(self.centred, 1)
                q.wait_ge(self.rstd_ready, g.at(1, 1))
                q.wait_ge(self.centred, g.at(1, 1))
                q.tensor_tensor(xo[:, p], xo[:, p], rs[:, p, :].unsqueeze(2).broadcast_to([P, TG, D]),
                                ALU.mult).then_inc(self.xn_ready, 1)

            def pe_transpose(self, pe, g):
                xo = self.bufs[4]
                pe.wait_ge(self.xn_ready, g.at(1, 1))
                for t in range(TG):
                    ins = pe.transpose(self.bank[:, t * P:(t + 1) * P], xo[:, g.parity, t, :], ident[:])
                ins.then_inc(self.t_ready, 1)

            def act_high(self, a, g):
                a.wait_ge(self.t_ready, g.at(1, 1))
                if self.split:
                    o = xh[:, g.cols(1), :]
                    a.activation(o, self.bank.rearrange("p (a c) -> p a c", a=1), ACT.Copy).then_inc(self.hi_done, 1)
                else:
                    a.activation(self.dst[:, g.parity, :], self.bank, ACT.Copy).then_inc(self.hi_done, 1)

            def dve_low(self, v, g):
                v.wait_ge(self.hi_done, g.at(1, 1))
                v.tensor_tensor(xl[:, g.cols(1), :], self.bank.rearrange("p (a c) -> p a c", a=1),
                                xh[:, g.cols(1), :].bitcast(F32), ALU.subtract).then_inc(self.lo_done, 1)

        class RouterLogits:

            def __init__(self, name, ln, wh, wl, lt_bank, lg_bank):
                self.ln, self.wh, self.wl, self.lt_bank, self.lg_bank = ln, wh, wl, lt_bank, lg_bank
                self.lt_ready = sem(f"{name}_logits_t")
                self.lt_copied = sem(f"{name}_logits_t_copied")
                self.lg_ready = sem(f"{name}_logits_ready")
                self.lg_copied = sem(f"{name}_logits_copied")

            def pe_product(self, pe, g):
                pe.wait_ge(self.ln.lo_done, g.at(1, 1))
                h, l = xh[:, g.cols(1), :], xl[:, g.cols(1), :]
                o = self.lt_bank.rearrange("p (a c) -> p a c", a=1)
                pe.matmul(o, self.wh, h, start=True, stop=False)
                pe.matmul(o, self.wh, l, start=False, stop=False)
                pe.matmul(o, self.wl, h, start=False, stop=True).then_inc(self.lt_ready, 1)

            def act_copy(self, a, g):
                a.wait_ge(self.lt_ready, g.at(1, 1))
                a.activation(lt_s[:, g.parity, :], self.lt_bank, ACT.Copy).then_inc(self.lt_copied, 1)

            def pe_transpose(self, pe, g):
                pe.wait_ge(self.lt_copied, g.at(1, 1))
                for t in range(TG):
                    ins = pe.transpose(self.lg_bank[:, t * P:(t + 1) * P],
                                       lt_s[:, g.parity, t * P:(t + 1) * P], ident[:])
                ins.then_inc(self.lg_ready, 1)

            def dve_copy(self, v, g):
                v.wait_ge(self.lg_ready, g.at(1, 1))
                v.tensor_copy(logits[:, g.tiles(), :],
                              self.lg_bank.rearrange("p (t e) -> p t e", t=TG)[:, :, 0:E]).then_inc(self.lg_copied, 1)

        def product3(pe, o, wh, wl, h, l, start=True, stop=True):
            pe.matmul(o, wh, h, start=start, stop=False)
            pe.matmul(o, wh, l, start=False, stop=False)
            return pe.matmul(o, wl, h, start=False, stop=stop)

        def sp_x(sp, g):
            xv = x.rearrange("b p d -> p b d")
            sp.dma_start(x_all[:, g * TG:(g + 1) * TG, :], xv[:, g * TG:(g + 1) * TG, :]).then_inc(s_x[g % 2], 16)

        def sp_setup(sp):
            for dst, src in first:
                sp.dma_start(dst, src).then_inc(s_first, 16)
            sp_x(sp, 0)
        sp_parts.append(sp_setup)

        def pool_setup(q):
            q.memset(half_neg[:], -0.5).then_inc(s_pool, 1)
            q.memset(ss[:], 0.0).then_inc(s_pool, 1)
            q.wait_ge(s_pool, 2)
        pool_parts.append(pool_setup)

        def dve_setup(v):
            v.memset(zero_col[:], 0.0).then_inc(s_dvec, 1)
        dve_parts.append(dve_setup)

        def act_setup(a):
            a.wait_ge(s_first, 16 * len(first))
            a.activation(tg[:], gate_in[:], ACT.Tanh).then_inc(s_tanh, 1)
            a.wait_ge(s_m0, 1)
            a.activation(w_m0[:], bank[0][:, 0:P], ACT.Copy).then_inc(s_m0e, 1)
            a.wait_ge(s_dvec, 1)
        act_parts.append(act_setup)

        def pe_setup(pe):
            pe.wait_ge(s_first, 16 * len(first))
            pe.matmul(bank[0][:, 0:P], w_wk0[:], w_wq0[:], start=True, stop=True).then_inc(s_m0, 1)
            pe.wait_ge(s_m0e, 1)
        pe_parts.append(pe_setup)

        def dve_setup_late(v):
            k = [1]

            def link(ins):
                k[0] += 1
                ins.then_inc(s_dvec, 1)
                v.wait_ge(s_dvec, k[0])
            v.memset(bias_hr[:], HALF_RANGE)
            v.memset(mask_f[:, S2:SK], 0.0)
            link(v.memset(ones_row[:], 1.0))
            v.wait_ge(s_small, 16 * len(small))
            v.tensor_copy(ident_bf[:], ident[:])
            link(v.tensor_copy(mask_f[:, 0:S2], mask_u8[:]))
            v.tensor_scalar(mask_bf[:], mask_f[:], MASK_FILL, None, ALU.mult)
            link(v.tensor_reduce(some_key[:], mask_f[:, 0:S2], AX.X, ALU.min))
            v.tensor_scalar(exp_scale[:], some_key[:], -float(DH) ** -0.5, float(DH) ** -0.5, ALU.mult,
                            ALU.add).then_inc(s_dve_setup, 1)

        def act_setup_late(a):
            a.wait_ge(s_m0, 2)
            a.activation(bo_all[:], M1[0:1, 0:P], ACT.Copy).then_inc(s_m0e, 1)

        def pe_setup_late(pe):
            pe.wait_ge(s_dve_setup, 1)
            pe.matmul(M1[0:1, 0:P], bv1[:], wo1[:], start=True, stop=False)
            pe.matmul(M1[0:1, 0:P], ones_row[:, 0:1], bo1[:], start=False, stop=True).then_inc(s_m0, 1)
            pe.wait_ge(s_m0e, 2)

        def act_split(a_, a):
            a_.wait_ge(s_dma[a.parity], a.pair(16, 16))
            a_.activation(w_hi[:, a.cols(WPIECE)], stage[:, a.parity, :], ACT.Copy).then_inc(s_split_hi, 1)

        def pool_split(q, a):
            q.wait_ge(s_split_hi, a.at(1, 1))
            cols = a.cols(WPIECE)
            q.tensor_tensor(w_lo[:, cols], stage[:, a.parity, :], w_hi[:, cols].bitcast(F32),
                            ALU.subtract).then_inc(s_split, 1)

        new_scope()
        stage = sb("stage", [P, 2, WPIECE])
        stats0, mv0 = sb("stats0", [P, 2, TG, 6]), sb("mv0", [P, 2, TG, 2])
        vpe0, rstd0, xn0 = sb("vpe0", [P, 2, TG]), sb("rstd0", [P, 2, TG]), sb("xn0", [P, 2, TG, D])
        with_a = dict(
            xt=sb("a_xt", [P, 2, GT]), k0=sb("a_k0", [P, 2, GK]), v0=sb("a_v0", [S2, 2, GT]),
            sm=sb("a_sm", [P, 2, TG, S2]), pr=sb("a_pr", [P, 2, TG, S2]), mx=sb("a_mx", [P, 2, TG]),
            rs=sb("a_rs", [P, 2, TG]), ri=sb("a_ri", [P, 2, TG]), rg=sb("a_rg", [P, 2, TG]),
            pt=sb("a_pt", [S2, 2, GT]))
        A = with_a
        a_ctx = [sem("a_ctx_loaded0"), sem("a_ctx_loaded1")]
        a_k_ready, a_v_ready = sem("a_keys_ready"), sem("a_values_ready")
        a_k_done, a_v_done = sem("a_keys_copied"), sem("a_values_copied")
        a_s_ready, a_sub = sem("a_scores_ready"), sem("a_scores_shifted")
        a_exp = sem("a_exp_done")
        a_pt_ready, a_pt_done = sem("a_probs_transposed"), sem("a_probs_copied")
        a_o_ready, a_res = sem("a_out_ready"), sem("a_residual_done")
        a_ch1, a_ch2 = sem("a_chain_max"), sem("a_chain_sum")
        a_rg = sem("a_inverse_ready")
        ln0 = LayerNorm("a_ln0", bank[0], (stats0, mv0, vpe0, rstd0, xn0), to_split=False, dst=A["xt"])
        ln1 = LayerNorm("a_ln1", bank[6], (stats, mv, vpe, rstd, xn))
        lg0 = RouterLogits("a_router", ln1, wg0h, wg0l, bank[7], bank[6])

        def sp_a(sp):
            for g in range(NG):
                if g >= 2:
                    sp.wait_ge(a_v_ready, g - 1)
                sp.dma_start(ctxg[:, g % 2, :], ctxT[:, g * GK:(g + 1) * GK]).then_inc(a_ctx[g % 2], 16)
                if g + 1 < NG:
                    if g >= 1:
                        sp.wait_ge(ln0.stats_ready, g)
                    sp_x(sp, g + 1)
                if g == 2:
                    for dst, src in small:
                        sp.dma_start(dst, src).then_inc(s_small, 16)
                if g >= 2:
                    sp.wait_ge(s_split, g - 1)
                sp.dma_start(stage[:, g % 2, :], weights[:, g * WPIECE:(g + 1) * WPIECE]).then_inc(s_dma[g % 2], 16)
        sp_parts.append(sp_a)

        def pool_a(q):
            def step(a, m, t):
                if t:
                    ln1.pool_rstd(q, t)
                if a:
                    ln0.pool_rstd(q, a)
                    pool_split(q, a)
            pipeline(q, step)
        pool_parts.append(pool_a)

        def pe_a(pe):
            def step(a, m, t):
                if m:
                    p = m.parity
                    pe.wait_ge(ln0.hi_done, m.at(1, 1))
                    pe.wait_ge(a_k_done, m.at(1, 1))
                    if not (m.i is None and m.c == 0):
                        pe.wait_ge(a_sub, m.at(1, 0))
                    for b in range(TG):
                        ins = pe.matmul(bank[3][:, b * SK:(b + 1) * SK], A["xt"][:, p, b * P:(b + 1) * P],
                                        A["k0"][:, p, b * SK:(b + 1) * SK], start=True, stop=True)
                    ins.then_inc(a_s_ready, 1)
                if a:
                    p = a.parity
                    first = a.i is None and a.c == 0
                    pe.wait_ge(a_ctx[p], a.pair(16, 16))
                    if not first:
                        pe.wait_ge(a_k_done, a.at(1, 0))
                        pe.wait_ge(a_v_done, a.at(1, 0))
                        pe.wait_ge(ln0.hi_done, a.at(1, 0))
                    pe.matmul(bank[1][:, 0:GK], w_m0[:], ctxg[:, p, :], start=True, stop=True).then_inc(a_k_ready, 1)
                    for b in range(TG):
                        ins = pe.matmul(bank[2][0:S2, b * P:(b + 1) * P], ctxg[:, p, b * SK:b * SK + S2],
                                        w_wv0[:], start=True, stop=True)
                    ins.then_inc(a_v_ready, 1)
                if m:
                    p = m.parity
                    pe.wait_ge(a_exp, m.at(1, 1))
                    if not (m.i is None and m.c == 0):
                        pe.wait_ge(a_pt_done, m.at(1, 0))
                    for b in range(TG):
                        ins = pe.transpose(bank[4][0:S2, b * P:(b + 1) * P], A["pr"][:, p, b, :], ident[:])
                    ins.then_inc(a_pt_ready, 1)
                if t:
                    ln1.pe_transpose(pe, t)
                if m:
                    p = m.parity
                    pe.wait_ge(a_pt_done, m.at(1, 1))
                    pe.wait_ge(a_v_done, m.at(1, 1))
                    if not (m.i is None and m.c == 0):
                        pe.wait_ge(a_res, m.at(1, 0))
                    for b in range(TG):
                        ins = pe.matmul(bank[5][:, b * P:(b + 1) * P], A["pt"][:, p, b * P:(b + 1) * P],
                                        A["v0"][:, p, b * P:(b + 1) * P], start=True, stop=True)
                    ins.then_inc(a_o_ready, 1)
                if a:
                    ln0.pe_transpose(pe, a)
                if t:
                    if t.i is None and t.c == 0:
                        pe.wait_ge(s_split, 1)
                    lg0.pe_product(pe, t)
                    lg0.pe_transpose(pe, t)
            pipeline(pe, step)
        pe_parts.append(pe_a)

        def act_a(a_):
            def step(a, m, t):
                if a:
                    p = a.parity
                    a_.wait_ge(a_k_ready, a.at(1, 1))
                    a_.activation(A["k0"][:, p, :], bank[1][:, 0:GK], ACT.Copy).then_inc(a_k_done, 1)
                    a_.wait_ge(a_v_ready, a.at(1, 1))
                    a_.activation(A["v0"][:, p, :], bank[2][0:S2, :], ACT.Copy).then_inc(a_v_done, 1)
                if m:
                    p = m.parity
                    a_.wait_ge(a_sub, m.at(1, 1))
                    a_.activation(A["pr"][:, p, :, :], A["sm"][:, p, :, :], ACT.Exp,
                                  bias=zero_col[:, 0:1], scale=float(D) ** -0.5).then_inc(a_exp, 1)
                    a_.wait_ge(a_pt_ready, m.at(1, 1))
                    a_.activation(A["pt"][:, p, :], bank[4][0:S2, :], ACT.Copy).then_inc(a_pt_done, 1)
                if a:
                    act_split(a_, a)
                if t:
                    ln1.act_high(a_, t)
                if a:
                    ln0.act_high(a_, a)
                if t:
                    lg0.act_copy(a_, t)
                    if not m:
                        Route(0, HEAD, rt_tail).act_ratio(a_)
            pipeline(a_, step)
        act_parts.append(act_a)

        def dve_a(v):
            route = Route(0, HEAD, route_buffers(stage[:].rearrange("p a c -> p (a c)")))

            def step(a, m, t):
                if t:
                    p = t.parity
                    v.wait_ge(a_o_ready, t.at(1, 1))
                    for b in range(TG):
                        ins = v.scalar_tensor_tensor(
                            out=x_all[:, t.tile(b), :], in0=bank[5][:, b * P:(b + 1) * P].rearrange("p (a c) -> p a c", a=1),
                            scalar=A["rg"][:, p, b:b + 1], in1=x_all[:, t.tile(b), :], op0=ALU.mult, op1=ALU.add)
                    ins.then_inc(a_res, 1)
                    wait_apart(v, a_res, t.at(1, 1))
                    ln1.dve_stats(v, t)
                    if not m:
                        v.wait_ge(s_split, NG)
                        v.wait_ge(s_small, 16 * len(small))
                        v.wait_ge(lg0.lg_copied, NG - 1)
                        route.first(v)
                if m:
                    p = m.parity
                    v.wait_ge(a_s_ready, m.at(1, 1))
                    s = bank[3][:, 0:GK].rearrange("p (b k) -> p b k", b=TG)[:, :, 0:S2]
                    link = Link(v, a_ch1, m, 1)
                    link(v.tensor_reduce(A["mx"][:, p, :], s, AX.X, ALU.max))
                    v.tensor_tensor(A["sm"][:, p, :, :], s,
                                    A["mx"][:, p, :].unsqueeze(2).broadcast_to([P, TG, S2]), ALU.subtract).then_inc(a_sub, 1)
                if a:
                    wait_apart(v, s_x[a.parity], a.pair(16, 16))
                    ln0.dve_stats(v, a)
                if t:
                    ln1.dve_norm(v, t)
                    if not m:
                        route.second(v)
                if a:
                    if not (a.i is None and a.c < 2):
                        v.wait_ge(ln0.t_ready, a.at(1, -1))
                    ln0.dve_norm(v, a)
                if m:
                    p = m.parity
                    v.wait_ge(a_exp, m.at(1, 1))
                    link = Link(v, a_ch2, m, 2)
                    link(v.tensor_reduce(A["rs"][:, p, :], A["pr"][:, p, :, :], AX.X, ALU.add))
                    link(v.reciprocal(A["ri"][:, p, :], A["rs"][:, p, :]))
                    if m.i is None and m.c == 0:
                        v.wait_ge(s_tanh, 1)
                    v.tensor_scalar(A["rg"][:, p, :], A["ri"][:, p, :], tg[:, 0:1], None, ALU.mult).then_inc(a_rg, 1)
                    v.wait_ge(a_rg, m.at(1, 1))
                if t:
                    ln1.dve_low(v, t)
                    if not m:
                        route.weights(v)
                    lg0.dve_copy(v, t)
            pipeline(v, step)
        dve_parts.append(dve_a)

        HEAD, TAIL = slice(0, NB - TG), slice(NB - TG, NB)

        def route_buffers(*memory):
            w = (NB - TG) * E
            places = [t[:, i * w:(i + 1) * w] for t in memory for i in range(t.shape[1] // w)]
            return {n: places[i].rearrange("p (t e) -> p t e", e=E) for i, n in enumerate(ROUTE_BUFS)}

        class Route:
            links = exps = asks = rounds = 0

            def __init__(self, layer, tiles, rt):
                self.layer, self.tiles, self.rt = layer, tiles, rt
                self.n = tiles.stop - tiles.start
                self.r1 = {n: r1[n][:, tiles] for n in r1}

            def link(self, v, ins):
                Route.links += 1
                ins.then_inc(s_rchain, 1)
                v.wait_ge(s_rchain, Route.links)

            def bc(self, t):
                return t.unsqueeze(2).broadcast_to([P, self.n, E])

            def pick(self, v, values, best, onehot):
                rt, r1, link = self.rt, self.r1, self.link
                rankb = rank[:].unsqueeze(1).broadcast_to([P, self.n, E])
                link(v, v.tensor_reduce(best, values, AX.X, ALU.max))
                link(v, v.tensor_tensor(rt["pick"][:], values, self.bc(best), ALU.is_ge))
                link(v, v.tensor_tensor(rt["tmp"][:], rt["pick"][:], rankb, ALU.mult))
                link(v, v.tensor_reduce(r1["c"], rt["tmp"][:], AX.X, ALU.max))
                link(v, v.tensor_tensor(onehot, rt["tmp"][:], self.bc(r1["c"]), ALU.is_equal))

            def act_sigmoid(self, a):
                a.activation(self.rt["wt"][:], logits[:, self.tiles, :], ACT.Exp, bias=zero_col[:, 0:1],
                             scale=-1.0).then_inc(s_re, 1)

            def act_ratio(self, a):
                Route.asks += 1
                a.wait_ge(s_ract, Route.asks)
                a.activation(self.r1["e"], self.r1["d"], ACT.Exp, bias=zero_col[:, 0:1]).then_inc(s_re, 1)

            def first(self, v):
                rt, r1, link = self.rt, self.r1, self.link
                if self.layer == 0:
                    self.values = logits[:, self.tiles, :]
                else:
                    Route.exps += 1
                    v.wait_ge(s_re, Route.exps)
                    link(v, v.tensor_scalar(rt["tmp"][:], rt["wt"][:], 1.0, None, ALU.add))
                    link(v, v.reciprocal(rt["sig"][:], rt["tmp"][:]))
                    link(v, v.tensor_tensor(rt["val"][:], rt["sig"][:],
                                            eb1[:].unsqueeze(1).broadcast_to([P, self.n, E]), ALU.add))
                    self.values = rt["val"][:]
                self.pick(v, self.values, r1["m"], rt["first"][:])

            def second(self, v):
                rt, r1 = self.rt, self.r1
                self.link(v, v.scalar_tensor_tensor(out=rt["wt"][:], in0=rt["first"][:], scalar=TAKEN,
                                                    in1=self.values, op0=ALU.mult, op1=ALU.add))
                self.pick(v, rt["wt"][:], r1["m2"], rt["second"][:])
                if self.layer == 0:
                    v.tensor_tensor(r1["d"], r1["m2"], r1["m"], ALU.subtract).then_inc(s_ract, 1)

            def weights(self, v):
                rt, r1, link, bc = self.rt, self.r1, self.link, self.bc
                if self.layer == 0:
                    Route.exps += 1
                    v.wait_ge(s_re, Route.exps)
                    link(v, v.tensor_scalar(r1["m"], r1["e"], 1.0, None, ALU.add))
                    link(v, v.reciprocal(r1["w1"], r1["m"]))
                    link(v, v.tensor_tensor(r1["w2"], r1["e"], r1["w1"], ALU.mult))
                    v.tensor_tensor(rt["pick"][:], rt["first"][:], bc(r1["w1"]), ALU.mult)
                    link(v, v.tensor_tensor(rt["tmp"][:], rt["second"][:], bc(r1["w2"]), ALU.mult))
                    link(v, v.tensor_tensor(rt["wt"][:], rt["pick"][:], rt["tmp"][:], ALU.add))
                else:
                    link(v, v.tensor_tensor(rt["pick"][:], rt["first"][:], rt["second"][:], ALU.add))
                    link(v, v.tensor_tensor(rt["tmp"][:], rt["pick"][:], rt["sig"][:], ALU.mult))
                    link(v, v.tensor_reduce(r1["d"], rt["tmp"][:], AX.X, ALU.add))
                    link(v, v.tensor_scalar(r1["m"], r1["d"], EPS_ROUTE, None, ALU.add))
                    link(v, v.reciprocal(r1["w1"], r1["m"]))
                    link(v, v.tensor_tensor(rt["wt"][:], rt["tmp"][:], bc(r1["w1"]), ALU.mult))
                gate = tg[:, 2 + self.layer:3 + self.layer]
                link(v, v.tensor_scalar(rt["pick"][:], rt["wt"][:], gate, None, ALU.mult))
                link(v, v.tensor_copy(sc_h[:, self.tiles, :], rt["pick"][:]))
                Route.rounds += 1
                v.tensor_tensor(sc_l[:, self.tiles, :], rt["pick"][:], sc_h[:, self.tiles, :].bitcast(F32),
                                ALU.subtract).then_inc(s_route, 1)
                v.wait_ge(s_route, Route.rounds)

            def all(self, v):
                self.first(v)
                self.second(v)
                self.weights(v)

        new_scope()
        B = dict(hr=sb("b_hr", [P, 2, HC, GT]), hs=sb("b_hs", [P, 2, HC, GT]),
                 hh=sb("b_hh", [P, 2, HC, GT], F32R), hl=sb("b_hl", [P, 2, HC, GT], F32R),
                 y=sb("b_y", [P, 2, GT]))

        class ExpertPass:

            def __init__(self, name, n, y):
                self.n, self.y = n, y
                self.ss_ready = sem(f"{name}_weights_placed")
                self.ss_chain = sem(f"{name}_weights_chain")
                self.st_ready = sem(f"{name}_weights_transposed")
                self.st_done = sem(f"{name}_weights_copied")
                self.z_ready = sem(f"{name}_hidden_ready")
                self.z_read = sem(f"{name}_hidden_read")
                self.bc_ready = sem(f"{name}_spread_ready")
                self.scaled = sem(f"{name}_hidden_scaled")
                self.hi_done = sem(f"{name}_hidden_high")
                self.lo_done = sem(f"{name}_hidden_low")
                self.used = sem(f"{name}_hidden_used")
                self.y_done = sem(f"{name}_y_copied")
                self.yt_ready = sem(f"{name}_y_transposed")
                self.res = sem(f"{name}_residual_done")

            def first(self, g):
                return g.i is None and g.c == 0

            def before(self, eng, s, g, k, back):
                if g.i is None and self.n * g.c + k - back < 0:
                    return
                eng.wait_ge(s, g.at(self.n, k - back + 1))

            def prev(self, m, t, k, back=1):
                return (m, k - back) if k >= back else (t, self.n + k - back)

            def dve_place(self, v, a):
                p = a.parity
                if not (a.i is None and a.c < 2):
                    v.wait_ge(self.st_ready, a.at(1, -1))
                v.tensor_copy(ss[:, p, :, 0:E], sc_h[:, a.tiles(), :].bitcast(F32))
                v.tensor_copy(ss[:, p, :, 32:32 + E], sc_l[:, a.tiles(), :].bitcast(F32)).then_inc(self.ss_ready, 1)

            def pe_place(self, pe, a, misc):
                pe.wait_ge(self.ss_ready, a.at(1, 1))
                for b in range(TG):
                    ins = pe.transpose(misc[:, b * P:(b + 1) * P], ss[:, a.parity, b, :], ident[:])
                ins.then_inc(self.st_ready, 1)

            def act_place(self, a_, a, misc):
                a_.wait_ge(self.st_ready, a.at(1, 1))
                a_.activation(st[:, a.parity, :], misc, ACT.Copy).then_inc(self.st_done, 1)

            def act_high(self, a_, g, k):
                self.before(a_, self.scaled, g, k, 0)
                self.before(a_, self.used, g, k, 2)
                q = (self.n * g.c + k) % 2
                a_.activation(*self.high(q), ACT.Copy).then_inc(self.hi_done, 1)

            def dve_low(self, v, g, k):
                self.before(v, self.hi_done, g, k, 0)
                q = (self.n * g.c + k) % 2
                o, i0, i1 = self.low(q)
                v.tensor_tensor(o, i0, i1, ALU.subtract).then_inc(self.lo_done, 1)

            def act_y(self, a_, t, ybank):
                a_.wait_ge(self.used, t.at(self.n, self.n))
                a_.activation(self.y[:, t.parity, :], ybank, ACT.Copy).then_inc(self.y_done, 1)

            def pe_y(self, pe, t, misc):
                pe.wait_ge(self.y_done, t.at(1, 1))
                for b in range(TG):
                    ins = pe.transpose(misc[:, b * P:(b + 1) * P], self.y[:, t.parity, b * P:(b + 1) * P], ident[:])
                ins.then_inc(self.yt_ready, 1)

            def dve_residual(self, v, t, misc):
                v.wait_ge(self.yt_ready, t.at(1, 1))
                xt = x_all[:, t.tiles(), :]
                v.tensor_tensor(xt, misc.rearrange("p (b c) -> p b c", b=TG), xt, ALU.add).then_inc(self.res, 1)
                wait_apart(v, self.res, t.at(1, 1))

        Z, SBC, Y, MISC = [bank[0:2], bank[2:4]], [bank[4], bank[5]], bank[6], bank[7]
        xb = ExpertPass("b", E, B["y"])
        Bb = B
        xb.high = lambda q: (Bb["hh"][:, q, :, :], Bb["hs"][:, q, :, :])
        xb.low = lambda q: (Bb["hl"][:, q, :, :], Bb["hs"][:, q, :, :], Bb["hh"][:, q, :, :].bitcast(F32))
        ln2 = LayerNorm("b_ln", MISC, (stats, mv, vpe, rstd, xn))

        def w1s(w, e, c):
            return w[:, (e * HC + c) * P:(e * HC + c + 1) * P]

        c_prepare = {}

        def pe_b(pe):
            pe.wait_ge(s_split, NG)
            pe.wait_ge(ln1.lo_done, NG)

            def up(g, e):
                q = e % 2
                h, l = xh[:, g.cols(1), :], xl[:, g.cols(1), :]
                xb.before(pe, xb.z_read, g, e, 2)
                for c in range(HC):
                    o = Z[q][c].rearrange("p (a c) -> p a c", a=1)
                    ins = product3(pe, o, w1s(w1h, e, c), w1s(w1l, e, c), h, l)
                ins.then_inc(xb.z_ready, 1)
                if e == 0:
                    pe.wait_ge(xb.st_done, g.at(1, 1))
                xb.before(pe, xb.scaled, g, e, 2)
                pe.matmul(SBC[q], sel0[:, e, :], st[:, g.parity, :], start=True, stop=True).then_inc(xb.bc_ready, 1)

            def down(g, e):
                q = e % 2
                if e == 0:
                    if not xb.first(g):
                        pe.wait_ge(xb.y_done, g.at(1, 0))
                    pe.matmul(Y, b2h, st[:, g.parity, :], start=True, stop=False)
                    pe.matmul(Y, b2l, st[:, g.parity, :], start=False, stop=False)
                xb.before(pe, xb.lo_done, g, e, 0)
                for c in range(HC):
                    ins = product3(pe, Y, w1s(w2h, e, c), w1s(w2l, e, c), Bb["hh"][:, q, c, :], Bb["hl"][:, q, c, :],
                                   start=False, stop=(e == E - 1 and c == HC - 1))
                ins.then_inc(xb.used, 1)

            def place(a):
                xb.pe_place(pe, a, MISC)

            def y_back(a, t):
                if a:
                    pe.wait_ge(xb.st_done, a.at(1, 1))
                elif not xb.first(t):
                    pe.wait_ge(ln2.lo_done, t.at(1, 0))
                xb.pe_y(pe, t, MISC)

            def step(a, m, t):
                for e in range(E if m else LAG):
                    if m:
                        up(m, e)
                    if m and e == 4 and t:
                        y_back(a, t)
                    g, k = xb.prev(m, t, e, LAG)
                    if g:
                        down(g, k)
                    if t and not m and e < 2:
                        c_prepare["pe"](pe, e)
                    if m and e == 2 and a:
                        place(a)
                    if m and e == 7 and t:
                        ln2.pe_transpose(pe, t)
                if not m:
                    if a:
                        place(a)
                    if t:
                        c_prepare["pe"](pe, 2)
                        y_back(a, t)
                        c_prepare["pe"](pe, 3, 4)
                        ln2.pe_transpose(pe, t)
                        c_prepare["pe"](pe, 5, 6, 7, 8)
            pipeline(pe, step)
        pe_parts.append(pe_b)

        def act_b(a_):
            tail = Route(0, TAIL, rt_tail)
            def relu(g, e):
                q = e % 2
                xb.before(a_, xb.z_ready, g, e, 0)
                xb.before(a_, xb.scaled, g, e, 2)
                for c in range(HC):
                    ins = a_.activation(Bb["hr"][:, q, c, :], Z[q][c], ACT.Relu, bias=b1s[:, e, c:c + 1])
                ins.then_inc(xb.z_read, 1)

            def step(a, m, t):
                if m:
                    for e in range(E):
                        if e == LAG and t:
                            xb.act_y(a_, t, Y)
                        relu(m, e)
                        g, k = xb.prev(m, t, e)
                        if g:
                            xb.act_high(a_, g, k)
                        if e == 3 and a:
                            xb.act_place(a_, a, MISC)
                        if e == 7 and t:
                            ln2.act_high(a_, t)
                else:
                    if a:
                        xb.act_place(a_, a, MISC)
                    if t:
                        xb.act_high(a_, t, E - 1)
                        c_prepare["act"](a_, 0, 1)
                        xb.act_y(a_, t, Y)
                        c_prepare["act"](a_, 2, 3, 4)
                        ln2.act_high(a_, t)
                        c_prepare["act"](a_, 5, 6, 7, 8)
            pipeline(a_, step, lambda: tail.act_ratio(a_))
        act_parts.append(act_b)

        def dve_b(v):
            tail = Route(0, TAIL, rt_tail)

            def route_last():
                v.wait_ge(lg0.lg_copied, NG)
                tail.all(v)
                v.tensor_scalar(bqlo[:], bq1[:], part[:, 0:1], None, ALU.mult)
                v.tensor_scalar(bklo[:], bk1[:], part[:, 1:2], None, ALU.mult).then_inc(s_biases, 1)
            v.wait_ge(s_pool, 2)

            def scale(g, e):
                q = e % 2
                xb.before(v, xb.z_read, g, e, 0)
                xb.before(v, xb.bc_ready, g, e, 0)
                xb.before(v, xb.lo_done, g, e, 2)
                v.tensor_tensor(Bb["hs"][:, q, :, :], Bb["hr"][:, q, :, :],
                                SBC[q].unsqueeze(1).broadcast_to([P, HC, GT]), ALU.mult).then_inc(xb.scaled, 1)

            def low(g, k):
                xb.before(v, xb.used, g, k, 2)
                xb.dve_low(v, g, k)

            def step(a, m, t):
                if m:
                    for e in range(E):
                        scale(m, e)
                        g, k = xb.prev(m, t, e)
                        if g:
                            low(g, k)
                        if e == 0 and a:
                            xb.dve_place(v, a)
                        if e == 4 and t:
                            xb.dve_residual(v, t, MISC)
                            ln2.dve_stats(v, t)
                        if e == 5 and t:
                            ln2.dve_norm(v, t)
                        if e == 7 and t:
                            ln2.dve_low(v, t)
                else:
                    if a:
                        xb.dve_place(v, a)
                    if t:
                        low(t, E - 1)
                        c_prepare["dve"](v, 0, 1)
                        xb.dve_residual(v, t, MISC)
                        ln2.dve_stats(v, t)
                        c_prepare["dve"](v, 2)
                        ln2.dve_norm(v, t)
                        c_prepare["dve"](v, 3, 4)
                        ln2.dve_low(v, t)
                        c_prepare["dve"](v, 5, 6, 7)
                        dve_setup_late(v)
            pipeline(v, step, route_last)
        dve_parts.append(dve_b)

        def pool_b(q):
            def step(a, m, t):
                if t and not m:
                    c_prepare["pool"](q)
                if t:
                    ln2.pool_rstd(q, t)
            pipeline(q, step)
        pool_parts.append(pool_b)

        new_scope()
        NU = 2 * NC4
        NQ = TG * NC4
        NHALF = NQ // 2
        w1_0, w1_1 = WCOL["w1"][0], WCOL["w2"][1]
        qs = w_hi[:, w1_0:w1_1].rearrange("p (a c t) -> p a c t", a=2, c=NC4)
        ks = w_lo[:, w1_0:w1_0 + 2 * NC4 * GK].rearrange("p (a c b k) -> p a c b k", a=2, c=NC4, b=TG)
        kb = sb("c_kb", [P, 2, NC4, HQ, SK], F32R)
        sm1 = sb("c_sm", [P, 2, 2 * HQ, S2])
        pf1 = sb("c_pf", [P, 2, 2 * HQ, S2])
        ph = sb("c_ph", [S2, NC4, HQ * P], F16)
        pl_ = sb("c_pl", [S2, NC4, HQ * P], F16)
        pt32 = sb("c_pt32", [S2, 2, HQ * P])
        on = sb("c_on", [P, TG, D])
        ot = sb("c_ot", [P, GT])
        o10 = sb("c_o10", [P, NH, VW])
        oi = sb("c_oi", [P, NH])
        lowpart = sb("c_lowpart", [P, 2, GT], F32R)
        v3 = sb("c_v3", [S2, 2, TG, NH, 3, VW], BF16)
        vf = sb("c_vf", [S2, TG * D])
        vr = sb("c_vr", [S2, TG * D])
        mx1 = sb("c_mx", [P, 2, 2 * HQ])
        c_ctx = [sem("c_ctx_loaded0"), sem("c_ctx_loaded1")]
        u_ready, u_act, u_read = sem("c_prep_ready"), sem("c_prep_low"), sem("c_prep_read")
        v_ready, v_copied = sem("c_values_ready"), sem("c_values_copied")
        v_split, v_chain = sem("c_values_split"), sem("c_values_chain")
        kb_zero, kb_placed = sem("c_keys_cleared"), [sem("c_keys_placed0"), sem("c_keys_placed1")]
        s1_ready, s1_max, s1_sub, s1_exp = sem("c_scores"), sem("c_max"), sem("c_shifted"), sem("c_exp")
        t1_ready, hi_done, pv_used = sem("c_probs_t"), sem("c_probs_high"), sem("c_pv")
        lo_done = [sem("c_probs_low_even"), sem("c_probs_low_odd")]
        o_read, o_inv, o_done = sem("c_out_summed"), sem("c_out_inverse"), sem("c_out_normed")
        ot_ready, ot_done = sem("c_out_transposed"), sem("c_out_t_copied")
        wo_ready, c_res = sem("c_projected"), sem("c_residual_done")
        M1 = bank[6]

        def prep_bank(a, u):
            return bank[(0, 1)[u % 2] if a.i is None and a.c == 0 else (5, 7)[u % 2]]

        ln3 = LayerNorm("c_ln", M1, (stats, mv, vpe, rstd, xn))
        lg1 = RouterLogits("c_router", ln3, wg1h, wg1l, M1, M1)

        def before(eng, s, n, g, k, back=0, wait=None):
            if g.i is None and n * g.c + k - back < 0:
                return
            if wait:
                wait(eng, s, g.at(n, k - back + 1))
            else:
                eng.wait_ge(s, g.at(n, k - back + 1))

        def lagged(m, t, k):
            return (m, k) if k >= 0 else (t, NQ + k)

        def route_buffers_c():
            return route_buffers(sm1[:].rearrange("p a h k -> p (a h k)"), ctxg[:].rearrange("p a k -> p (a k)"))

        def sp_c(sp):
            def place_keys(g, b):
                for j in range(HQ):
                    r = slice(4 * DH * j, 4 * DH * (j + 1))
                    sp.dma_start(kb[r, b % 2, :, j, :].bitcast(F32),
                                 ks[r, g.parity, :, b, :].bitcast(F32)).then_inc(kb_placed[b % 2], 16)

            def step(a, m, t):
                if m:
                    for b in range(1, TG):
                        before(sp, s1_ready, NHALF, m, 2 * b + 1, 4)
                        place_keys(m, b)
                if a:
                    if m:
                        before(sp, s1_sub, NHALF, m, 5)
                    else:
                        before(sp, u_read, NU, a, NU - 1)
                    place_keys(a, 0)
            sp.wait_ge(kb_zero, 2)
            pipeline(sp, step)
        sp_parts.append(sp_c)

        def pe_c(pe, early_only=False):
            def prepare(a, u):
                p = a.parity
                o = prep_bank(a, u)
                if u == 0:
                    before(pe, v_copied, 1, a, 0, 1)
                before(pe, u_read, NU, a, u, 2)
                if u < NC4:
                    w = slice(u * P, (u + 1) * P)
                    ins = product3(pe, o.rearrange("p (a c) -> p a c", a=1), wqh[:, w], wql[:, w],
                                   xh[:, a.cols(1), :], xl[:, a.cols(1), :])
                else:
                    if u == NC4:
                        pe.wait_ge(c_ctx[p], a.pair(16, 16))
                    c = u - NC4
                    ins = pe.matmul(o[:, 0:GK], wk1[:, c * P:(c + 1) * P], ctxg[:, p, :], start=True, stop=True)
                ins.then_inc(u_ready, 1)

            def prepare_values(a):
                before(pe, u_read, NU, a, NU - 2)
                for b in range(TG):
                    ins = pe.matmul(prep_bank(a, 0)[0:S2, b * D:(b + 1) * D], ctxg[:, a.parity, b * SK:b * SK + S2], wv1[:],
                                    start=True, stop=True)
                ins.then_inc(v_ready, 1)

            def scores(m, h):
                b = h // 2
                before(pe, s1_sub, NHALF, m, h, 1)
                if h == 0:
                    pe.wait_ge(u_read, m.at(NU, NU))
                    if m.i is None and m.c == 0:
                        pe.wait_ge(v_copied, 1)
                if h % 2 == 0:
                    pe.wait_ge(kb_placed[b % 2], m.at(16 * HQ * TG // 2, 16 * HQ * (b // 2 + 1)))
                for k in range(2):
                    c = (h % 2) * 2 + k
                    o = bank[k][:, 0:GK]
                    pe.matmul(o, ident_bf[:], mask_bf[:].unsqueeze(1).broadcast_to([P, HQ, SK]), start=True, stop=False)
                    ins = pe.matmul(o, qs[:, m.parity, c, b * P:(b + 1) * P],
                                    kb[:, b % 2, c, :, :].rearrange("p j k -> p (j k)"), start=False, stop=True)
                ins.then_inc(s1_ready, 1)

            def transpose(g, q):
                h = q // 2
                before(pe, s1_exp, NHALF, g, h)
                if q % 2 == 0:
                    before(pe, hi_done, NQ, g, q, 2)
                else:
                    before(pe, lo_done[1], NHALF, g, q // 2, 1)
                for j in range(HQ):
                    ins = pe.transpose(bank[2 + q % 2][0:S2, j * P:(j + 1) * P],
                                       pf1[:, h % 2, (q % 2) * HQ + j, :], ident[:])
                ins.then_inc(t1_ready, 1)

            def values(g, q):
                b, c = q // NC4, q % NC4
                before(pe, lo_done[q % 2], NHALF, g, q // 2)
                if c == 0:
                    before(pe, o_read, TG, g, b, 1)
                    if b == 0:
                        pe.wait_ge(v_split, g.at(1, 1))
                for j in range(HQ):
                    h = c * HQ + j
                    o = bank[4][:, h * 3 * VW:(h + 1) * 3 * VW]
                    vv = v3[:, g.parity, b, h, :, :].rearrange("p s d -> p (s d)")
                    pe.matmul(o, ph[:, q % NC4, j * P:(j + 1) * P], vv, start=True, stop=False)
                    ins = pe.matmul(o, pl_[:, q % NC4, j * P:(j + 1) * P], vv, start=False, stop=True)
                ins.then_inc(pv_used, 1)

            def turn_out(t):
                pe.wait_ge(o_done, t.at(TG, TG))
                for b in range(TG):
                    ins = pe.transpose(M1[:, b * P:(b + 1) * P], on[:, b, :], ident[:])
                ins.then_inc(ot_ready, 1)

            def project(t):
                pe.wait_ge(ot_done, t.at(1, 1))
                pe.matmul(M1.rearrange("p (b d) -> p b d", b=TG), ones_row[:],
                          bo_all[:].unsqueeze(1).broadcast_to([1, TG, D]), start=True, stop=False)
                for b in range(TG):
                    ins = pe.matmul(M1[:, b * P:(b + 1) * P], ot[:, b * P:(b + 1) * P], wo1[:], start=False,
                                    stop=(b == TG - 1))
                ins.then_inc(wo_ready, 1)

            def early(*units):
                for u in units:
                    if u == 0:
                        pe.wait_ge(xb.z_read, NG * E)
                    if u < NU:
                        prepare(Group(None, 0), u)
                    else:
                        prepare_values(Group(None, 0))
            if early_only:
                return early

            def step(a, m, t):
                for i in range(NQ):
                    g, q = lagged(m, t, i - 6)
                    if g:
                        values(g, q)
                    if t and i == 6:
                        turn_out(t)
                    g, q = lagged(m, t, i - 3)
                    if g:
                        transpose(g, q)
                    if m and i % 2 == 1 and i < NQ - 1:
                        scores(m, (i + 1) // 2)
                    if a and i == NQ - 1:
                        scores(a, 0)
                    if a and m and i < NU:
                        prepare(a, i)
                    if t and i == 6:
                        project(t)
                    if a and m and i == NU:
                        prepare_values(a)
                    if t and i == 11:
                        ln3.pe_transpose(pe, t)
                    if t and i == 13:
                        lg1.pe_product(pe, t)
                    if t and i == 14:
                        lg1.pe_transpose(pe, t)
            pe.wait_ge(ln2.lo_done, NG)
            pe_setup_late(pe)
            pipeline(pe, step)
        pe_parts.append(pe_c)

        def act_c(a_, early_only=False):
            def load_context(a):
                if a.i is None and a.c < 2:
                    a_.wait_ge(a_v_ready, NG)
                before(a_, v_ready, 1, a, 0, 2)
                a_.dma_start(ctxg[:, a.parity, :], ctxT[:, a.cols(GK)]).then_inc(c_ctx[a.parity], 16)

            def prepare(a, u):
                k, c, w = (0, u, GT) if u < NC4 else (1, u - NC4, GK)
                before(a_, u_ready, NU, a, u)
                blo = (bqlo, bklo)[k]
                a_.activation(lowpart[:, u % 2, 0:w], prep_bank(a, u)[:, 0:w], ACT.Identity, bias=blo[:, c:c + 1],
                              scale=part[:, k:k + 1]).then_inc(u_act, 1)

            def prepare_values(a):
                before(a_, v_ready, 1, a, 0)
                before(a_, v_split, 1, a, 0, 1)
                a_.activation(vf[:], prep_bank(a, 0)[0:S2, :], ACT.Copy).then_inc(v_copied, 1)

            def high(g, q):
                before(a_, t1_ready, NQ, g, q)
                before(a_, pv_used, NQ, g, q, NC4)
                if q % 2 == 0:
                    before(a_, lo_done[0], NHALF, g, q // 2, 2)
                    a_.activation(pt32[:, q // 2 % 2, :], bank[2][0:S2, :], ACT.Copy)
                a_.activation(ph[:, q % NC4, :], bank[2 + q % 2][0:S2, :], ACT.Copy).then_inc(hi_done, 1)

            def exp(m, h):
                before(a_, s1_sub, NHALF, m, h)
                before(a_, t1_ready, NQ, m, 2 * h + 1, 4)
                a_.activation(pf1[:, h % 2, :, :], sm1[:, h % 2, :, :], ACT.Exp, bias=bias_hr[:, 0:1],
                              scale=exp_scale[:, 0:1]).then_inc(s1_exp, 1)

            def early(*units):
                for u in units:
                    if u == 0:
                        a_.wait_ge(s_biases, 1)
                        load_context(Group(None, 0))
                    if u < NU:
                        prepare(Group(None, 0), u)
                    else:
                        prepare_values(Group(None, 0))
            if early_only:
                return early

            def step(a, m, t):
                if a and m:
                    load_context(a)
                if t and not m:
                    a_.wait_ge(lg1.lg_copied, NG - 1)
                    Route(1, HEAD, route_buffers_c()).act_sigmoid(a_)
                for i in range(NQ):
                    if m and i % 2 == 1:
                        exp(m, i // 2)
                    if t and i == 6:
                        a_.wait_ge(ot_ready, t.at(1, 1))
                        a_.activation(ot[:], M1, ACT.Copy).then_inc(ot_done, 1)
                    g, q = lagged(m, t, i - 3)
                    if g:
                        high(g, q)
                    if a and m and i < NU:
                        prepare(a, i)
                    if a and m and i == NU:
                        prepare_values(a)
                    if t and i == 11:
                        ln3.act_high(a_, t)
                    if t and i == 13:
                        lg1.act_copy(a_, t)
            act_setup_late(a_)
            pipeline(a_, step)
        act_parts.append(act_c)

        def dve_c(v, early_only=False):
            route = Route(1, HEAD, route_buffers_c())

            def prepare(a, u):
                p, o = a.parity, prep_bank(a, u)
                lp = lowpart[:, u % 2, :].bitcast(F32)
                before(v, u_act, NU, a, u)
                if u < NC4:
                    v.scalar_tensor_tensor(out=qs[:, p, u, :], in0=o, scalar=bq1[:, u:u + 1], in1=lp,
                                           op0=ALU.add, op1=ALU.subtract).then_inc(u_read, 1)
                else:
                    c = u - NC4
                    v.scalar_tensor_tensor(out=ks[:, p, c, :, :].rearrange("p b k -> p (b k)"), in0=o[:, 0:GK],
                                           scalar=bk1[:, c:c + 1], in1=lp[:, 0:GK],
                                           op0=ALU.add, op1=ALU.subtract).then_inc(u_read, 1)

            def scores_of(h):
                s = psum[:, 0:2, 0:GK].rearrange("p k (j s) -> p k j s", j=HQ)[:, :, :, 0:S2]
                return s, mx1[:, h % 2, :].rearrange("p (k j) -> p k j", k=2)

            def maximum(m, h):
                before(v, s1_ready, NHALF, m, h)
                s, mm = scores_of(h)
                v.tensor_reduce(mm, s, AX.X, ALU.max).then_inc(s1_max, 1)

            def shift(m, h):
                before(v, s1_exp, NHALF, m, h, 2)
                before(v, s1_max, NHALF, m, h)
                s, mm = scores_of(h)
                v.tensor_tensor(sm1[:, h % 2, :, :].rearrange("p (k j) s -> p k j s", k=2), s,
                                mm.unsqueeze(3).broadcast_to([P, 2, HQ, S2]), ALU.subtract).then_inc(s1_sub, 1)

            def low(g, q):
                before(v, hi_done, NQ, g, q)
                before(v, pv_used, NQ, g, q, NC4)
                v.tensor_tensor(pl_[:, q % NC4, :], bank[2 + q % 2][0:S2, :], ph[:, q % NC4, :],
                                ALU.subtract).then_inc(lo_done[1], 1)

            def combine(g, b):
                before(v, pv_used, NQ, g, NC4 * b + NC4 - 1)
                v.tensor_reduce(o10[:], bank[4][:, 0:NH * 3 * VW].rearrange("p (h s d) -> p h d s", h=NH, s=3),
                                AX.X, ALU.add).then_inc(o_read, 1)

            def invert(g, b):
                before(v, o_read, TG, g, b)
                v.reciprocal(oi[:], o10[:, :, DH]).then_inc(o_inv, 1)

            def divide(g, b):
                before(v, o_inv, TG, g, b)
                v.tensor_tensor(on[:, b, :].rearrange("p (h d) -> p h d", h=NH), o10[:, :, 0:DH],
                                oi[:].unsqueeze(2).broadcast_to([P, NH, DH]), ALU.mult).then_inc(o_done, 1)

            def residual(t):
                v.wait_ge(wo_ready, t.at(1, 1))
                xt = x_all[:, t.tiles(), :].rearrange("p b d -> p (b d)")
                v.scalar_tensor_tensor(out=xt, in0=M1, scalar=tg[:, 1:2], in1=xt,
                                       op0=ALU.mult, op1=ALU.add).then_inc(c_res, 1)
                wait_apart(v, c_res, t.at(1, 1))

            def early(*units):
                for u in units:
                    prepare(Group(None, 0), u)
            if early_only:
                return early

            def step(a, m, t):
                for i in range(NQ):
                    if m and i % 2 == 0:
                        maximum(m, i // 2)
                    go, qo = lagged(m, t, i - 9)
                    if go and qo % NC4 == 0:
                        combine(go, qo // NC4)
                    g, q = lagged(m, t, i - 4)
                    if g and q % 2 == 1:
                        low(g, q)
                    if go and qo % NC4 == 0:
                        invert(go, qo // NC4)
                    if m and i % 2 == 0:
                        shift(m, i // 2)
                    if a and m and 0 <= i - 1 < NU:
                        prepare(a, i - 1)
                    if go and qo % NC4 == 0:
                        divide(go, qo // NC4)
                    if t and i == 7:
                        residual(t)
                        ln3.dve_stats(v, t)
                        if not m:
                            route.first(v)
                            route.second(v)
                    if t and i == 12:
                        ln3.dve_low(v, t)
                        if not m:
                            route.weights(v)
                    if t and i == 15:
                        lg1.dve_copy(v, t)
            pipeline(v, step)
        dve_parts.append(dve_c)

        def pool_c(q_):
            q_.wait_ge(kb_zero, 3)

            def heads(t):
                return t[:].rearrange("p (b h d) -> p b h d", b=TG, h=NH)

            def split_values(a, part):
                def to(s):
                    return v3[:, a.parity, :, :, s, 0:DH]
                if part == 0:
                    before(q_, v_copied, 1, a, 0)
                    before(q_, pv_used, NQ, a, NQ - 1, 2 * NQ, wait_apart)
                else:
                    wait_apart(q_, v_chain, a.at(4, part))
                ins = (lambda: q_.tensor_copy(to(0), heads(vf)),
                       lambda: q_.tensor_tensor(heads(vr), heads(vf), to(0), ALU.subtract),
                       lambda: q_.tensor_copy(to(1), heads(vr)),
                       lambda: q_.tensor_tensor(heads(vf), heads(vr), to(1), ALU.subtract),
                       lambda: q_.tensor_copy(to(2), heads(vf)))[part]()
                ins.then_inc(v_chain if part < 4 else v_split, 1)

            def low(g, q):
                before(q_, pv_used, NQ, g, q, NC4)
                before(q_, hi_done, NQ, g, q)
                q_.tensor_tensor(pl_[:, q % NC4, :], pt32[:, q // 2 % 2, :], ph[:, q % NC4, :],
                                 ALU.subtract).then_inc(lo_done[0], 1)

            def step(a, m, t):
                for i in range(NQ):
                    g, q = lagged(m, t, i - 4)
                    if g and q % 2 == 0:
                        low(g, q)
                    if t and i == 8:
                        ln3.pool_rstd(q_, t)
                        ln3.pool_norm(q_, t)
                    if a and i in (9, 11, 13, 15):
                        split_values(a, (i - 9) // 2)
                    if m and i == 1:
                        split_values(m, 4)
            pipeline(q_, step)
        pool_parts.append(pool_c)


        def pool_clear(q_):
            q_.wait_ge(xb.lo_done, NG * E)
            q_.memset(kb[:].bitcast(F32), 0.0).then_inc(kb_zero, 1)
            q_.memset(v3[:], 0.0).then_inc(kb_zero, 1)
            q_.wait_ge(kb_zero, 2)
            q_.memset(v3[:, :, :, :, 0, DH:DH + 1], 1.0).then_inc(kb_zero, 1)

        c_prepare["pool"] = pool_clear
        c_prepare["pe"] = lambda pe, *units: pe_c(pe, early_only=True)(*units)
        c_prepare["act"] = lambda a, *units: act_c(a, early_only=True)(*units)
        c_prepare["dve"] = lambda v, *units: dve_c(v, early_only=True)(*units)

        new_scope()
        B = dict(hr=sb("d_hr", [P, 2, HC, GT]), hs=sb("d_hs", [P, 2, 1, GT]),
                 hh=sb("d_hh", [P, 2, 1, GT], F32R), hl=sb("d_hl", [P, 2, 1, GT], F32R),
                 y=sb("d_y", [P, 2, GT]))
        xd = ExpertPass("d", FC, B["y"])
        sg = B["hr"]
        d_silu, d_mul = sem("d_silu_done"), sem("d_product_done")
        xd.high = lambda q: (B["hh"][:, q, 0, :], B["hs"][:, q, 0, :])
        xd.low = lambda q: (B["hl"][:, q, 0, :], B["hs"][:, q, 0, :], B["hh"][:, q, 0, :].bitcast(F32))

        def gus(w, k, c):
            return w[:, (k * FC + c) * P:(k * FC + c + 1) * P]

        def pe_d(pe):
            pe.wait_ge(ln3.lo_done, NG)

            def up(g, e):
                q = (FC * g.c + e) % 2
                h, l = xh[:, g.cols(1), :], xl[:, g.cols(1), :]
                xd.before(pe, d_mul, g, e, 2)
                for k in range(2):
                    o = Z[q][k].rearrange("p (a c) -> p a c", a=1)
                    ins = product3(pe, o, gus(wguh, k, e), gus(wgul, k, e), h, l)
                ins.then_inc(xd.z_ready, 1)
                if e == 0:
                    pe.wait_ge(xd.st_done, g.at(1, 1))
                xd.before(pe, xd.scaled, g, e, 2)
                pe.matmul(SBC[q], sel1[:, e, :], st[:, g.parity, :], start=True, stop=True).then_inc(xd.bc_ready, 1)

            def down(g, e):
                q = (FC * g.c + e) % 2
                if e == 0 and not xd.first(g):
                    pe.wait_ge(xd.y_done, g.at(1, 0))
                xd.before(pe, xd.lo_done, g, e, 0)
                product3(pe, Y, wdh[:, e * P:(e + 1) * P], wdl[:, e * P:(e + 1) * P], B["hh"][:, q, 0, :],
                         B["hl"][:, q, 0, :], start=(e == 0), stop=(e == FC - 1)).then_inc(xd.used, 1)

            def place(a):
                xd.pe_place(pe, a, MISC)

            def y_back(a, t):
                if a:
                    pe.wait_ge(xd.st_done, a.at(1, 1))
                elif not xd.first(t):
                    pe.wait_ge(xd.res, t.at(1, 0))
                xd.pe_y(pe, t, MISC)

            def step(a, m, t):
                for e in range(FC if m else LAG):
                    if m:
                        up(m, e)
                    g, k = xd.prev(m, t, e, LAG)
                    if g:
                        down(g, k)
                    if m and e == 2 and a:
                        place(a)
                    if m and e == 5 and t:
                        y_back(a, t)
                if not m:
                    if a:
                        place(a)
                    if t:
                        y_back(a, t)
            pipeline(pe, step)
        pe_parts.append(pe_d)

        def act_d(a_):
            tail = Route(1, TAIL, rt_tail)

            def route_last():
                a_.wait_ge(lg1.lg_copied, NG)
                tail.act_sigmoid(a_)

            def silu(g, e):
                q = (FC * g.c + e) % 2
                xd.before(a_, xd.z_ready, g, e, 0)
                xd.before(a_, d_mul, g, e, 2)
                a_.activation(sg[:, q, 0, :], Z[q][0], ACT.Silu).then_inc(d_silu, 1)

            def step(a, m, t):
                if m:
                    for e in range(FC):
                        if e == LAG and t:
                            xd.act_y(a_, t, Y)
                        silu(m, e)
                        g, k = xd.prev(m, t, e)
                        if g:
                            xd.act_high(a_, g, k)
                        if e == 3 and a:
                            xd.act_place(a_, a, MISC)
                else:
                    if t:
                        xd.act_high(a_, t, FC - 1)
                        xd.act_y(a_, t, Y)
                    if a:
                        xd.act_place(a_, a, MISC)
            pipeline(a_, step, route_last)
        act_parts.append(act_d)

        def dve_d(v):
            tail = Route(1, TAIL, rt_tail)

            v.tensor_copy(sg_gate_h[:], tg[:, 3:4]).then_inc(xd.ss_chain, 1)
            v.wait_ge(xd.ss_chain, 1)
            v.tensor_tensor(sg_gate_l[:], tg[:, 3:4], sg_gate_h[:].bitcast(F32), ALU.subtract).then_inc(xd.ss_chain, 1)
            v.wait_ge(xd.ss_chain, 2)
            v.tensor_copy(ss[:, :, :, E:E + 1].rearrange("p a b c -> p (a b) c"),
                          sg_gate_h[:].bitcast(F32).unsqueeze(1).broadcast_to([P, 2 * TG, 1]))
            v.tensor_copy(ss[:, :, :, 32 + E:33 + E].rearrange("p a b c -> p (a b) c"),
                          sg_gate_l[:].bitcast(F32).unsqueeze(1).broadcast_to([P, 2 * TG, 1]))

            def mul(g, e):
                q = (FC * g.c + e) % 2
                xd.before(v, d_silu, g, e, 0)
                v.tensor_tensor(sg[:, q, 1, :], sg[:, q, 0, :], Z[q][1], ALU.mult).then_inc(d_mul, 1)

            def scale(g, e):
                q = (FC * g.c + e) % 2
                xd.before(v, d_mul, g, e, 0)
                xd.before(v, xd.bc_ready, g, e, 0)
                xd.before(v, xd.lo_done, g, e, 2)
                v.tensor_tensor(B["hs"][:, q, 0, :], sg[:, q, 1, :], SBC[q], ALU.mult).then_inc(xd.scaled, 1)

            def low(g, k):
                xd.before(v, xd.used, g, k, 2)
                xd.dve_low(v, g, k)

            def step(a, m, t):
                if m:
                    for e in range(FC):
                        mul(m, e)
                        g, k = xd.prev(m, t, e)
                        if g:
                            low(g, k)
                        scale(m, e)
                        if e == 0 and a:
                            xd.dve_place(v, a)
                        if e == 6 and t:
                            xd.dve_residual(v, t, MISC)
                else:
                    if a:
                        xd.dve_place(v, a)
                    if t:
                        low(t, FC - 1)
                        xd.dve_residual(v, t, MISC)
            pipeline(v, step, lambda: tail.all(v))
        dve_parts.append(dve_d)

        def sp_d(sp):
            ov = out.rearrange("b p d -> p b d")
            with sp.Fori(0, NG // 2) as i:
                for c in range(2):
                    g = Group(i, c)
                    sp.wait_ge(xd.res, g.at(1, 1))
                    sp.dma_start(ov[:, g.tiles(), :], x_all[:, g.tiles(), :]).then_inc(s_out[c], 16)
            for c in range(2):
                sp.wait_ge(s_out[c], 16 * (NG // 2))
        sp_parts.append(sp_d)

        scope[0].close()

        @block.sync
        def _(sp):
            for f in sp_parts:
                f(sp)

        @block.gpsimd
        def _(q):
            for f in pool_parts:
                f(q)

        @block.scalar
        def _(a):
            for f in act_parts:
                f(a)

        @block.vector
        def _(v):
            for f in dve_parts:
                f(v)

        @block.tensor
        def _(pe):
            for f in pe_parts:
                f(pe)


_OUT_SHAPE = (NB, P, D)


def kernel(**inputs):
    import numpy as np
    import concourse.bacc as bacc
    from concourse.bass_utils import run_bass_kernel_spmd

    a = {k: np.asarray(v) for k, v in inputs.items()}
    z = lambda *shape: np.zeros(shape, np.float32)

    ctxT = z(D, NB, SK)
    ctxT[:, :, :S2] = a["ctx_1024"].transpose(2, 0, 1)
    gates = np.broadcast_to(np.concatenate([a["g_xattn"], a["g_ffn"]])[None, :], (P, 4))

    def stack(w):
        o = np.zeros(w.shape[:-1] + (NC4, HQ, 4, DH), np.float32)
        o[..., 0:3, :] = w.reshape(w.shape[:-1] + (NC4, HQ, 1, DH))
        return o.reshape(w.shape[:-1] + (NC4 * P,))

    def columns(v):
        return stack(v).reshape(NC4, P).T

    def side_by_side(w):
        n = -(-w.shape[0] // P)
        o = z(n * P, w.shape[1])
        o[:w.shape[0]] = w
        return o.reshape(n, P, w.shape[1]).transpose(1, 0, 2).reshape(P, -1)

    def router(w):
        o = z(D, P)
        o[:, :E] = w
        return o

    def hidden(experts, shared):
        o = z(D, FC * P)
        o[:, :E * F1] = experts.transpose(1, 0, 2).reshape(D, E * F1)
        o[:, E * F1:(E + 1) * F1] = shared
        return o

    b2 = z(P, D)
    b2[0:E] = a["L0_ffn_b2"]
    b2[32:32 + E] = a["L0_ffn_b2"]
    part = {
        "wg0": router(a["L0_ffn_Wg"]), "b2": b2,
        "w1": a["L0_ffn_W1"].transpose(1, 0, 2).reshape(D, -1),
        "w2": side_by_side(a["L0_ffn_W2"].reshape(-1, D)),
        "wq": stack(a["L1_xattn_wq"].T), "wg1": router(a["L1_ffn_W_gate_router"]),
        "wgu": np.concatenate([hidden(a["L1_ffn_Wg"], a["L1_ffn_Wg_s"]),
                               hidden(a["L1_ffn_Wu"], a["L1_ffn_Wu_s"])], 1),
        "wd": side_by_side(np.concatenate([a["L1_ffn_Wd"].reshape(-1, D), a["L1_ffn_Wd_s"]])),
    }
    sel0, sel1 = z(P, E, P), z(P, FC, P)
    for e in range(E):
        sel0[[e, 32 + e], e, :] = 1.0
    for r in range(FC * P):
        e = r // F1
        if e <= E:
            sel1[[e, 32 + e], r // P, r % P] = 1.0
    part["sel0"], part["sel1"] = sel0.reshape(P, -1), sel1.reshape(P, -1)
    lows = z(P, 2)
    rows = np.arange(P) % (4 * DH) // DH
    lows[rows == 2, 0] = 1.0
    lows[rows == 1, 1] = 1.0
    rank = np.broadcast_to(np.arange(E, 0, -1).astype(np.float32)[None, :], (P, E))

    arrays = dict(
        x=a["x"], ctxT=ctxT.reshape(D, -1), mask=a["mask_SxS2_bk1"], gates=gates, ident_in=np.eye(P, dtype=np.float32),
        part_in=lows, rank_in=rank, weights=np.concatenate([part[n] for n in WIDTH], 1),
        wq0=a["L0_xattn_w_q"], wk0=a["L0_xattn_w_k"], wv0T=a["L0_xattn_w_v"].T,
        b1=a["L0_ffn_b1"].reshape(E, HC, P).transpose(2, 0, 1),
        bqs=columns(a["L1_xattn_bq"]), wks=stack(a["L1_xattn_wk"].T), bks=columns(a["L1_xattn_bk"]),
        wvT=a["L1_xattn_wv"].T, bv=a["L1_xattn_bv"][:, None],
        woT=a["L1_xattn_wo"].T, bo=a["L1_xattn_bo"][None, :],
        ebias=np.broadcast_to(a["L1_ffn_expert_bias"][None, :], (P, E)))

    nc = bacc.Bacc("TRN2", target_bir_lowering=False, num_devices=1)
    maps, args = {}, {}
    for name, v in arrays.items():
        v = np.ascontiguousarray(v)
        maps[f"in_{name}"] = v
        args[name] = nc.dram_tensor(f"in_{name}", v.shape, mybir.dt.from_np(v.dtype), kind="ExternalInput").ap()
    args["out"] = nc.dram_tensor("out_dram", _OUT_SHAPE, F32, kind="ExternalOutput").ap()
    flamingo_kernel(nc, **args)
    r = run_bass_kernel_spmd(nc, [maps], core_ids=[0])
    return r.results[0]["out_dram"]
```
